# Optimizing a Trainium2 kernel written in Bass

```python
import numpy as np
import jax
import jax.numpy as jnp

def _softmax(x, axis=-1):
    return jax.nn.softmax(x, axis=axis)

def _gelu(x):
    return jax.nn.gelu(x, approximate=True)

def _silu(x):
    return jax.nn.silu(x)

def _sigmoid(x):
    return jax.nn.sigmoid(x)

def _layernorm(x, axis=-1, eps=1e-05):
    m = jnp.mean(x, axis=axis, keepdims=True)
    v = jnp.var(x, axis=axis, keepdims=True)
    return (x - m) / jnp.sqrt(v + eps)

def _scatter_add(tgt, idx, src, axis=0):
    return tgt.at[idx].add(src)

def _segment_sum(src, seg, n):
    return jax.ops.segment_sum(src, seg, n)
kernel_name = 'mk_conv_attn_hybrid_d2_conv_nchw256_r2_53d833'

def setup_inputs(seed: int=0):
    np.random.seed(seed)
    _w = jnp.asarray

    def _rec_inputs():
        import jax
        import jax.numpy as jnp
        _gk = jax.random.key(seed)
        x = -0.0002928 + 1 * jax.random.normal(jax.random.fold_in(_gk, 1), (4, 128, 32, 32), jnp.float32)
        return x
    x = _rec_inputs()

    def _L0_conv_setup():
        import jax, jax.numpy as jnp
        import numpy as np
        N, C, H, W = (4, 128, 32, 32)
        C_EMBED = C // 2
        key = jax.random.key(seed)
        k1, k2, k3, k4 = jax.random.split(key, 4)
        x = jax.random.normal(k1, (N, C, H, W), dtype=jnp.float32)
        theta_w = jax.random.normal(k2, (C_EMBED, C), dtype=jnp.float32) * 0.01
        phi_w = jax.random.normal(k3, (C_EMBED, C), dtype=jnp.float32) * 0.01
        proj_w = jax.random.normal(k4, (C, C), dtype=jnp.float32) * 0.01
        return {'x': x, 'theta_w': theta_w, 'phi_w': phi_w, 'proj_w': proj_w}
    _L0_conv_all = _L0_conv_setup()
    _L0_conv_in = {k: v for k, v in _L0_conv_all.items() if k in ('theta_w', 'phi_w', 'proj_w')}
    del _L0_conv_all

    def _L1_attn_setup():
        import jax, jax.numpy as jnp
        import numpy as np
        D = 128
        key = jax.random.key(seed)
        ks = jax.random.split(key, 7)
        B, N = (4, 2048)
        s = 1.0 / np.sqrt(D)
        return {'x': jax.random.normal(ks[0], (B, N, D), dtype=jnp.float32), 'Wk': jax.random.normal(ks[1], (D, D), dtype=jnp.float32) * s, 'bk': jax.random.normal(ks[2], (D,), dtype=jnp.float32) * 0.01, 'Wq': jax.random.normal(ks[3], (D, D), dtype=jnp.float32) * s, 'bq': jax.random.normal(ks[4], (D,), dtype=jnp.float32) * 0.01, 'Wv': jax.random.normal(ks[5], (D, D), dtype=jnp.float32) * s, 'bv': jax.random.normal(ks[6], (D,), dtype=jnp.float32) * 0.01}
    _L1_attn_all = _L1_attn_setup()
    _L1_attn_in = {k: v for k, v in _L1_attn_all.items() if k in ('Wk', 'bk', 'Wq', 'bq', 'Wv', 'bv')}
    del _L1_attn_all

    def _L1_ffn_setup():
        import jax, jax.numpy as jnp
        import numpy as np
        TOP_K = 2
        key = jax.random.key(seed)
        ks = jax.random.split(key, 4)
        B, L, D, H, E = (8, 2048, 128, 512, 8)
        s = 0.02
        return {'x': jax.random.normal(ks[0], (B, L, D), jnp.float32), 'Wg': jax.random.normal(ks[1], (D, E), jnp.float32) * s, 'bg': jnp.zeros((E,), jnp.float32), 'W1': jax.random.normal(ks[2], (E, D, H), jnp.float32) * s, 'b1': jnp.zeros((E, H), jnp.float32), 'W2': jax.random.normal(ks[3], (E, H, D), jnp.float32) * s, 'b2': jnp.zeros((E, D), jnp.float32)}
    _L1_ffn_all = _L1_ffn_setup()
    _L1_ffn_in = {k: v for k, v in _L1_ffn_all.items() if k in ('Wg', 'bg', 'W1', 'b1', 'W2', 'b2')}
    del _L1_ffn_all
    return {'x': x, 'L0_conv_theta_w': _L0_conv_in['theta_w'], 'L0_conv_phi_w': _L0_conv_in['phi_w'], 'L0_conv_proj_w': _L0_conv_in['proj_w'], 'L1_attn_Wk': _L1_attn_in['Wk'], 'L1_attn_bk': _L1_attn_in['bk'], 'L1_attn_Wq': _L1_attn_in['Wq'], 'L1_attn_bq': _L1_attn_in['bq'], 'L1_attn_Wv': _L1_attn_in['Wv'], 'L1_attn_bv': _L1_attn_in['bv'], 'L1_ffn_Wg': _L1_ffn_in['Wg'], 'L1_ffn_bg': _L1_ffn_in['bg'], 'L1_ffn_W1': _L1_ffn_in['W1'], 'L1_ffn_b1': _L1_ffn_in['b1'], 'L1_ffn_W2': _L1_ffn_in['W2'], 'L1_ffn_b2': _L1_ffn_in['b2']}

def reference(x, L0_conv_theta_w, L0_conv_phi_w, L0_conv_proj_w, L1_attn_Wk, L1_attn_bk, L1_attn_Wq, L1_attn_bq, L1_attn_Wv, L1_attn_bv, L1_ffn_Wg, L1_ffn_bg, L1_ffn_W1, L1_ffn_b1, L1_ffn_W2, L1_ffn_b2):
    import jax
    import jax.numpy as jnp

    def _L0_conv_ref(x, theta_w, phi_w, proj_w):
        import jax, jax.numpy as jnp
        import numpy as np
        N, C, H, W = (4, 128, 32, 32)
        C_EMBED = C // 2
        n, c, h, w = x.shape
        s = h * w
        xf = x.reshape(n, c, s)
        theta = jnp.einsum('ec,ncs->nse', theta_w, xf)
        phi = jnp.einsum('ec,ncs->nes', phi_w, xf)
        scale = jnp.sqrt(jnp.float32(theta_w.shape[0]))
        f = jnp.einsum('nse,net->nst', theta, phi) / scale
        f = jax.nn.softmax(f, axis=-1)
        y = jnp.einsum('nst,nct->ncs', f, xf)
        res = jnp.einsum('oc,ncs->nos', proj_w, y)
        return x + res.reshape(n, c, h, w)

    def _L1_attn_ref(x, Wk, bk, Wq, bq, Wv, bv):
        import jax, jax.numpy as jnp
        import numpy as np
        D = 128
        keys = jnp.einsum('bnd,de->bne', x, Wk) + bk
        queries = jnp.einsum('bnd,de->bne', x, Wq) + bq
        values = jnp.einsum('bnd,de->bne', x, Wv) + bv
        scale = 1.0 / jnp.sqrt(jnp.float32(D))
        scores = jnp.einsum('bqd,bkd->bqk', queries, keys) * scale
        attn = jax.nn.softmax(scores, axis=-1)
        out = jnp.einsum('bqk,bkd->bqd', attn, values)
        return out

    def _L1_ffn_ref(x, Wg, bg, W1, b1, W2, b2):
        import jax, jax.numpy as jnp
        import numpy as np
        TOP_K = 2
        B, L, D = x.shape
        E = W1.shape[0]
        xf = x.reshape(-1, D)
        gate_logits = xf @ Wg + bg
        top_w, top_i = jax.lax.top_k(gate_logits, TOP_K)
        top_w = jax.nn.softmax(top_w, axis=-1)
        w_dense = jnp.sum(jax.nn.one_hot(top_i, E, dtype=xf.dtype) * top_w[..., None], axis=1)
        out = jnp.zeros_like(xf)
        for e in range(E):
            h = jax.nn.gelu(xf @ W1[e] + b1[e], approximate=False)
            out = out + w_dense[:, e:e + 1] * (h @ W2[e] + b2[e])
        return out.reshape(B, L, D)

    def _gn(v, G=32, eps=1e-05):
        B_, C_, H_, W_ = v.shape
        g = v.reshape(B_, G, C_ // G, H_, W_)
        m = jnp.mean(g, axis=(2, 3, 4), keepdims=True)
        s = jnp.var(g, axis=(2, 3, 4), keepdims=True)
        return ((g - m) / jnp.sqrt(s + eps)).reshape(v.shape)

    def _ln_c(v, eps=1e-06):
        m = jnp.mean(v, axis=1, keepdims=True)
        s = jnp.var(v, axis=1, keepdims=True)
        return (v - m) / jnp.sqrt(s + eps)

    def _ln_t(v, eps=1e-05):
        m = jnp.mean(v, axis=-1, keepdims=True)
        s = jnp.var(v, axis=-1, keepdims=True)
        return (v - m) / jnp.sqrt(s + eps)

    def _to_tokens(v):
        B_, C_, H_, W_ = v.shape
        return v.reshape(B_, C_, H_ * W_).transpose(0, 2, 1)

    def _from_tokens(t, like):
        B_, C_, H_, W_ = like.shape
        return t.transpose(0, 2, 1).reshape(B_, C_, H_, W_)
    x = _L0_conv_ref(x, L0_conv_theta_w, L0_conv_phi_w, L0_conv_proj_w)
    t = _to_tokens(x)
    t = t + _L1_attn_ref(_ln_t(t), L1_attn_Wk, L1_attn_bk, L1_attn_Wq, L1_attn_bq, L1_attn_Wv, L1_attn_bv)
    t = t + _L1_ffn_ref(_ln_t(t), L1_ffn_Wg, L1_ffn_bg, L1_ffn_W1, L1_ffn_b1, L1_ffn_W2, L1_ffn_b2)
    x = _from_tokens(t, x)
    return x

_drawn_inputs = setup_inputs


def setup_inputs(seed=0):
    import zlib

    import numpy as np

    out = dict(_drawn_inputs(seed))
    spreads = {'L1_ffn_bg': (0.0, 0.1), 'L1_ffn_b1': (0.0, 0.458), 'L1_ffn_b2': (0.0, 0.1)}
    factors = {'L0_conv_theta_w': 8.0,
     'L0_conv_phi_w': 8.0,
     'L0_conv_proj_w': 8.0,
     'L1_attn_bk': 64.0,
     'L1_attn_bq': 34.342,
     'L1_attn_bv': 4.368}
    for name, (base, spread) in spreads.items():
        noise = np.random.default_rng([zlib.crc32(name.encode()), seed]).standard_normal(out[name].shape)
        drawn = base * np.exp(spread * noise) if base else spread * noise
        out[name] = jnp.asarray(drawn.astype(out[name].dtype))
    for name, factor in factors.items():
        out[name] = (out[name] * factor).astype(out[name].dtype)
    return out
```

```python
from contextlib import ExitStack

import concourse.bass as bass
from concourse import mybir

F32 = mybir.dt.float32
F16 = mybir.dt.float16
BF16 = mybir.dt.bfloat16
I32 = mybir.dt.int32
U32 = mybir.dt.uint32
ALU = mybir.AluOpType
ACT = mybir.ActivationFunctionType
AX = mybir.AxisListType

P = 128
B = 4
S = 1024
T = S // P
TT = B * T
PAIRS = T // 2
UNITS = 2 * B
CE = 64
SCALE = [CE ** -0.5, P ** -0.5]
EPS = 1e-5
WS = 64.0
HALF = 512
VW = P + 1


E = 8
HID = 512
HC = HID // P
CAP = TT * P + P
NT = TT * 2 + E
ROW = 2 * P + 2
PADS = E + E
IN_BUFS = 8


def build(nc, x, theta_w, phi_w, proj_w, Wk, bk, Wq, bq, Wv, bv, Wg, bg, W1, b1, W2, b2, out):
    ds = bass.ds
    with ExitStack() as ctx:
        def sb(name, shape, dt):
            return ctx.enter_context(nc.sbuf_tensor(name, shape, dt))

        def ps(name, shape, dt=F32):
            return ctx.enter_context(nc.psum_tensor(name, shape, dt))

        def sem(name):
            return ctx.enter_context(nc.semaphore(name))

        X = sb("X", [P, B, S], F32)
        X16h = sb("X16h", [P, S], F16)
        X16l = sb("X16l", [P, S], F16)
        TOK = sb("TOK", [P, TT, P], F32)
        ZZ = sb("ZZ", [P, TT, 2, P], F16)
        QK = sb("QK", [P, 3, 4, S], F16)
        QH, QL, KH, KL = (QK[:, :, j, :] for j in range(4))
        VH = sb("VH", [P, 4, T, VW], F16)
        VL = sb("VL", [P, 4, T, P], F16)
        EH = sb("EH", [P, 2, T, S], F16)
        EL = sb("EL", [P, 2, T, S], F16)
        E32 = sb("E32", [P, 2, S], F32)
        DG = sb("DG", [P, 2, T, P], BF16)
        mx = sb("mx", [P, T], F32)
        ident16 = sb("ident16", [P, P], F16)
        identb = sb("identb", [P, P], BF16)
        ident32 = sb("ident32", [P, P], F32)
        onesb = sb("onesb", [P, P], BF16)
        ones16 = sb("ones16", [P, 2 * P], F16)
        W32 = sb("W32", [P, 5, P], F32)
        W16 = sb("W16", [P, 2, 3, 2, P], F16)
        B32 = sb("B32", [P, 3, P], F32)
        B16 = sb("B16", [P, 3, P], F16)
        rec = sb("rec", [P, 1], F32)
        stats = sb("stats", [P, 2, 6], F32)
        mv = sb("mv", [P, 2, 2], F32)
        ve = sb("ve", [P, 2], F32)
        lnv = sb("lnv", [P, 2], F32)
        r0 = sb("r0", [P, 2], F32)
        nt = sb("nt", [P, 2], F32)
        nt2 = sb("nt2", [P, 2], F32)
        rstd = sb("rstd", [P, 2], F32)
        Z = sb("Z", [P, 2, P], F32)
        carry = sb("carry", [P, 4], F32)
        bgb = sb("bgb", [P, E], F32)
        Wg32 = sb("Wg32", [P, E], F32)
        WG16 = sb("WG16", [P, 2, E], F16)
        LG = sb("LG", [P, T, E], F32)
        top = sb("top", [P, T, 8], F32)
        topi = sb("topi", [P, T, 8], U32)
        topf = sb("topf", [P, 2, T], F32)
        iota_e = sb("iota_e", [P, E, T], F32)
        ecap = sb("ecap", [P, E], F32)
        start = sb("start", [P, E], F32)
        hot = sb("hot", [P, 2, E, T], F32)
        picked = sb("picked", [P, E, T], F16)
        tri = sb("tri", [P, P], F16)
        restart = sb("restart", [P, E, T], F32)
        tots = sb("tots", [P, E, T], F32)
        incl = sb("incl", [P, E, T], F32)
        befo = sb("befo", [P, E, T], F32)
        rank = sb("rank", [P, E, T], F32)
        rows = sb("rows", [P, E, T], F32)
        mine = sb("mine", [P, 2, E, T], F32)
        posf = sb("posf", [P, 2, T], F32)
        posi = sb("posi", [P, 2, B * T], U32)
        gap = sb("gap", [P, T], F32)
        egap = sb("egap", [P, T], F32)
        den = sb("den", [P, T], F32)
        WT = sb("WT", [P, 2, TT], F32)
        ids = sb("ids", [P, TT, 2], I32)
        padid = sb("padid", [P, PADS, 2], I32)
        zer = sb("zer", [P, 2 * P], F16)
        EH0, EH1 = (EH[:, j].rearrange("p a b -> p (a b)") for j in range(2))
        EL0, EL1 = (EL[:, j].rearrange("p a b -> p (a b)") for j in range(2))
        E32f = E32[:].rearrange("p a b -> p (a b)")
        iota33 = sb("iota33", [P, TT + 1], F32)
        iotaj = sb("iotaj", [P, NT], F32)
        over = E32f[:, 2 * NT * E:2 * NT * E + E * (TT + 1)].rearrange("p (e n) -> p e n", e=E)
        cnt = sb("cnt", [P, E], F32)
        tiles = sb("tiles", [P, E], F32)
        ends = sb("ends", [P, E], F32)
        skip = sb("skip", [P, E], F32)
        past, jump = (E32f[:, j * NT * E:(j + 1) * NT * E].rearrange("p (j e) -> p j e", e=E) for j in range(2))
        tabf = sb("tabf", [P, 2, NT], F32)
        tabi = sb("tabi", [P, 2, NT], I32)
        padrow = sb("padrow", [P, E], I32)
        ones8 = sb("ones8", [P, E], F32)
        W1H = sb("W1H", [P, E * HID], F16)
        W1L = sb("W1L", [P, E * HID], F16)
        W2H = EL0[:, 0:E * HID]
        W2L = QK[:, 2].rearrange("p a b -> p (a b)")
        b1r = sb("b1r", [E * HC, P], F32)
        b1T = sb("b1T", [P, E * HC], F32)
        b2b = DG[:].rearrange("p a b c -> p (a b c)").bitcast(F32)
        Xw = X[:].rearrange("p a b -> p (a b)")
        sortrow = [EH0[:, h * T * ROW:(h + 1) * T * ROW].rearrange("p (t s r) -> p t s r", s=2, r=ROW)
                   for h in range(2)]
        tin = EH0[:, 2 * T * ROW:2 * T * ROW + IN_BUFS * ROW].rearrange("p (b r) -> p b r", r=ROW)
        at = 0
        zT = EH1[:, at:at + 4 * P].rearrange("p (b r) -> p b r", b=2)
        at += 4 * P
        hh = EH1[:, at:at + 2 * HID].rearrange("p (b r) -> p b r", b=2)
        at += 2 * HID
        hl = EH1[:, at:at + 2 * HID].rearrange("p (b r) -> p b r", b=2)
        at += 2 * HID
        h32 = EH1[:, at:at + 4 * HID].bitcast(F32).rearrange("p (b r) -> p b r", b=2)
        at += 4 * HID
        y32 = EH1[:, at:at + 2 * IN_BUFS * P].bitcast(F32).rearrange("p (b r) -> p b r", b=IN_BUFS)
        yin = EL1.bitcast(F32).rearrange("p (b t s c) -> p b t s c", b=2, t=T, s=2)

        zbuf = nc.dram_tensor("zbuf", [E * CAP + E * P, ROW], F16, kind="Internal").ap()
        ybuf = nc.dram_tensor("ybuf", [2 * TT * P + PADS * P, P], F32, kind="Internal").ap()

        SC = ps("SC", [P, 2, S])
        MX = ps("MX", [P, S])
        PV = ps("PV", [P, HALF])
        PR = ps("PR", [P, HALF])

        x_in = [sem(f"x_in{b}") for b in range(B)]
        w_in = sem("w_in")
        b_in = sem("b_in")
        const_ready = sem("const_ready")
        zero_ready = sem("zero_ready")
        bias_zeroed = sem("bias_zeroed")
        wt_full = sem("wt_full")
        w_hi = sem("w_hi")
        w_ready = sem("w_ready")
        x_hi = sem("x_hi")
        x_lo = sem("x_lo")
        mx_full = sem("mx_full")
        mx_free = sem("mx_free")
        max_ready = sem("max_ready")
        diag_ready = sem("diag_ready")
        sc_full = sem("sc_full")
        sc_free = sem("sc_free")
        e32_free = sem("e32_free")
        proj_full = sem("proj_full")
        proj_hi = sem("proj_hi")
        proj_free = sem("proj_free")
        pv_full = sem("pv_full")
        pv_free = sem("pv_free")
        rec_ready = sem("rec_ready")
        stats_ready = sem("stats_ready")
        mv_ready = sem("mv_ready")
        ve_ready = sem("ve_ready")
        ln_ready = sem("ln_ready")
        r0_ready = sem("r0_ready")
        newton = sem("newton")
        z_ready = sem("z_ready")
        zh_ready = sem("zh_ready")
        z_split = sem("z_split")
        out_done = sem("out_done")
        g_in = sem("g_in")
        iotas = sem("iotas")
        tri_zero = sem("tri_zero")
        wexp_in = sem("wexp_in")
        wexp_scaled = sem("wexp_scaled")
        wexp_lo = sem("wexp_lo")
        b1_full = sem("b1_full")
        b1_ready = sem("b1_ready")
        b2_in = sem("b2_in")
        chain = sem("chain")
        picked_ready = sem("picked_ready")
        gap_ready = sem("gap_ready")
        egap_ready = sem("egap_ready")
        rows_ready = sem("rows_ready")
        pos_ready = sem("pos_ready")
        scattered = [sem(f"scattered{h}") for h in range(2)]
        table_ready = sem("table_ready")
        pad_done = sem("pad_done")
        pad_static = sem("pad_static")
        tin_full = [sem(f"tin_full{b}") for b in range(IN_BUFS)]
        zt_full = sem("zt_full")
        zt_ready = sem("zt_ready")
        h_full = sem("h_full")
        h_ready = sem("h_ready")
        hh_ready = sem("hh_ready")
        hl_ready = sem("hl_ready")
        y_full = sem("y_full")
        y_ready = sem("y_ready")
        carried = sem("carried")
        y_out = [sem(f"y_out{b}") for b in range(IN_BUFS)]
        y_in = [sem(f"y_in{b}") for b in range(B)]
        mixed = sem("mixed")
        summed = sem("summed")
        o_full = sem("o_full")
        o_ready = sem("o_ready")

        STEPS = range(-2, UNITS + 2)

        def roles(s):
            return (s if 0 <= s < UNITS else None, s - 1 if 0 <= s - 1 < UNITS else None,
                    s + 1 if 0 <= s + 1 < UNITS else None, s + 2 if s + 2 < UNITS + B else None)

        def pr_base(v):
            n = 0
            for w in range(v):
                n += PAIRS * (2 if w < B else 3 if w < UNITS else 2)
            return n + max(0, v - UNITS - 1)

        def prefix_uses(s):
            batches = {7: [0], 8: [1], 9: [2, 3]}.get(s, [])
            return [(c, pr_base(s + 2) + 2 * PAIRS + j) for j, c in enumerate(batches)]

        def hi_base(v):
            return pr_base(min(v, UNITS)) + PAIRS * max(v - UNITS, 0)

        def per_pair(v):
            return 2 if v < B else 3 if v < UNITS else 2

        def mx_base(s):
            return sum((1 if t + 2 < B else 0) + (T if 0 <= t + 1 < UNITS else 0) for t in range(-2, s))

        def expert_registers(engine, name, n):
            return [engine.alloc_register(f"{name}{b}") for b in range(n)]

        def load_experts(engine, registers, j):
            n = len(registers)
            engine.load(registers, tabi[0:1, 1, ds(j, n)])

        def expert(engine, registers, b):
            return engine.snap(registers[b], min_val=0, max_val=E - 1)

        block = ctx.enter_context(nc.Block())

        @block.sync
        def _(sp):
            sp.dma_start(X[:, 0, :], x[0]).then_inc(x_in[0], 16)
            sp.dma_start(W32[0:CE, 0, :], theta_w).then_inc(w_in, 16)
            sp.dma_start(W32[CE:P, 0, :], phi_w).then_inc(w_in, 16)
            sp.dma_start(W32[:, 1, :], proj_w).then_inc(w_in, 16)
            for b in range(1, B):
                sp.dma_start(X[:, b, :], x[b]).then_inc(x_in[b], 16)
            for j, w in enumerate((Wq, Wk, Wv)):
                sp.dma_start(W32[:, 2 + j, :], w).then_inc(w_in, 16)
            sp.wait_ge(bias_zeroed, 1)
            for j, v in enumerate((bq, bk, bv)):
                for r in (0, 32):
                    sp.dma_start(B32[r:r + 1, j, :], v).then_inc(b_in, 16)
            sp.dma_start(Wg32[:], Wg).then_inc(g_in, 16)
            sp.dma_start(bgb[:], bg.partition_broadcast(P)).then_inc(g_in, 16)
            sp.dma_start(b1r[:], b1).then_inc(g_in, 16)
            sp.wait_ge(iotas, 7)
            unused = zbuf[E * CAP:, :].rearrange("(n p) r -> p n r", p=P)
            for n in range(E):
                sp.dma_start(unused[:, n, 0:2 * P], zer[:]).then_inc(pad_static, 16)
                sp.dma_start(unused[:, n, 2 * P:ROW], padid[:, E + n, 0:1].bitcast(F16)).then_inc(pad_static, 16)
            sp.wait_ge(x_lo, B)
            sp.wait_ge(mx_full, mx_base(1) + 1)
            sp.dma_start(Xw.rearrange("p (e h) -> p e h", e=E), W1.rearrange("e d h -> d e h")).then_inc(wexp_in, 16)
            sp.wait_ge(wexp_lo, PAIRS)
            sp.dma_start(Xw.rearrange("p (e c d) -> p e c d", e=E, c=HC),
                         W2.rearrange("e (c h) d -> h e c d", c=HC)).then_inc(wexp_in, 16)
            sp.wait_ge(sc_full, T * UNITS)
            sp.dma_start(b2b, b2.partition_broadcast(P)).then_inc(b2_in, 16)
            sp.wait_ge(table_ready, 2)
            for e in range(E):
                r = sp.value_load(padrow[0:1, e:e + 1], min_val=e * CAP, max_val=e * CAP + TT * P)
                sp.dma_start(zbuf[ds(r, P), 0:2 * P], zer[:]).then_inc(pad_done, 16)
                sp.dma_start(zbuf[ds(r, P), 2 * P:ROW], padid[:, e, 0:1].bitcast(F16)).then_inc(pad_done, 16)
            sp.wait_ge(pad_done, 16 * 2 * E)
            sp.wait_ge(pad_static, 16 * 2 * E)
            for h in range(2):
                sp.wait_ge(scattered[h], 16 * T * B)

            def load_tile(j, b, again):
                r = sp.value_load(tabi[0:1, 0, ds(j, 1)], min_val=0, max_val=(E * CAP + E * P) // P - 1)
                if again is not None:
                    sp.wait_ge(y_out[b], again)
                sp.dma_start(tin[:, b, :], zbuf[ds(r * P, P), :]).then_inc(tin_full[b], 16)

            for b in range(IN_BUFS):
                load_tile(b, b, None)
            with sp.Fori(1, NT // IN_BUFS) as i:
                for b in range(IN_BUFS):
                    load_tile(i * IN_BUFS + b, b, i * 16)
            for b in range(IN_BUFS):
                sp.wait_ge(y_out[b], 16 * (NT // IN_BUFS))
            for b in range(B):
                if b >= 2:
                    sp.wait_ge(summed, T * (b - 1))
                sp.dma_start(yin[:, b % 2], ybuf[2 * S * b:2 * S * (b + 1), :].rearrange("(t p s) c -> p t s c", p=P, s=2)) \
                    .then_inc(y_in[b], 16)
            for b in range(B):
                sp.wait_ge(o_ready, b + 1)
                sp.dma_start(out[b], X[:, b, :]).then_inc(out_done, 16)
            sp.wait_ge(out_done, 16 * B)

        @block.gpsimd
        def _(pool):
            nc.gpsimd.memset(ident32[:], 0.0).then_inc(zero_ready, 1)
            pool.wait_ge(zero_ready, 1)
            nc.gpsimd.affine_select(out=ident32[:], in_=ident32[:], compare_op=ALU.not_equal, fill=1.0, base=0,
                                    pattern=[[-1, P]], channel_multiplier=1).then_inc(zero_ready, 1)
            pool.wait_ge(zero_ready, 2)
            nc.gpsimd.tensor_copy(ident16[:], ident32[:]).then_inc(const_ready, 1)
            nc.gpsimd.tensor_copy(identb[:], ident32[:]).then_inc(const_ready, 1)

            nc.gpsimd.memset(carry[:, 0:2], 0.0).then_inc(iotas, 1)
            nc.gpsimd.memset(carry[:, 3:4], 0.0).then_inc(carried, 1)
            iot = nc.gpsimd.iota
            iot(ids[:], [[2 * P, TT], [1, 2]], base=0, channel_multiplier=2).then_inc(iotas, 1)
            iot(padid[:], [[P, PADS], [0, 2]], base=2 * TT * P, channel_multiplier=1).then_inc(iotas, 1)
            nc.gpsimd.memset(zer[:], 0.0).then_inc(iotas, 1)
            kw = dict(channel_multiplier=0, allow_small_or_imprecise_dtypes=True)
            iot(iota_e[:], [[1, E], [0, T]], base=0, **kw).then_inc(iotas, 1)
            iot(iota33[:], [[P, TT + 1]], base=0, **kw).then_inc(iotas, 1)
            iot(iotaj[:], [[1, NT]], base=0, **kw).then_inc(iotas, 1)
            iot(ecap[:], [[CAP, E]], base=0, **kw).then_inc(iotas, 1)
            iot(start[:], [[CAP, E]], base=0, **kw).then_inc(iotas, 1)
            nc.gpsimd.memset(restart[:], 1.0).then_inc(iotas, 1)
            nc.gpsimd.memset(ones8[:], 1.0).then_inc(iotas, 1)
            nc.gpsimd.memset(tri[:], 1.0).then_inc(tri_zero, 1)
            pool.wait_ge(tri_zero, 1)
            pool.wait_ge(iotas, 11)
            nc.gpsimd.affine_select(out=tri[:], in_=tri[:], compare_op=ALU.is_gt, fill=0.0, base=0,
                                    pattern=[[1, P]], channel_multiplier=-1).then_inc(iotas, 1)
            nc.gpsimd.memset(restart[:, :, 0:1], 0.0).then_inc(iotas, 1)

            def scatter(c):
                for h in range(2):
                    pool.wait_ge(rows_ready, 2 * c + h + 1)
                    for t in range(T // 2):
                        for q in range(2):
                            g = T * c + T // 2 * h + t
                            nc.gpsimd.indirect_dma_start(
                                out=zbuf, out_offset=bass.IndirectOffsetOnAxis(ap=posi[:, q, g:g + 1], axis=0),
                                in_=sortrow[h][:, t, q, :], in_offset=None).then_inc(scattered[h], 16)

            for s in STEPS:
                _, a, _, _ = roles(s)
                if a is None:
                    continue
                b = a % B
                with pool.Fori(0, PAIRS) as i:
                    for q in range(2):
                        pool.wait_ge(z_ready, i * 2 + (T * a + q + 1))
                        nc.gpsimd.tensor_copy(ZZ[:, ds(i * 2 + (T * b + q), 1), 0, :], Z[:, q:q + 1, :]) \
                            .then_inc(zh_ready, 1)
                    for q in range(2):
                        pool.wait_ge(zh_ready, i * 2 + (T * a + q + 1))
                        last = nc.gpsimd.tensor_tensor(ZZ[:, ds(i * 2 + (T * b + q), 1), 1, :], Z[:, q:q + 1, :],
                                                       ZZ[:, ds(i * 2 + (T * b + q), 1), 0, :], ALU.subtract)
                    last.then_inc(z_split, 1)
                    if s in (4, 8):
                        pool.wait_ge(wexp_scaled, i + (1 if s == 4 else PAIRS + 1))
                        c = ds(i * S, S)
                        hi, lo = (W1H, W1L) if s == 4 else (W2H, W2L)
                        nc.gpsimd.tensor_tensor(lo[:, c], Xw[:, c], hi[:, c], ALU.subtract).then_inc(wexp_lo, 1)
                for c, _ in prefix_uses(s):
                    scatter(c)
            for c, _ in prefix_uses(UNITS + 1):
                scatter(c)

            def put(j4, b):
                pool.wait_ge(y_ready, j4 + (b + 1))
                pool.wait_ge(carried, j4 + (b + 1))
                nc.gpsimd.tensor_tensor(carry[:, 0:1], carry[:, 1:2], carry[:, 1:2], ALU.add).then_inc(carried, 1)
                nc.gpsimd.indirect_dma_start(
                    out=ybuf, out_offset=bass.IndirectOffsetOnAxis(ap=tin[:, b, 2 * P:ROW].bitcast(U32), axis=0),
                    in_=y32[:, b, :], in_offset=None).then_inc(y_out[b], 16)

            with pool.Fori(0, NT // IN_BUFS) as i:
                for b in range(IN_BUFS):
                    put(i * IN_BUFS, b)

        @block.tensor
        def _(pe):
            def mm(o, w, r, start, stop):
                return nc.tensor.matmul(o, w, r, start=start, stop=stop)

            pe.wait_ge(const_ready, 4)
            pe.wait_ge(w_in, 16 * 6)
            nc.tensor.transpose(SC[:, 0, 0:P], W32[:, 0, :], ident32[:])
            nc.tensor.transpose(SC[:, 0, P:2 * P], W32[:, 1, :], ident32[:]).then_inc(wt_full, 1)
            pe.wait_ge(g_in, 48)
            nc.tensor.transpose(SC[:, 1, 0:E * HC], b1r[:], ident32[0:E * HC, 0:E * HC]).then_inc(b1_full, 1)

            for s in STEPS:
                u, a, m, v = roles(s)
                n_mx = mx_base(s)
                if v is not None and v < B:
                    pe.wait_ge(x_in[v], 16)
                    pe.wait_ge(mx_free, n_mx + 1)
                    for t in range(T):
                        last = nc.tensor.transpose(MX[:, t * P:(t + 1) * P], X[:, v, t * P:(t + 1) * P], ident32[:])
                    last.then_inc(mx_full, 1)
                    n_mx += 1
                    pe.wait_ge(w_ready, 3)
                    pe.wait_ge(x_lo, v + 1)
                if m is not None:
                    pe.wait_ge(proj_free, pr_base(m + 1) + 1)
                if a is not None:
                    pe.wait_ge(e32_free, T * (a + 1) + 2)
                lay = None if v is None else 0 if v < B else 1

                def transposes(i):
                    n = pr_base(v)
                    pe.wait_ge(proj_free, i * per_pair(v) + (n + 1))
                    pe.wait_ge(z_split, i + (PAIRS * (v - B) + 2))
                    for q in range(2):
                        t = i * 2 + (T * (v % B) + q)
                        for h in range(2):
                            last = mm(PR[:, q * P:(q + 1) * P], ZZ[:, ds(t, 1), h, :], ident16[:], h == 0, h == 1)
                    last.then_inc(proj_full, 1)

                def values(i):
                    o = 0 if v < B else 1
                    pe.wait_ge(proj_free, i * per_pair(v) + (pr_base(v) + o + 1))
                    for q in range(2):
                        c = i * 256 + q * P
                        o_ = PR[:, q * P:(q + 1) * P]
                        mm(o_, X16h[:, ds(c, P)], W16[:, lay, 2, 0, :], True, False)
                        mm(o_, X16h[:, ds(c, P)], W16[:, lay, 2, 1, :], False, False)
                        last = mm(o_, X16l[:, ds(c, P)], W16[:, lay, 2, 0, :], False, lay == 0)
                        if lay:
                            last = mm(o_, ones16[:, 0:P], B16[:, 2, :], False, True)
                    last.then_inc(proj_full, 1)

                def queries_keys(i):
                    o = per_pair(v) - 1
                    pe.wait_ge(proj_free, i * per_pair(v) + (pr_base(v) + o + 1))
                    for j in range(2):
                        o_ = PR[:, 256 * j:256 * j + 256]
                        mm(o_, W16[:, lay, j, 0, :], X16h[:, ds(i * 256, 256)], True, False)
                        mm(o_, W16[:, lay, j, 0, :], X16l[:, ds(i * 256, 256)], False, False)
                        last = mm(o_, W16[:, lay, j, 1, :], X16h[:, ds(i * 256, 256)], False, lay == 0)
                        if lay:
                            last = mm(o_, B16[:, j, :], ones16[:], False, True)
                    last.then_inc(proj_full, 1)

                def maxima(i, p):
                    pe.wait_ge(mx_free, i * 2 + (n_mx + p + 1))
                    for h in range(2):
                        last = mm(MX[:, h * HALF:(h + 1) * HALF], QH[:, m % 3, ds(i * 256 + p * P, P)],
                                  KH[:, m % 3, h * HALF:(h + 1) * HALF], True, True)
                    last.then_inc(mx_full, 1)

                def scores(i, p):
                    pe.wait_ge(sc_free, i * 2 + (T * u + p + 1))
                    w = u % 3
                    kh = KH[:, w, ds(i * 256 + p * P, P)]
                    for h in range(2):
                        c = slice(h * HALF, (h + 1) * HALF)
                        o_ = SC[:, p, c]
                        mm(o_, kh, QH[:, w, c], True, False)
                        mm(o_, kh, QL[:, w, c], False, False)
                        if u >= B:
                            mm(o_, KL[:, w, ds(i * 256 + p * P, P)], QH[:, w, c], False, False)
                        pe.wait_ge(diag_ready, T * u + T // 2 * (h + 1))
                        last = mm(o_, onesb[:], DG[:, u % 2, 4 * h:4 * h + 4, :], False, True)
                    last.then_inc(sc_full, 1)

                def outputs(i, p):
                    pe.wait_ge(pv_free, i * 2 + (T * a + p + 1))
                    for j in range(T):
                        e = ds(i * 256 + p * P, P)
                        mm(PV[:, 0:VW], EH[:, a % 2, j, e], VH[:, a % 4, j, :], j == 0, False)
                        mm(PV[:, 0:P], EH[:, a % 2, j, e], VL[:, a % 4, j, :], False, False)
                        last = mm(PV[:, 0:VW], EL[:, a % 2, j, e], VH[:, a % 4, j, :], False, j == T - 1)
                    last.then_inc(pv_full, 1)

                def logits(i):
                    pe.wait_ge(proj_free, i * 2 + (pr_base(v) + 2))
                    for q in range(2):
                        c = ds(i * 256 + q * P, P)
                        o_ = PR[:, q * E:(q + 1) * E]
                        mm(o_, X16h[:, c], WG16[:, 0, :], True, False)
                        mm(o_, X16l[:, c], WG16[:, 0, :], False, False)
                        last = mm(o_, X16h[:, c], WG16[:, 1, :], False, True)
                    last.then_inc(proj_full, 1)

                with pe.Fori(0, PAIRS) as i:
                    for p in range(2):
                        if u is not None:
                            scores(i, p)
                        if p == 0 and v is not None and v >= B:
                            transposes(i)
                        if a is not None:
                            outputs(i, p)
                        if m is not None:
                            maxima(i, p)
                        if v is not None and v >= UNITS:
                            if p == 1:
                                logits(i)
                        elif v is not None:
                            (values if p == 0 else queries_keys)(i)

                for c, n in prefix_uses(s):
                    pe.wait_ge(proj_free, n + 1)
                    pe.wait_ge(picked_ready, c + 1)
                    flat = picked[:].rearrange("p e t -> p (e t)")
                    mm(PR[:, 0:E * T], tri[:], flat, True, True)
                    mm(PR[:, E * T:2 * E * T], ones16[:, 0:P], flat, True, True).then_inc(proj_full, 1)

            FT = SC[:, 0, :].bitcast(F16)
            FH = [SC[:, 1, 0:HID], SC[:, 1, HID:2 * HID]]
            FY = [MX[:, 0:P], MX[:, HALF:HALF + P]]

            def rows_T(j, b, n):
                pe.wait_ge(tin_full[b], n)
                if j is not None:
                    pe.wait_ge(zt_ready, j - 1)
                f = FT[:, (b % 2) * 2 * HALF:(b % 2) * 2 * HALF + 2 * P]
                nc.tensor.transpose(f[:, 0:P], tin[:, b, 0:P], ident16[:])
                nc.tensor.transpose(f[:, P:2 * P], tin[:, b, P:2 * P], ident16[:]).then_inc(zt_full, 1)

            def hidden(j, b, first):
                e = expert(pe, tile_expert, b)
                pe.wait_ge(zt_ready, j + 1)
                if not first:
                    pe.wait_ge(h_ready, j - 1)
                for c in range(HC):
                    o_ = FH[b % 2][:, c * P:(c + 1) * P]
                    w = ds(e * HID + c * P, P)
                    mm(o_, W1H[:, w], zT[:, b % 2, 0:P], True, False)
                    mm(o_, W1H[:, w], zT[:, b % 2, P:2 * P], False, False)
                    last = mm(o_, W1L[:, w], zT[:, b % 2, 0:P], False, True)
                last.then_inc(h_full, 1)

            def output(j, b, first, carried_over=False):
                e = expert(pe, last_experts if carried_over else tile_expert, b % 2 if carried_over else b)
                pe.wait_ge(hl_ready, j + 1)
                if not first:
                    pe.wait_ge(y_ready, j - 1)
                for c in range(HC):
                    w = ds(e * HID + c * P, P)
                    k = slice(c * P, (c + 1) * P)
                    mm(FY[b % 2], hh[:, b % 2, k], W2H[:, w], c == 0, False)
                    mm(FY[b % 2], hh[:, b % 2, k], W2L[:, w], False, False)
                    last = mm(FY[b % 2], hl[:, b % 2, k], W2H[:, w], False, c == HC - 1)
                last.then_inc(y_full, 1)

            pe.wait_ge(table_ready, 3)
            pe.wait_ge(wexp_lo, 2 * PAIRS)
            pe.wait_ge(egap_ready, B)
            tile_expert = expert_registers(pe, "pe_expert", IN_BUFS)
            last_experts = expert_registers(pe, "pe_last_expert", 2)
            load_experts(pe, tile_expert, 0)
            rows_T(None, 0, 16)
            rows_T(None, 1, 16)
            hidden(0, 0, True)
            rows_T(2, 2, 16)
            hidden(1, 1, True)
            rows_T(3, 3, 16)
            R = IN_BUFS
            for j in range(2, R):
                hidden(j, j, False)
                output(j - 2, j - 2, j < 4)
                rows_T(j + 2, (j + 2) % R, 16 * ((j + 2) // R + 1))
            with pe.Fori(1, NT // R - 1) as i:
                load_experts(pe, last_experts, i * R - 2)
                load_experts(pe, tile_expert, i * R)
                for b in range(R):
                    hidden(i * R + b, b, False)
                    output(i * R + (b - 2), (b - 2) % R, False, b < 2)
                    rows_T(i * R + (b + 2), (b + 2) % R, i * 16 + 16 * ((b + 2) // R + 1))
            load_experts(pe, last_experts, NT - R - 2)
            load_experts(pe, tile_expert, NT - R)
            for j in range(NT - R, NT):
                hidden(j, j % R, False)
                output(j - 2, (j - 2) % R, False, j < NT - R + 2)
                if j + 2 < NT:
                    rows_T(j + 2, (j + 2) % R, 16 * (NT // R))
            for j in (NT - 2, NT - 1):
                output(j, j % R, False)

            for b in range(B):
                if b == 0:
                    pe.wait_ge(y_ready, NT)
                if b >= 2:
                    pe.wait_ge(o_ready, b - 1)
                for t in range(T):
                    pe.wait_ge(summed, T * b + t + 1)
                    last = nc.tensor.transpose(SC[:, b % 2, t * P:(t + 1) * P], TOK[:, T * b + t, :], ident32[:])
                last.then_inc(o_full, 1)

        @block.scalar
        def _(act):
            def cp(o, i_, scale=1.0):
                return nc.scalar.activation(o, i_, ACT.Copy, scale=scale)

            nc.scalar.preload_act_table_set("natural_log_exp_and_others")
            act.wait_ge(wt_full, 1)
            for j in range(2):
                for h in range(2):
                    cp(W16[:, 0, j, 0, CE * h:CE * h + CE], SC[:, 0, CE * j:CE * j + CE], WS)
            cp(W16[:, 0, 2, 0, :], SC[:, 0, P:2 * P], WS)
            cp(W16[:, 1, :, 0, :], W32[:, 2:5, :], WS).then_inc(w_hi, 1)
            act.wait_ge(b_in, 16 * 6)
            act.wait_ge(b1_full, 1)
            cp(b1T[:], SC[:, 1, 0:E * HC]).then_inc(b1_ready, 1)
            cp(WG16[:, 0, :], Wg32[:], WS)
            cp(B16[0:1, :, :], B32[0:1, :, :], WS)
            cp(B16[32:33, :, :], B32[32:33, :, :], WS).then_inc(w_hi, 1)

            for s in STEPS:
                u, a, m, v = roles(s)
                n_mx = mx_base(s)
                if v is not None and v < B:
                    if v > 0:
                        act.wait_ge(proj_full, pr_base(v))
                    act.wait_ge(x_in[v], 16)
                    cp(X16h[:], X[:, v, :]).then_inc(x_hi, 1)
                    act.wait_ge(mx_full, n_mx + 1)
                    cp(TOK[:, T * v:T * v + T, :], MX[:]).then_inc(mx_free, 1)
                if s in (3, 8):
                    act.wait_ge(wexp_in, 16 if s == 3 else 32)
                if s == 8:
                    act.wait_ge(pv_full, T * 7)

                def expert_weights(i):
                    c = ds(i * S, S)
                    cp((W1H if s == 3 else W2H)[:, c], Xw[:, c], WS)
                    cp(Xw[:, c], Xw[:, c], WS).then_inc(wexp_scaled, 1)

                def transposed(i):
                    act.wait_ge(proj_full, i * per_pair(v) + (pr_base(v) + 1))
                    cp(X16h[:, ds(i * 256, 256)], PR[:, 0:256]).then_inc(proj_hi, 1)

                def values(i):
                    o = per_pair(v) - 2
                    act.wait_ge(proj_full, i * per_pair(v) + (pr_base(v) + o + 1))
                    cp(VH[:, v % 4, ds(i * 2, 2), 0:P], PR[:, 0:256], 1 / WS).then_inc(proj_hi, 1)

                def queries_keys(i):
                    o = per_pair(v) - 1
                    act.wait_ge(proj_full, i * per_pair(v) + (pr_base(v) + o + 1))
                    cp(QH[:, v % 3, ds(i * 256, 256)], PR[:, 0:256], 1 / WS)
                    cp(KH[:, v % 3, ds(i * 256, 256)], PR[:, 256:512], 1 / WS).then_inc(proj_hi, 1)

                def exp_whole(i, p):
                    k = i * 2 + (T * u + p + 1)
                    act.wait_ge(sc_full, k)
                    act.wait_ge(e32_free, k)
                    nc.scalar.activation(E32[:, p, :], SC[:, p, :], ACT.Exp, scale=SCALE[0 if u < B else 1])

                def exp_high(i, p):
                    sc = SCALE[0 if u < B else 1]
                    nc.scalar.activation(EH[:, u % 2, ds(i * 2 + p, 1), :], SC[:, p, :], ACT.Exp, scale=sc) \
                        .then_inc(sc_free, 1)

                def rstds(i):
                    k = i + (PAIRS * a + 1)
                    act.wait_ge(ve_ready, k)
                    nc.scalar.activation(lnv[:], ve[:], ACT.Ln).then_inc(ln_ready, 1)
                    act.wait_ge(ln_ready, k)
                    nc.scalar.activation(r0[:], lnv[:], ACT.Exp, scale=-0.5).then_inc(r0_ready, 1)

                with act.Fori(0, PAIRS) as i:
                    for p in range(2):
                        if u is not None:
                            exp_whole(i, p)
                        if p == 0 and v is not None and v >= B:
                            transposed(i)
                        if u is not None:
                            exp_high(i, p)
                        if v is not None and v < UNITS:
                            (values if p == 0 else queries_keys)(i)
                        if p == 1 and a is not None:
                            rstds(i)
                        if p == 1 and s in (3, 8):
                            expert_weights(i)
                for c in [v - UNITS] if v is not None and v >= UNITS else []:
                    act.wait_ge(gap_ready, c + 1)
                    nc.scalar.activation(egap[:], gap[:], ACT.Exp).then_inc(egap_ready, 1)

            act.wait_ge(table_ready, 3)

            def gelu(j, b, first):
                e = expert(act, tile_expert, b)
                act.wait_ge(h_full, j + 1)
                if not first:
                    act.wait_ge(hl_ready, j - 1)
                for c in range(HC):
                    k = slice(c * P, (c + 1) * P)
                    last = nc.scalar.activation(h32[:, b % 2, k], SC[:, 1, (b % 2) * HID + c * P:(b % 2) * HID + c * P + P],
                                                ACT.Gelu, bias=b1T[:, ds(e * HC + c, 1)], scale=1 / WS)
                last.then_inc(h_ready, 1)

            tile_expert = expert_registers(act, "act_expert", IN_BUFS)
            load_experts(act, tile_expert, 0)
            for j in range(IN_BUFS):
                gelu(j, j, j < 2)
            with act.Fori(1, NT // IN_BUFS) as i:
                load_experts(act, tile_expert, i * IN_BUFS)
                for b in range(IN_BUFS):
                    gelu(i * IN_BUFS + b, b, False)
            for b in range(B):
                act.wait_ge(o_full, b + 1)
                cp(X[:, b, :], SC[:, b % 2, :]).then_inc(o_ready, 1)

        @block.vector
        def _(dve):
            nc.vector.memset(B32[:], 0.0).then_inc(bias_zeroed, 1)
            nc.vector.memset(B16[:], 0.0).then_inc(const_ready, 1)
            nc.vector.memset(ones16[:], 1.0)
            nc.vector.memset(onesb[:], 1.0).then_inc(const_ready, 1)
            nc.vector.memset(VH[:, :, :, P:VW], 1.0)
            nc.vector.memset(rec[:], 0.0).then_inc(mx_free, 1)
            nc.vector.memset(ve[:], 1.0).then_inc(sc_free, 2)
            nc.vector.memset(lnv[:], 0.0).then_inc(e32_free, 2)
            nc.vector.memset(nt[:], 0.0).then_inc(proj_free, 1)
            nc.vector.memset(nt2[:], 0.0).then_inc(pv_free, 1)
            nc.vector.memset(rstd[:], 0.0).then_inc(z_split, 1)

            dve.wait_ge(w_hi, 1)
            for j in range(2):
                for h in range(2):
                    w = W16[:, 0, j, :, CE * h:CE * h + CE]
                    nc.vector.scalar_tensor_tensor(out=w[:, 1, :], in0=SC[:, 0, CE * j:CE * j + CE], scalar=WS,
                                                   in1=w[:, 0, :], op0=ALU.mult, op1=ALU.subtract)
            nc.vector.scalar_tensor_tensor(out=W16[:, 0, 2, 1, :], in0=SC[:, 0, P:2 * P], scalar=WS,
                                           in1=W16[:, 0, 2, 0, :], op0=ALU.mult, op1=ALU.subtract).then_inc(w_ready, 1)
            nc.vector.scalar_tensor_tensor(out=W16[:, 1, :, 1, :], in0=W32[:, 2:5, :], scalar=WS,
                                           in1=W16[:, 1, :, 0, :], op0=ALU.mult, op1=ALU.subtract).then_inc(w_ready, 1)
            dve.wait_ge(w_hi, 2)
            r = slice(32, 33)
            nc.vector.scalar_tensor_tensor(out=B16[r, :, :], in0=B32[r, :, :], scalar=WS, in1=B16[r, :, :],
                                           op0=ALU.mult, op1=ALU.subtract).then_inc(w_ready, 1)
            nc.vector.scalar_tensor_tensor(out=WG16[:, 1, :], in0=Wg32[:], scalar=WS, in1=WG16[:, 0, :],
                                           op0=ALU.mult, op1=ALU.subtract).then_inc(w_ready, 1)
            dve.wait_ge(const_ready, 4)
            dve.wait_ge(iotas, 13)
            links = 0

            def link(instruction):
                nonlocal links
                links += 1
                instruction.then_inc(chain, 1)
                dve.wait_ge(chain, links)

            def choose(c):
                for t in range(T):
                    nc.vector.max(top[:, t, :], LG[:, t, :])
                link(nc.vector.memset(gap[:], 0.0))
                for t in range(T):
                    nc.vector.max_index(topi[:, t, :], top[:, t, :], LG[:, t, :])
                nc.vector.tensor_tensor(gap[:], top[:, :, 1], top[:, :, 0], ALU.subtract).then_inc(gap_ready, 1)
                link(nc.vector.memset(den[:], 0.0))
                link(nc.vector.tensor_copy(topf[:], topi[:, :, 0:2].rearrange("p t s -> p s t")))
                for q in range(2):
                    last = nc.vector.tensor_tensor(hot[:, q], iota_e[:],
                                                   topf[:, q:q + 1, :].to_broadcast([P, E, T]), ALU.is_equal)
                link(last)
                nc.vector.tensor_tensor(picked[:], hot[:, 0], hot[:, 1], ALU.add).then_inc(picked_ready, 1)
                dve.wait_ge(egap_ready, c + 1)
                link(nc.vector.tensor_scalar(den[:], egap[:], 1.0, None, ALU.add))
                w = WT[:, :, T * c:T * c + T]
                link(nc.vector.reciprocal(w[:, 0, :], den[:]))
                link(nc.vector.tensor_tensor(w[:, 1, :], egap[:], w[:, 0, :], ALU.mult))

            def place(c, n):
                def flat(t):
                    return t[:].rearrange("p e t -> p (e t)")
                dve.wait_ge(proj_full, n + 1)
                if c == 0:
                    dve.wait_ge(pv_full, T * 7)
                link(nc.vector.tensor_copy(flat(tots), PR[:, E * T:2 * E * T]))
                link(nc.vector.tensor_tensor_scan(flat(incl), flat(restart), flat(tots), 0.0, ALU.mult, ALU.add))
                link(nc.vector.tensor_tensor(befo[:], incl[:], tots[:], ALU.subtract))
                nc.vector.tensor_tensor(flat(rank), PR[:, 0:E * T], flat(befo), ALU.add).then_inc(proj_free, 1)
                dve.wait_ge(proj_free, n + 2)
                link(nc.vector.tensor_tensor(rows[:], rank[:], start[:].unsqueeze(2).to_broadcast([P, E, T]), ALU.add))
                link(nc.vector.tensor_tensor(start[:], start[:], incl[:, :, T - 1], ALU.add))
                for q in range(2):
                    last = nc.vector.tensor_tensor(mine[:, q], hot[:, q], rows[:], ALU.mult)
                link(last)
                for q in range(2):
                    last = nc.vector.reduce_sum(posf[:, q, :], mine[:, q].rearrange("p e t -> p t e"), AX.X)
                link(last)
                link(nc.vector.tensor_copy(posi[:, :, T * c:T * c + T], posf[:]))
                H = T // 2
                for h in range(2):
                    if c > 0:
                        dve.wait_ge(scattered[h], 16 * T * c)
                    g = T * c + H * h
                    for q in range(2):
                        nc.vector.tensor_copy(sortrow[h][:, :, q, 0:2 * P],
                                              ZZ[:, g:g + H].rearrange("p t a c -> p t (a c)"))
                        last = nc.vector.tensor_copy(sortrow[h][:, :, q, 2 * P:ROW].bitcast(I32),
                                                     ids[:, g:g + H, q:q + 1])
                    link(last)
                    nc.vector.memset(den[:], 0.0).then_inc(rows_ready, 1)

            def tile_table():
                link(nc.vector.tensor_tensor(cnt[:], start[:], ecap[:], ALU.subtract))
                link(nc.vector.tensor_tensor(over[:], cnt[:].unsqueeze(2).to_broadcast([P, E, TT + 1]),
                                             iota33[:].unsqueeze(1).to_broadcast([P, E, TT + 1]), ALU.is_gt))
                link(nc.vector.reduce_sum(tiles[:], over[:], AX.X))
                nc.vector.tensor_copy(padrow[:], start[:]).then_inc(table_ready, 1)
                link(nc.vector.tensor_tensor_scan(ends[:], ones8[:], tiles[:], 0.0, ALU.mult, ALU.add))
                link(nc.vector.tensor_scalar(skip[:], tiles[:], -1.0, float(CAP // P), ALU.mult, ALU.add))
                link(nc.vector.tensor_tensor(past[:], iotaj[:].unsqueeze(2).to_broadcast([P, NT, E]),
                                             ends[:].unsqueeze(1).to_broadcast([P, NT, E]), ALU.is_ge))
                link(nc.vector.tensor_tensor(jump[:], past[:], skip[:].unsqueeze(1).to_broadcast([P, NT, E]), ALU.mult))
                nc.vector.reduce_sum(tabf[:, 1, :], past[:], AX.X)
                link(nc.vector.reduce_sum(tabf[:, 0, :], jump[:], AX.X))
                nc.vector.tensor_tensor(tabi[:, 0, :], tabf[:, 0, :], iotaj[:], ALU.add).then_inc(table_ready, 1)
                nc.vector.tensor_scalar(tabi[:, 1, :], tabf[:, 1, :], float(E - 1), None, ALU.min) \
                    .then_inc(table_ready, 1)

            for s in STEPS:
                u, a, m, v = roles(s)
                n_mx = mx_base(s) + (1 if v is not None and v < B else 0)
                if v is not None and v < B:
                    dve.wait_ge(x_hi, v + 1)
                    nc.vector.tensor_tensor(X16l[:], X[:, v, :], X16h[:], ALU.subtract).then_inc(x_lo, 1)
                if a is not None and a < B:
                    dve.wait_ge(mx_free, mx_base(a - 2) + 2)
                def low(o, i_, hi, scale=1 / WS):
                    return nc.vector.scalar_tensor_tensor(out=o, in0=i_, scalar=scale, in1=hi, op0=ALU.mult,
                                                          op1=ALU.subtract)

                def transposed(i):
                    dve.wait_ge(proj_hi, i * (3 if v < UNITS else 1) + (hi_base(v) + 1))
                    low(X16l[:, ds(i * 256, 256)], PR[:, 0:256], X16h[:, ds(i * 256, 256)], 1.0) \
                        .then_inc(proj_free, 1)

                def values(i):
                    dve.wait_ge(proj_hi, i * per_pair(v) + (hi_base(v) + per_pair(v) - 1))
                    low(VL[:, v % 4, ds(i * 2, 2), :], PR[:, 0:256].rearrange("p (t c) -> p t c", c=P),
                        VH[:, v % 4, ds(i * 2, 2), 0:P]).then_inc(proj_free, 1)

                def queries(i):
                    dve.wait_ge(proj_hi, i * per_pair(v) + (hi_base(v) + per_pair(v)))
                    c = ds(i * 256, 256)
                    low(QL[:, v % 3, c], PR[:, 0:256], QH[:, v % 3, c])

                def keys(i):
                    c = ds(i * 256, 256)
                    if v < B:
                        r_ = slice(CE, P)
                        low(KH[r_, v % 3, c], PR[r_, 256:512], KH[r_, v % 3, c]).then_inc(proj_free, 1)
                    else:
                        low(KL[:, v % 3, c], PR[:, 256:512], KH[:, v % 3, c]).then_inc(proj_free, 1)

                def logits(i):
                    dve.wait_ge(proj_full, i * 2 + (pr_base(v) + 2))
                    nc.vector.scalar_tensor_tensor(out=LG[:, ds(i * 2, 2), :],
                                                   in0=PR[:, 0:2 * E].rearrange("p (t e) -> p t e", e=E),
                                                   scalar=1 / WS, in1=bgb[:].unsqueeze(1).to_broadcast([P, 2, E]),
                                                   op0=ALU.mult, op1=ALU.add).then_inc(proj_free, 1)

                def maxima(i, p):
                    dve.wait_ge(mx_full, i * 2 + (n_mx + p + 1))
                    nc.vector.reduce_max(mx[:, p:p + 1], MX[:], AX.X).then_inc(mx_free, 1)

                def diagonals(i, p):
                    dve.wait_ge(mx_free, i * 2 + (n_mx + p + 2))
                    nc.vector.tensor_scalar(DG[:, m % 2, ds(i * 2 + p, 1), :], identb[:], mx[:, p:p + 1], -1.0,
                                            ALU.mult, ALU.mult).then_inc(diag_ready, 1)

                def take_wait():
                    nc.vector.memset(carry[:, 2:3], 0.0)

                def written(i, p):
                    dve.wait_ge(pv_free, i * 2 + (T * a + p + 2))

                def counted(i, p):
                    dve.wait_ge(stats_ready, i * 2 + (T * a + p + 1))

                def e_low(i, p):
                    dve.wait_ge(sc_free, i * 2 + (T * u + p + 3))
                    nc.vector.tensor_tensor(EL[:, u % 2, ds(i * 2 + p, 1), :], E32[:, p:p + 1, :],
                                            EH[:, u % 2, ds(i * 2 + p, 1), :], ALU.subtract).then_inc(e32_free, 1)

                def sums(i, p):
                    k = i * 2 + (T * a + p)
                    dve.wait_ge(pv_full, k + 1)
                    nc.vector.reciprocal(rec[:], PV[:, P:VW]).then_inc(rec_ready, 1)

                def residual(i, p):
                    k = i * 2 + (T * a + p)
                    t = ds(i * 2 + (T * (a % B) + p), 1)
                    dve.wait_ge(rec_ready, k + 1)
                    nc.vector.scalar_tensor_tensor(out=TOK[:, t, :], in0=PV[:, 0:P], scalar=rec[:, 0:1],
                                                   in1=TOK[:, t, :], op0=ALU.mult, op1=ALU.add).then_inc(pv_free, 1)

                def statistics(i, p):
                    nc.vector.bn_stats(stats[:, p, :], TOK[:, ds(i * 2 + (T * (a % B) + p), 1), :]) \
                        .then_inc(stats_ready, 1)

                def moments(i, p):
                    nc.vector.bn_aggr(mv[:, p, :], stats[:, p, :]).then_inc(mv_ready, 1)

                def variances(i):
                    dve.wait_ge(mv_ready, i * 2 + (T * a + 2))
                    nc.vector.tensor_scalar(ve[:], mv[:, :, 1], EPS, None, ALU.add).then_inc(ve_ready, 1)

                def newton_square(i):
                    dve.wait_ge(r0_ready, i + (PAIRS * a + 1))
                    nc.vector.tensor_tensor(nt[:], r0[:], r0[:], ALU.mult).then_inc(newton, 1)

                def newton_slope(i):
                    dve.wait_ge(newton, i * 3 + (3 * PAIRS * a + 1))
                    nc.vector.scalar_tensor_tensor(out=nt2[:], in0=nt[:], scalar=-0.5, in1=ve[:], op0=ALU.mult,
                                                   op1=ALU.mult).then_inc(newton, 1)

                def newton_end(i):
                    dve.wait_ge(newton, i * 3 + (3 * PAIRS * a + 2))
                    nc.vector.scalar_tensor_tensor(out=rstd[:], in0=nt2[:], scalar=1.5, in1=r0[:], op0=ALU.add,
                                                   op1=ALU.mult).then_inc(newton, 1)

                def normalised(i):
                    dve.wait_ge(newton, i * 3 + (3 * PAIRS * a + 3))
                    dve.wait_ge(z_split, i + (PAIRS * a + 1))
                    for q in range(2):
                        nc.vector.tensor_scalar(Z[:, q:q + 1, :], TOK[:, ds(i * 2 + (T * (a % B) + q), 1), :],
                                                mv[:, q, 0:1], rstd[:, q:q + 1], ALU.subtract, ALU.mult) \
                            .then_inc(z_ready, 1)

                on_a, on_m, on_u, on_v = (r is not None for r in (a, m, u, v))
                with dve.Fori(0, PAIRS) as i:
                    if on_v and v >= B:
                        transposed(i)
                    if on_a:
                        sums(i, 0)
                        residual(i, 0)
                        written(i, 0)
                    if on_u:
                        e_low(i, 0)
                    elif on_a:
                        take_wait()
                    if on_a:
                        statistics(i, 0)
                        counted(i, 0)
                    if on_m:
                        maxima(i, 0)
                    elif on_a:
                        take_wait()
                    if on_a:
                        moments(i, 0)
                    if on_m:
                        diagonals(i, 0)
                    if on_v and v < UNITS:
                        values(i)
                    if on_a:
                        sums(i, 1)
                        residual(i, 1)
                        written(i, 1)
                    if on_u:
                        e_low(i, 1)
                    elif on_a:
                        take_wait()
                    if on_a:
                        statistics(i, 1)
                        counted(i, 1)
                    if on_v and v < UNITS:
                        queries(i)
                    elif on_a:
                        take_wait()
                    if on_a:
                        moments(i, 1)
                    if on_a:
                        variances(i)
                    if on_v and v < UNITS:
                        keys(i)
                    if on_v and v >= UNITS:
                        logits(i)
                    if on_m:
                        maxima(i, 1)
                        diagonals(i, 1)
                    if on_a:
                        newton_square(i)
                        newton_slope(i)
                        newton_end(i)
                        normalised(i)
                for c, n in prefix_uses(s):
                    if c < 3:
                        place(c, n)
                if on_v and v >= UNITS:
                    dve.wait_ge(proj_free, pr_base(v) + 2 * PAIRS + 1)
                    choose(v - UNITS)
            place(3, prefix_uses(UNITS + 1)[1][1])
            tile_table()

            FT = SC[:, 0, :].bitcast(F16)

            def rows_T(j, b):
                dve.wait_ge(zt_full, j + 1)
                nc.vector.tensor_copy(zT[:, b % 2, :], FT[:, (b % 2) * 2 * HALF:(b % 2) * 2 * HALF + 2 * P]) \
                    .then_inc(zt_ready, 1)

            def halves(j, b, first=False):
                dve.wait_ge(h_ready, j + 1)
                if not first:
                    dve.wait_ge(y_full, j - 1)
                nc.vector.tensor_copy(hh[:, b % 2, :], h32[:, b % 2, :]).then_inc(hh_ready, 1)
                dve.wait_ge(hh_ready, j + 1)
                nc.vector.tensor_tensor(hl[:, b % 2, :], h32[:, b % 2, :], hh[:, b % 2, :], ALU.subtract) \
                    .then_inc(hl_ready, 1)

            def output(j, b):
                e = expert(dve, tile_expert, b)
                dve.wait_ge(y_full, j + 1)
                nc.vector.scalar_tensor_tensor(out=y32[:, b, :], in0=MX[:, (b % 2) * HALF:(b % 2) * HALF + P],
                                               scalar=1 / WS, in1=b2b[:, ds(e * P, P)], op0=ALU.mult,
                                               op1=ALU.add).then_inc(y_ready, 1)

            dve.wait_ge(table_ready, 3)
            dve.wait_ge(b2_in, 16)
            R = IN_BUFS
            tile_expert = expert_registers(dve, "dve_expert", R)
            load_experts(dve, tile_expert, 0)
            rows_T(0, 0)
            rows_T(1, 1)
            for j in range(R):
                halves(j, j, j < 2)
                if j >= 2:
                    output(j - 2, j - 2)
                rows_T(j + 2, (j + 2) % R)
            with dve.Fori(1, NT // R - 1) as i:
                for b in range(R):
                    halves(i * R + b, b)
                    output(i * R + (b - 2), (b - 2) % R)
                    if b == 1:
                        load_experts(dve, tile_expert, i * R)
                    rows_T(i * R + (b + 2), (b + 2) % R)
            for j in range(NT - R, NT):
                halves(j, j % R)
                output(j - 2, (j - 2) % R)
                if j == NT - R + 1:
                    load_experts(dve, tile_expert, NT - R)
                if j + 2 < NT:
                    rows_T(j + 2, (j + 2) % R)
            for j in (NT - 2, NT - 1):
                output(j, j % R)

            for b in range(B):
                dve.wait_ge(y_in[b], 16)
                for t in range(T):
                    g = T * b + t
                    nc.vector.scalar_tensor_tensor(out=TOK[:, g, :], in0=yin[:, b % 2, t, 0, :], scalar=WT[:, 0, g:g + 1],
                                                   in1=TOK[:, g, :], op0=ALU.mult, op1=ALU.add).then_inc(mixed, 1)
                    if t > 0:
                        dve.wait_ge(mixed, g)
                        h = g - 1
                        nc.vector.scalar_tensor_tensor(out=TOK[:, h, :], in0=yin[:, b % 2, t - 1, 1, :],
                                                       scalar=WT[:, 1, h:h + 1], in1=TOK[:, h, :], op0=ALU.mult,
                                                       op1=ALU.add).then_inc(summed, 1)
                dve.wait_ge(mixed, T * (b + 1))
                h = T * (b + 1) - 1
                nc.vector.scalar_tensor_tensor(out=TOK[:, h, :], in0=yin[:, b % 2, T - 1, 1, :], scalar=WT[:, 1, h:h + 1],
                                               in1=TOK[:, h, :], op0=ALU.mult, op1=ALU.add).then_inc(summed, 1)


_INS = ["x", "L0_conv_theta_w", "L0_conv_phi_w", "L0_conv_proj_w", "L1_attn_Wk", "L1_attn_bk", "L1_attn_Wq",
        "L1_attn_bq", "L1_attn_Wv", "L1_attn_bv", "L1_ffn_Wg", "L1_ffn_bg", "L1_ffn_W1", "L1_ffn_b1", "L1_ffn_W2",
        "L1_ffn_b2"]
_SHAPES = {"x": (B, P, S), "L1_attn_bk": (1, P), "L1_attn_bq": (1, P), "L1_attn_bv": (1, P),
           "L1_ffn_bg": (E,), "L1_ffn_b1": (E * HC, P), "L1_ffn_b2": (E * P,)}


def kernel(**inputs):
    import numpy as np
    import concourse.bacc as bacc
    from concourse.bass_utils import run_bass_kernel_spmd

    nc = bacc.Bacc("TRN2", target_bir_lowering=False, num_devices=1)
    arrays, args = {}, []
    for name in _INS:
        a = np.ascontiguousarray(inputs[name])
        a = a.reshape(_SHAPES.get(name, a.shape))
        arrays[f"in_{name}_dram"] = a
        args.append(nc.dram_tensor(f"in_{name}_dram", a.shape, mybir.dt.from_np(a.dtype), kind="ExternalInput").ap())
    out = nc.dram_tensor("out_0_dram", (B, P, S), F32, kind="ExternalOutput").ap()
    build(nc, *args, out)
    r = run_bass_kernel_spmd(nc, [arrays], core_ids=[0])
    return r.results[0]["out_0_dram"].reshape(B, P, 32, 32)
```

```python
from contextlib import ExitStack

import concourse.bass as bass
from concourse import mybir

F32 = mybir.dt.float32
F16 = mybir.dt.float16
BF16 = mybir.dt.bfloat16
I32 = mybir.dt.int32
U32 = mybir.dt.uint32
ALU = mybir.AluOpType
ACT = mybir.ActivationFunctionType
AX = mybir.AxisListType

P = 128
B = 4
S = 1024
T = S // P
TT = B * T
PAIRS = T // 2
UNITS = 2 * B
CE = 64
SCALE = [CE ** -0.5, P ** -0.5]
EPS = 1e-5
WS = 64.0
HALF = 512
VW = P + 1


E = 8
HID = 512
HC = HID // P
TR = 2 * P
CAP = TT * P + TR
NT = TT * P * 2 // TR + E
MT = TT * P // TR
ROW = 2 * P + 4
PADS = E + E
IN_BUFS = 8


def build(nc, x, theta_w, phi_w, proj_w, Wk, bk, Wq, bq, Wv, bv, Wg, bg, W1, b1, W2, b2, out):
    ds = bass.ds
    with ExitStack() as ctx:
        def sb(name, shape, dt):
            return ctx.enter_context(nc.sbuf_tensor(name, shape, dt))

        def ps(name, shape, dt=F32):
            return ctx.enter_context(nc.psum_tensor(name, shape, dt))

        def sem(name):
            return ctx.enter_context(nc.semaphore(name))

        X = sb("X", [P, B, S], F32)
        X16h = sb("X16h", [P, S], F16)
        X16l = sb("X16l", [P, S], F16)
        TOK = sb("TOK", [P, TT, P], F32)
        ZZ = sb("ZZ", [P, TT, ROW], F16)
        ZN = ZZ[:, :, 2 * P:ROW].bitcast(I32)
        QK = sb("QK", [P, 3, 4, S], F16)
        QH, QL, KH, KL = (QK[:, :, j, :] for j in range(4))
        VH = sb("VH", [P, 4, T, VW], F16)
        VL = sb("VL", [P, 4, T, P], F16)
        EH = sb("EH", [P, 2, T, S], F16)
        EL = sb("EL", [P, 2, T, S], F16)
        E32 = sb("E32", [P, 2, S], F32)
        DG = sb("DG", [P, 2, T, P], BF16)
        mx = sb("mx", [P, T], F32)
        ident16 = sb("ident16", [P, P], F16)
        identb = sb("identb", [P, P], BF16)
        ident32 = sb("ident32", [P, P], F32)
        onesb = sb("onesb", [P, P], BF16)
        ones16 = sb("ones16", [P, 2 * P], F16)
        W32 = sb("W32", [P, 5, P], F32)
        W16 = sb("W16", [P, 2, 3, 2, P], F16)
        B32 = sb("B32", [P, 3, P], F32)
        B16 = sb("B16", [P, 3, P], F16)
        rec = sb("rec", [P, 1], F32)
        stats = sb("stats", [P, 2, 6], F32)
        mv = sb("mv", [P, 2, 2], F32)
        ve = sb("ve", [P, 2], F32)
        lnv = sb("lnv", [P, 2], F32)
        r0 = sb("r0", [P, 2], F32)
        nt = sb("nt", [P, 2], F32)
        nt2 = sb("nt2", [P, 2], F32)
        rstd = sb("rstd", [P, 2], F32)
        mean = sb("mean", [P, 2], F32)
        ZC = sb("ZC", [P, 2, P], F32)
        Z = sb("Z", [P, 2, P], F32)
        carry = sb("carry", [P, 4], F32)
        bgb = sb("bgb", [P, E], F32)
        Wg32 = sb("Wg32", [P, E], F32)
        WG16 = sb("WG16", [P, 2, E], F16)
        LG = sb("LG", [P, T, E], F32)
        top = sb("top", [P, T, 8], F32)
        topi = sb("topi", [P, T, 8], U32)
        topf = sb("topf", [P, 2, T], F32)
        iota_e = sb("iota_e", [P, E, T], F32)
        ecap = sb("ecap", [P, E], F32)
        start = sb("start", [P, E], F32)
        hot = sb("hot", [P, 2, E, T], F32)
        picked = sb("picked", [P, E, T], F16)
        tri = sb("tri", [P, P], F16)
        restart = sb("restart", [P, E, T], F32)
        tots = sb("tots", [P, E, T], F32)
        incl = sb("incl", [P, E, T], F32)
        befo = sb("befo", [P, E, T], F32)
        rank = sb("rank", [P, E, T], F32)
        rows = sb("rows", [P, E, T], F32)
        mine = sb("mine", [P, 2, E, T], F32)
        posf = sb("posf", [P, 2, T], F32)
        posi = sb("posi", [P, 2, B * T], U32)
        gap = sb("gap", [P, T], F32)
        egap = sb("egap", [P, T], F32)
        den = sb("den", [P, T], F32)
        WT = sb("WT", [P, 2, TT], F32)
        padid = sb("padid", [P, PADS, 2, 2], I32)
        zer = sb("zer", [P, 2, 2 * P], F16)
        EH0, EH1 = (EH[:, j].rearrange("p a b -> p (a b)") for j in range(2))
        EL0, EL1 = (EL[:, j].rearrange("p a b -> p (a b)") for j in range(2))
        E32f = E32[:].rearrange("p a b -> p (a b)")
        tile_ends = sb("tile_ends", [P, MT], F32)
        iotaj = sb("iotaj", [P, NT], F32)
        over = E32f[:, 2 * NT * E:2 * NT * E + E * MT].rearrange("p (e n) -> p e n", e=E)
        cnt = sb("cnt", [P, E], F32)
        tiles = sb("tiles", [P, E], F32)
        ends = sb("ends", [P, E], F32)
        skip = sb("skip", [P, E], F32)
        past, jump = (E32f[:, j * NT * E:(j + 1) * NT * E].rearrange("p (j e) -> p j e", e=E) for j in range(2))
        tabf = sb("tabf", [P, 2, NT], F32)
        tabi = sb("tabi", [P, 2, NT], I32)
        padrow = sb("padrow", [P, E], I32)
        ones8 = sb("ones8", [P, E], F32)
        W1H = sb("W1H", [P, E * HID], F16)
        W1L = sb("W1L", [P, E * HID], F16)
        W2HL = EL0.rearrange("p (g k d) -> p g k d", g=E * HC, k=2)
        b1r = sb("b1r", [E * HC, P], F32)
        b1T = sb("b1T", [P, E * HC], F32)
        b2b = DG[:].rearrange("p a b c -> p (a b c)").bitcast(F32)
        Xw = X[:].rearrange("p a b -> p (a b)")
        Xg = Xw.rearrange("p (g d) -> p g d", g=E * HC)
        tin = EH0[:, 0:IN_BUFS * 2 * ROW].rearrange("p (b q r) -> p b q r", q=2, r=ROW)
        zT = EH1[:, 0:4 * TR].rearrange("p (b h r) -> p b h r", b=2, h=2)
        hh, hl = (EH1[:, at:at + 2 * HC * TR].rearrange("p (b r) -> p b r", b=2)
                  for at in (4 * TR, 4 * TR + 2 * HC * TR))
        h32 = E32
        y32 = QK[:, 0].rearrange("p a b -> p (a b)").bitcast(F32).rearrange("p (b q c) -> p b q c", b=IN_BUFS, q=2)
        yid = sb("yid", [P, IN_BUFS, 2], U32)
        yin = EL1.bitcast(F32).rearrange("p (b t s c) -> p b t s c", b=2, t=T, s=2)

        zbuf = nc.dram_tensor("zbuf", [E * CAP + E * TR, ROW], F16, kind="Internal").ap()
        ybuf = nc.dram_tensor("ybuf", [2 * TT * P + PADS * TR, P], F32, kind="Internal").ap()

        SC = ps("SC", [P, 2, HALF])
        MX = ps("MX", [P, S])
        PV = ps("PV", [P, 2, HALF])
        PR = ps("PR", [P, 2, HALF])
        WIDE = [t[:].rearrange("p b n -> p (b n)") for t in (SC, PV)]

        x_in = [sem(f"x_in{b}") for b in range(B)]
        w_in = sem("w_in")
        b_in = sem("b_in")
        const_ready = sem("const_ready")
        zero_ready = sem("zero_ready")
        bias_zeroed = sem("bias_zeroed")
        wt_full = sem("wt_full")
        w_hi = sem("w_hi")
        w_ready = sem("w_ready")
        x_hi = sem("x_hi")
        x_lo = sem("x_lo")
        mx_full = sem("mx_full")
        mx_free = sem("mx_free")
        max_ready = sem("max_ready")
        diag_ready = sem("diag_ready")
        sc_full = sem("sc_full")
        sc_free = sem("sc_free")
        e32_free = [sem(f"e32_free{p}") for p in range(2)]
        half_full = [sem(f"half_full{h}") for h in range(3)]
        half_high = [sem(f"half_high{h}") for h in range(3)]
        half_free = [sem(f"half_free{h}") for h in range(3)]
        pv_full = sem("pv_full")
        pv_free = sem("pv_free")
        rec_ready = sem("rec_ready")
        stats_ready = sem("stats_ready")
        mv_ready = sem("mv_ready")
        ve_ready = sem("ve_ready")
        ln_ready = sem("ln_ready")
        r0_ready = sem("r0_ready")
        newton = sem("newton")
        z_ready = sem("z_ready")
        zh_ready = sem("zh_ready")
        zc_ready = sem("zc_ready")
        z_split = sem("z_split")
        out_done = sem("out_done")
        g_in = sem("g_in")
        iotas = sem("iotas")
        tri_zero = sem("tri_zero")
        wexp_in = sem("wexp_in")
        wexp_scaled = sem("wexp_scaled")
        wexp_lo = sem("wexp_lo")
        b1_full = sem("b1_full")
        b1_ready = sem("b1_ready")
        b2_in = sem("b2_in")
        chain = sem("chain")
        picked_ready = sem("picked_ready")
        gap_ready = sem("gap_ready")
        egap_ready = sem("egap_ready")
        rows_ready = sem("rows_ready")
        pos_ready = sem("pos_ready")
        scattered = [sem(f"scattered{h}") for h in range(2)]
        table_ready = sem("table_ready")
        pad_done = sem("pad_done")
        pad_static = sem("pad_static")
        tin_full = [sem(f"tin_full{b}") for b in range(IN_BUFS)]
        zt_full = sem("zt_full")
        zt_ready = sem("zt_ready")
        h_full = sem("h_full")
        h_ready = sem("h_ready")
        hh_ready = sem("hh_ready")
        hl_ready = sem("hl_ready")
        y_full = sem("y_full")
        y_half = sem("y_half")
        y_ready = sem("y_ready")
        carried = sem("carried")
        y_out = [sem(f"y_out{b}") for b in range(IN_BUFS)]
        y_in = [sem(f"y_in{b}") for b in range(B)]
        mixed = sem("mixed")
        summed = sem("summed")
        o_full = sem("o_full")
        o_ready = sem("o_ready")

        STEPS = range(-2, UNITS + 2)

        def pair_before(s):
            return (s - 2, PAIRS - 1) if s > 1 else None

        def roles(s):
            return (s if 0 <= s < UNITS else None, s - 1 if 0 <= s - 1 < UNITS else None,
                    s + 1 if 0 <= s + 1 < UNITS else None, s + 2 if s + 2 < UNITS + B else None)

        USES = [{"values": (0, 0), "queries": (1, 0), "keys": (2, 0)},
                {"values": (0, 0), "queries": (1, 0), "keys": (0, 1)},
                {"rows": (0, 0), "values": (1, 0), "queries": (0, 1), "keys": (1, 1)},
                {"rows": (0, 0), "logits": (1, 0)}]

        def uses(v):
            return USES[0 if v < 3 else 1 if v < B else 2 if v < UNITS else 3]

        def per_pair(v, half):
            return sum(h == half for h, _ in uses(v).values())

        def uses_before(v, half):
            return sum(PAIRS * per_pair(w, half) for w in range(v)) + (max(0, v - UNITS) if half == 0 else 0)

        def used(v, name, i):
            half, k = uses(v)[name]
            return i * per_pair(v, half) + (uses_before(v, half) + k)

        def highs(v, name, i):
            half, k = uses(v)[name]
            ranks = max(0, v - UNITS) if half == 0 else 0
            return i * per_pair(v, half) + (uses_before(v, half) - ranks + k)

        def product(v, name, width=256):
            half, _ = uses(v)[name]
            return half, (PR[:, half, 0:width] if half < 2 else PV[:, 0, 0:width])

        def ranked(c):
            return uses_before(UNITS + c, 0) + (PAIRS if c < B - 1 else 0)

        def mx_base(s):
            return sum((1 if t + 2 < B else 0) + (T if 0 <= t + 1 < UNITS else 0) for t in range(-2, s))

        def expert_registers(engine, name, n):
            return [engine.alloc_register(f"{name}{b}") for b in range(n)]

        def load_experts(engine, registers, j):
            n = len(registers)
            engine.load(registers, tabi[0:1, 1, ds(j, n)])

        def expert(engine, registers, b):
            return engine.snap(registers[b], min_val=0, max_val=E - 1)

        block = ctx.enter_context(nc.Block())

        @block.sync
        def _(sp):
            sp.dma_start(W32[0:CE, 0, :], theta_w).then_inc(w_in, 16)
            sp.dma_start(W32[CE:P, 0, :], phi_w).then_inc(w_in, 16)
            sp.dma_start(W32[:, 1, :], proj_w).then_inc(w_in, 16)
            for b in range(B):
                sp.dma_start(X[:, b, :], x[b]).then_inc(x_in[b], 16)
            for j, w in enumerate((Wq, Wk, Wv)):
                sp.dma_start(W32[:, 2 + j, :], w).then_inc(b_in, 16)
            sp.wait_ge(bias_zeroed, 1)
            for j, v in enumerate((bq, bk, bv)):
                for r in (0, 32):
                    sp.dma_start(B32[r:r + 1, j, :], v).then_inc(b_in, 16)
            sp.dma_start(Wg32[:], Wg).then_inc(g_in, 16)
            sp.dma_start(bgb[:], bg.partition_broadcast(P)).then_inc(g_in, 16)
            sp.dma_start(b1r[:], b1).then_inc(g_in, 16)
            sp.wait_ge(iotas, 7)
            unused = zbuf[E * CAP:, :].rearrange("(n q p) r -> n p q r", q=2, p=P)
            for n in range(E):
                sp.dma_start(unused[n, :, :, 0:2 * P], zer[:]).then_inc(pad_static, 16)
                sp.dma_start(unused[n, :, :, 2 * P:ROW], padid[:, E + n].bitcast(F16)).then_inc(pad_static, 16)
            sp.wait_ge(x_lo, B)
            sp.wait_ge(mx_full, mx_base(1) + 1)
            sp.dma_start(Xw.rearrange("p (e h) -> p e h", e=E), W1.rearrange("e d h -> d e h")).then_inc(wexp_in, 16)
            sp.wait_ge(wexp_lo, PAIRS)
            sp.dma_start(Xw.rearrange("p (e c d) -> p e c d", e=E, c=HC),
                         W2.rearrange("e (c h) d -> h e c d", c=HC)).then_inc(wexp_in, 16)
            sp.wait_ge(sc_full, 2 * T * UNITS)
            sp.dma_start(b2b, b2.partition_broadcast(P)).then_inc(b2_in, 16)
            sp.wait_ge(table_ready, 2)
            for e in range(E):
                r = sp.value_load(padrow[0:1, e:e + 1], min_val=e * CAP, max_val=e * CAP + TT * P)
                pad = zbuf[ds(r, TR), :].rearrange("(q p) r -> p q r", q=2)
                sp.dma_start(pad[:, :, 0:2 * P], zer[:]).then_inc(pad_done, 16)
                sp.dma_start(pad[:, :, 2 * P:ROW], padid[:, e].bitcast(F16)).then_inc(pad_done, 16)
            sp.wait_ge(pad_done, 16 * 2 * E)
            sp.wait_ge(pad_static, 16 * 2 * E)
            for h in range(2):
                sp.wait_ge(scattered[h], 16 * T * B)

            def load_tile(j, b, again):
                r = sp.value_load(tabi[0:1, 0, ds(j, 1)], min_val=0, max_val=(E * CAP + E * TR) // TR - 1)
                if again is not None:
                    sp.wait_ge(y_out[b], again)
                sp.dma_start(tin[:, b], zbuf[ds(r * TR, TR), :].rearrange("(q p) r -> p q r", q=2)) \
                    .then_inc(tin_full[b], 16)

            for b in range(IN_BUFS):
                load_tile(b, b, None)
            with sp.Fori(1, NT // IN_BUFS) as i:
                for b in range(IN_BUFS):
                    load_tile(i * IN_BUFS + b, b, i * 32)
            for b in range(IN_BUFS):
                sp.wait_ge(y_out[b], 32 * (NT // IN_BUFS))
            for b in range(B):
                if b >= 2:
                    sp.wait_ge(summed, T * (b - 1))
                sp.dma_start(yin[:, b % 2], ybuf[2 * S * b:2 * S * (b + 1), :].rearrange("(t p s) c -> p t s c", p=P, s=2)) \
                    .then_inc(y_in[b], 16)
            for b in range(B):
                sp.wait_ge(o_ready, b + 1)
                sp.dma_start(out[b], X[:, b, :]).then_inc(out_done, 16)
            sp.wait_ge(out_done, 16 * B)

        @block.gpsimd
        def _(pool):
            nc.gpsimd.memset(ident32[:], 0.0).then_inc(zero_ready, 1)
            pool.wait_ge(zero_ready, 1)
            nc.gpsimd.affine_select(out=ident32[:], in_=ident32[:], compare_op=ALU.not_equal, fill=1.0, base=0,
                                    pattern=[[-1, P]], channel_multiplier=1).then_inc(zero_ready, 1)
            pool.wait_ge(zero_ready, 2)
            nc.gpsimd.tensor_copy(ident16[:], ident32[:]).then_inc(const_ready, 1)
            nc.gpsimd.tensor_copy(identb[:], ident32[:]).then_inc(const_ready, 1)

            nc.gpsimd.memset(carry[:, 0:2], 0.0).then_inc(iotas, 1)
            nc.gpsimd.memset(carry[:, 3:4], 0.0).then_inc(carried, 1)
            iot = nc.gpsimd.iota
            iot(ZN[:, :, 0], [[2 * P, TT]], base=0, channel_multiplier=2).then_inc(iotas, 1)
            nc.gpsimd.memset(padid[:, :, :, 1], 2 * E)
            iot(padid[:, :, :, 0], [[TR, PADS], [P, 2]], base=2 * TT * P - 1, channel_multiplier=1) \
                .then_inc(iotas, 1)
            nc.gpsimd.memset(zer[:], 0.0).then_inc(iotas, 1)
            kw = dict(channel_multiplier=0, allow_small_or_imprecise_dtypes=True)
            iot(iota_e[:], [[1, E], [0, T]], base=0, **kw).then_inc(iotas, 1)
            iot(tile_ends[:], [[TR, MT]], base=0, **kw).then_inc(iotas, 1)
            iot(iotaj[:], [[1, NT]], base=0, **kw).then_inc(iotas, 1)
            iot(ecap[:], [[CAP, E]], base=0, **kw).then_inc(iotas, 1)
            iot(start[:], [[CAP, E]], base=0, **kw).then_inc(iotas, 1)
            nc.gpsimd.memset(restart[:], 1.0).then_inc(iotas, 1)
            nc.gpsimd.memset(ones8[:], 1.0).then_inc(iotas, 1)
            nc.gpsimd.memset(tri[:], 1.0).then_inc(tri_zero, 1)
            pool.wait_ge(tri_zero, 1)
            pool.wait_ge(iotas, 11)
            nc.gpsimd.affine_select(out=tri[:], in_=tri[:], compare_op=ALU.is_gt, fill=0.0, base=0,
                                    pattern=[[1, P]], channel_multiplier=-1).then_inc(iotas, 1)
            nc.gpsimd.memset(restart[:, :, 0:1], 0.0).then_inc(iotas, 1)

            def scatter(t):
                for q in range(2):
                    nc.gpsimd.indirect_dma_start(
                        out=zbuf, out_offset=bass.IndirectOffsetOnAxis(ap=posi[:, q, t:t + 1], axis=0),
                        in_=ZZ[:, t, :], in_offset=None).then_inc(scattered[q], 16)

            for s in STEPS:
                u, a, _, _ = roles(s)
                before = pair_before(s)
                if u is None and a is None and before is None:
                    continue

                def normalise(a_, i):
                    n = i + (PAIRS * a_ + 1)
                    t = ds(i * 2 + T * (a_ % B), 2)

                    def wide(r):
                        return r[:].unsqueeze(2).to_broadcast([P, 2, P])
                    pool.wait_ge(ve_ready, n)
                    nc.gpsimd.tensor_tensor(ZC[:], TOK[:, t, :], wide(mean), ALU.subtract).then_inc(zc_ready, 1)
                    pool.wait_ge(zc_ready, n)
                    pool.wait_ge(newton, i * 3 + (3 * PAIRS * a_ + 3))
                    nc.gpsimd.tensor_tensor(ZZ[:, t, 0:P], ZC[:], wide(rstd), ALU.mult)
                    nc.gpsimd.tensor_tensor(Z[:], ZC[:], wide(rstd), ALU.mult).then_inc(zh_ready, 1)

                def split(a_, i):
                    pool.wait_ge(zh_ready, i + (PAIRS * a_ + 1))
                    t = ds(i * 2 + T * (a_ % B), 2)
                    nc.gpsimd.tensor_tensor(ZZ[:, t, P:2 * P], Z[:], ZZ[:, t, 0:P], ALU.subtract).then_inc(z_split, 1)

                def e_low(i):
                    pool.wait_ge(sc_free, i * 4 + (2 * T * u + 6))
                    nc.gpsimd.tensor_tensor(EL[:, u % 2, ds(i * 2 + 1, 1), :], E32[:, 1:2, :],
                                            EH[:, u % 2, ds(i * 2 + 1, 1), :], ALU.subtract).then_inc(e32_free[1], 1)

                def pair(i, before):
                    if before is not None and s < UNITS:
                        normalise(*before)
                        split(*before)
                    if u is not None:
                        e_low(i)

                if s < UNITS - 1:
                    def low_weights(i):
                        pool.wait_ge(wexp_scaled, i + 1)
                        c = ds(i * S, S)
                        nc.gpsimd.tensor_tensor(W1L[:, c], Xw[:, c], W1H[:, c], ALU.subtract).then_inc(wexp_lo, 1)

                    pair(0, before)
                    if s == 4:
                        low_weights(0)
                    with pool.Fori(1, PAIRS) as i:
                        pair(i, None if a is None else (a, i - 1))
                        if s == 4:
                            low_weights(i)
                elif a is not None:
                    c = s - UNITS + 1
                    for i in range(PAIRS):
                        pair(i, (a, i - 1) if i else before)
                        if i == 0:
                            pool.wait_ge(rows_ready, c + 1)
                        scatter(T * c + 2 * i)
                        scatter(T * c + 2 * i + 1)
            for t in range(2 * T, TT):
                if t % T == 0:
                    pool.wait_ge(rows_ready, t // T + 1)
                scatter(t)

            def put(j4, b):
                pool.wait_ge(y_ready, j4 + (b + 1))
                pool.wait_ge(carried, j4 + (b + 1))
                nc.gpsimd.tensor_tensor(carry[:, 0:1], carry[:, 1:2], carry[:, 1:2], ALU.add).then_inc(carried, 1)
                for q in range(2):
                    nc.gpsimd.indirect_dma_start(
                        out=ybuf, out_offset=bass.IndirectOffsetOnAxis(ap=yid[:, b, q:q + 1], axis=0),
                        in_=y32[:, b, q, :], in_offset=None).then_inc(y_out[b], 16)

            with pool.Fori(0, NT // IN_BUFS) as i:
                for b in range(IN_BUFS):
                    put(i * IN_BUFS, b)

        @block.tensor
        def _(pe):
            def mm(o, w, r, start, stop):
                return nc.tensor.matmul(o, w, r, start=start, stop=stop)

            pe.wait_ge(const_ready, 4)
            pe.wait_ge(w_in, 16 * 3)
            nc.tensor.transpose(SC[:, 0, 0:P], W32[:, 0, :], ident32[:])
            nc.tensor.transpose(SC[:, 0, P:2 * P], W32[:, 1, :], ident32[:]).then_inc(wt_full, 1)

            for s in STEPS:
                u, a, m, v = roles(s)
                n_mx = mx_base(s)
                if v is not None and v < B:
                    pe.wait_ge(x_in[v], 16)
                    pe.wait_ge(mx_free, n_mx + 1)
                    for t in range(T):
                        last = nc.tensor.transpose(MX[:, t * P:(t + 1) * P], X[:, v, t * P:(t + 1) * P], ident32[:])
                    last.then_inc(mx_full, 1)
                    n_mx += 1
                    if s == -1:
                        pe.wait_ge(g_in, 48)
                        nc.tensor.transpose(SC[:, 1, 0:E * HC], b1r[:], ident32[0:E * HC, 0:E * HC]).then_inc(b1_full, 1)
                    pe.wait_ge(w_ready, 1)
                    pe.wait_ge(x_lo, v + 1)
                if m is not None:
                    for h in range(3):
                        pe.wait_ge(half_free[h], uses_before(m + 1, h) + 1)
                if a is not None:
                    for p in range(2):
                        pe.wait_ge(e32_free[p], PAIRS * (a + 1) + 1)
                lay = None if v is None else 0 if v < B else 1
                if v == B:
                    pe.wait_ge(w_ready, 4)

                def transposes(i):
                    half, o_ = product(v, "rows")
                    pe.wait_ge(half_free[half], used(v, "rows", i) + 1)
                    pe.wait_ge(z_split, i + (PAIRS * (v - B) + 2))
                    for q in range(2):
                        t = i * 2 + (T * (v % B) + q)
                        for h in range(2):
                            last = mm(o_[:, q * P:(q + 1) * P], ZZ[:, ds(t, 1), h * P:(h + 1) * P], ident16[:],
                                      h == 0, h == 1)
                    last.then_inc(half_full[half], 1)

                def values(i):
                    half, o = product(v, "values")
                    pe.wait_ge(half_free[half], used(v, "values", i) + 1)
                    if lay:
                        pe.wait_ge(half_free[0], used(v, "rows", i) + 2)
                    for q in range(2):
                        c = i * 256 + q * P
                        o_ = o[:, q * P:(q + 1) * P]
                        mm(o_, X16h[:, ds(c, P)], W16[:, lay, 2, 0, :], True, False)
                        mm(o_, X16h[:, ds(c, P)], W16[:, lay, 2, 1, :], False, False)
                        last = mm(o_, X16l[:, ds(c, P)], W16[:, lay, 2, 0, :], False, lay == 0)
                        if lay:
                            last = mm(o_, ones16[:, 0:P], B16[:, 2, :], False, True)
                    last.then_inc(half_full[half], 1)

                def projected(name, i):
                    half, o_ = product(v, name)
                    j = 0 if name == "queries" else 1
                    pe.wait_ge(half_free[half], used(v, name, i) + 1)
                    mm(o_, W16[:, lay, j, 0, :], X16h[:, ds(i * 256, 256)], True, False)
                    mm(o_, W16[:, lay, j, 0, :], X16l[:, ds(i * 256, 256)], False, False)
                    last = mm(o_, W16[:, lay, j, 1, :], X16h[:, ds(i * 256, 256)], False, lay == 0)
                    if lay:
                        last = mm(o_, B16[:, j, :], ones16[:], False, True)
                    last.then_inc(half_full[half], 1)

                def maxima(i, p):
                    pe.wait_ge(mx_free, i * 2 + (n_mx + p + 1))
                    for h in range(2):
                        last = mm(MX[:, h * HALF:(h + 1) * HALF], QH[:, m % 3, ds(i * 256 + p * P, P)],
                                  KH[:, m % 3, h * HALF:(h + 1) * HALF], True, True)
                    last.then_inc(mx_full, 1)

                def scores(i, p, h):
                    w = u % 3
                    kh = KH[:, w, ds(i * 256 + p * P, P)]
                    pe.wait_ge(sc_free, i * 4 + (2 * T * u + 2 * p + h + 1))
                    c = slice(h * HALF, (h + 1) * HALF)
                    o_ = SC[:, h, :]
                    mm(o_, kh, QH[:, w, c], True, False)
                    mm(o_, kh, QL[:, w, c], False, False)
                    if u >= B:
                        mm(o_, KL[:, w, ds(i * 256 + p * P, P)], QH[:, w, c], False, False)
                    pe.wait_ge(diag_ready, T * u + T // 2 * (h + 1))
                    mm(o_, onesb[:], DG[:, u % 2, 4 * h:4 * h + 4, :], False, True).then_inc(sc_full, 1)

                def outputs(i, p):
                    pe.wait_ge(pv_free, i * 2 + (T * a + p + 1))
                    o_ = PV[:, p, 0:VW]
                    for j in range(T):
                        e = ds(i * 256 + p * P, P)
                        mm(o_, EH[:, a % 2, j, e], VH[:, a % 4, j, :], j == 0, False)
                        mm(o_[:, 0:P], EH[:, a % 2, j, e], VL[:, a % 4, j, :], False, False)
                        last = mm(o_, EL[:, a % 2, j, e], VH[:, a % 4, j, :], False, j == T - 1)
                    last.then_inc(pv_full, 1)

                def router(o_, c):
                    mm(o_, X16h[:, c], WG16[:, 0, :], True, False)
                    mm(o_, X16l[:, c], WG16[:, 0, :], False, False)
                    return mm(o_, X16h[:, c], WG16[:, 1, :], False, True)

                def logits(i):
                    half, o_ = product(v, "logits")
                    pe.wait_ge(half_free[half], used(v, "logits", i) + 1)
                    pe.wait_ge(half_free[0], used(v, "rows", i) + 2)
                    for q in range(2):
                        last = router(o_[:, q * E:(q + 1) * E], ds(i * 256 + q * P, P))
                    last.then_inc(half_full[half], 1)

                def rank(c):
                    pe.wait_ge(half_free[0], ranked(c) + 1)
                    pe.wait_ge(picked_ready, c + 1)
                    flat = picked[:].rearrange("p e t -> p (e t)")
                    mm(PR[:, 0, 0:E * T], tri[:], flat, True, True)
                    mm(PR[:, 0, E * T:2 * E * T], ones16[:, 0:P], flat, True, True).then_inc(half_full[0], 1)

                if v == UNITS + B - 1:
                    for h in range(2):
                        if h == 0:
                            pe.wait_ge(mx_free, n_mx + 1)
                        for t in range(h * PAIRS, (h + 1) * PAIRS):
                            if t % 2 == 0:
                                pe.wait_ge(z_split, t // 2 + (PAIRS * (v - B) + 2))
                            for k in range(2):
                                last = mm(MX[:, t * P:(t + 1) * P], ZZ[:, T * (v % B) + t, k * P:(k + 1) * P],
                                          ident16[:], k == 0, k == 1)
                        last.then_inc(mx_full, 1)
                    half, o_ = product(v, "logits")
                    pe.wait_ge(half_free[half], uses_before(v, half) + 1)
                    for h in range(2):
                        pe.wait_ge(mx_free, n_mx + h + 2)
                        for t in range(h * PAIRS, (h + 1) * PAIRS):
                            last = router(o_[:, t * E:(t + 1) * E], slice(t * P, (t + 1) * P))
                    last.then_inc(half_full[half], 1)
                    rank(v - UNITS)
                    continue

                with pe.Fori(0, PAIRS) as i:
                    if u is not None:
                        scores(i, 0, 0)
                    if v is not None and v >= B:
                        transposes(i)
                    if u is not None:
                        scores(i, 0, 1)
                    if a is not None:
                        outputs(i, 0)
                    if u is not None:
                        scores(i, 1, 0)
                    if m is not None:
                        maxima(i, 0)
                    if v is not None and v < UNITS:
                        values(i)
                    if u is not None:
                        scores(i, 1, 1)
                    if v is not None and v < UNITS:
                        projected("queries", i)
                    if a is not None:
                        outputs(i, 1)
                    if v is not None and v < UNITS:
                        projected("keys", i)
                    if v is not None and v >= UNITS:
                        logits(i)
                    if m is not None:
                        maxima(i, 1)

                if v is not None and v >= UNITS:
                    rank(v - UNITS)

            FT = [PR[:, h, :].bitcast(F16) for h in range(2)]

            def rows_T(j, b, n):
                pe.wait_ge(tin_full[b], n)
                if j is not None:
                    pe.wait_ge(zt_ready, j - 1)
                for h in range(2):
                    for q in range(2):
                        at = h * TR + q * P
                        last = nc.tensor.transpose(FT[b % 2][:, at:at + P], tin[:, b, q, h * P:(h + 1) * P], ident16[:])
                last.then_inc(zt_full, 1)

            def hidden(j, b, first):
                e = expert(pe, tile_expert, b)
                pe.wait_ge(zt_ready, j + 1)
                if not first:
                    pe.wait_ge(h_ready, j - 1)
                for c in range(HC):
                    o_ = WIDE[b % 2][:, c * TR:(c + 1) * TR]
                    w = ds(e * HID + c * P, P)
                    mm(o_, W1H[:, w], zT[:, b % 2, 0, :], True, False)
                    mm(o_, W1H[:, w], zT[:, b % 2, 1, :], False, False)
                    last = mm(o_, W1L[:, w], zT[:, b % 2, 0, :], False, True)
                last.then_inc(h_full, 1)

            def output(j, b, first, carried_over=False):
                e = expert(pe, last_experts if carried_over else tile_expert, b % 2 if carried_over else b)
                pe.wait_ge(hl_ready, j + 1)
                if not first:
                    pe.wait_ge(y_ready, j - 1)
                for q in range(2):
                    o_ = MX[:, (b % 2) * HALF + q * TR:(b % 2) * HALF + (q + 1) * TR]
                    for c in range(HC):
                        k = slice(c * TR + q * P, c * TR + (q + 1) * P)
                        g = ds(e * HC + c, 1)
                        def high():
                            return mm(o_, hh[:, b % 2, k], W2HL[:, g, :, :], c == 0, c == HC - 1)

                        def low():
                            mm(o_[:, 0:P], hl[:, b % 2, k], W2HL[:, g, 0, :], False, False)
                        if c == 0:
                            high()
                            low()
                        else:
                            low()
                            last = high()
                last.then_inc(y_full, 1)

            pe.wait_ge(table_ready, 3)
            pe.wait_ge(wexp_lo, 2 * PAIRS)
            pe.wait_ge(egap_ready, B)
            tile_expert = expert_registers(pe, "pe_expert", IN_BUFS)
            last_experts = expert_registers(pe, "pe_last_expert", 2)
            load_experts(pe, tile_expert, 0)
            rows_T(None, 0, 16)
            rows_T(None, 1, 16)
            hidden(0, 0, True)
            rows_T(2, 2, 16)
            hidden(1, 1, True)
            rows_T(3, 3, 16)
            R = IN_BUFS
            for j in range(2, R):
                hidden(j, j, False)
                output(j - 2, j - 2, j < 4)
                rows_T(j + 2, (j + 2) % R, 16 * ((j + 2) // R + 1))
            with pe.Fori(1, NT // R - 1) as i:
                load_experts(pe, last_experts, i * R - 2)
                load_experts(pe, tile_expert, i * R)
                for b in range(R):
                    hidden(i * R + b, b, False)
                    output(i * R + (b - 2), (b - 2) % R, False, b < 2)
                    rows_T(i * R + (b + 2), (b + 2) % R, i * 16 + 16 * ((b + 2) // R + 1))
            load_experts(pe, last_experts, NT - R - 2)
            load_experts(pe, tile_expert, NT - R)
            for j in range(NT - R, NT):
                hidden(j, j % R, False)
                output(j - 2, (j - 2) % R, False, j < NT - R + 2)
                if j + 2 < NT:
                    rows_T(j + 2, (j + 2) % R, 16 * (NT // R))
            for j in (NT - 2, NT - 1):
                output(j, j % R, False)

            for b in range(B):
                if b == 0:
                    pe.wait_ge(y_ready, NT)
                if b >= 2:
                    pe.wait_ge(o_ready, b - 1)
                for t in range(T):
                    pe.wait_ge(summed, T * b + t + 1)
                    last = nc.tensor.transpose(WIDE[b % 2][:, t * P:(t + 1) * P], TOK[:, T * b + t, :], ident32[:])
                last.then_inc(o_full, 1)

        @block.scalar
        def _(act):
            def cp(o, i_, scale=1.0):
                return nc.scalar.activation(o, i_, ACT.Copy, scale=scale)

            nc.scalar.preload_act_table_set("natural_log_exp_and_others")
            act.wait_ge(wt_full, 1)
            for j in range(2):
                for h in range(2):
                    cp(W16[:, 0, j, 0, CE * h:CE * h + CE], SC[:, 0, CE * j:CE * j + CE], WS)
            cp(W16[:, 0, 2, 0, :], SC[:, 0, P:2 * P], WS).then_inc(w_hi, 1)

            def later_weights():
                act.wait_ge(b_in, 16 * 9)
                cp(W16[:, 1, :, 0, :], W32[:, 2:5, :], WS)
                cp(B16[0:1, :, :], B32[0:1, :, :], WS)
                cp(B16[32:33, :, :], B32[32:33, :, :], WS)
                act.wait_ge(b1_full, 1)
                cp(b1T[:], SC[:, 1, 0:E * HC]).then_inc(b1_ready, 1)
                cp(WG16[:, 0, :], Wg32[:], WS).then_inc(w_hi, 1)

            for s in STEPS:
                u, a, m, v = roles(s)
                n_mx = mx_base(s)
                if v is not None and v < B:
                    if v > 0:
                        for h in range(3):
                            act.wait_ge(half_full[h], uses_before(v, h))
                    act.wait_ge(x_in[v], 16)
                    cp(X16h[:], X[:, v, :]).then_inc(x_hi, 1)
                    act.wait_ge(mx_full, n_mx + 1)
                    cp(TOK[:, T * v:T * v + T, :], MX[:]).then_inc(mx_free, 1)
                    if s == -1:
                        later_weights()
                if s == 3:
                    act.wait_ge(wexp_in, 16)

                def first_weights(i):
                    c = ds(i * S, S)
                    cp(W1H[:, c], Xw[:, c], WS)
                    cp(Xw[:, c], Xw[:, c], WS).then_inc(wexp_scaled, 1)

                def transposed(i):
                    half, product_ = product(v, "rows")
                    act.wait_ge(half_full[half], used(v, "rows", i) + 1)
                    cp(X16h[:, ds(i * 256, 256)], product_).then_inc(half_high[half], 1)

                def values(i):
                    half, product_ = product(v, "values")
                    act.wait_ge(half_full[half], used(v, "values", i) + 1)
                    cp(VH[:, v % 4, ds(i * 2, 2), 0:P], product_, 1 / WS).then_inc(half_high[half], 1)

                def projected(name, i):
                    half, product_ = product(v, name)
                    act.wait_ge(half_full[half], used(v, name, i) + 1)
                    cp((QH if name == "queries" else KH)[:, v % 3, ds(i * 256, 256)], product_, 1 / WS) \
                        .then_inc(half_high[half], 1)

                def exponentials(i, p, h):
                    n = i * 4 + (2 * T * u + 2 * p + h + 1)
                    sc = SCALE[0 if u < B else 1]
                    c = slice(h * HALF, (h + 1) * HALF)
                    act.wait_ge(sc_full, n)
                    if h == 0:
                        act.wait_ge(e32_free[p], i + (PAIRS * u + 1))
                    nc.scalar.activation(E32[:, p, c], SC[:, h, :], ACT.Exp, scale=sc)
                    nc.scalar.activation(EH[:, u % 2, ds(i * 2 + p, 1), c], SC[:, h, :], ACT.Exp, scale=sc) \
                        .then_inc(sc_free, 1)

                def rstds(a_, i):
                    k = i + (PAIRS * a_ + 1)
                    act.wait_ge(ve_ready, k)
                    nc.scalar.activation(lnv[:], ve[:], ACT.Ln).then_inc(ln_ready, 1)
                    act.wait_ge(ln_ready, k)
                    nc.scalar.activation(r0[:], lnv[:], ACT.Exp, scale=-0.5).then_inc(r0_ready, 1)

                def pair(i, before):
                    if u is not None:
                        exponentials(i, 0, 0)
                    if v is not None and v >= B:
                        transposed(i)
                    if u is not None:
                        exponentials(i, 0, 1)
                    if before is not None:
                        rstds(*before)
                    if v is not None and v < UNITS:
                        values(i)
                    if u is not None:
                        exponentials(i, 1, 0)
                        exponentials(i, 1, 1)
                    if v is not None and v < UNITS:
                        projected("queries", i)
                        projected("keys", i)
                    if s == 3:
                        first_weights(i)

                before = pair_before(s)
                if v == UNITS + B - 1:
                    rstds(*before)
                    for h in range(2):
                        act.wait_ge(mx_full, n_mx + h + 1)
                        c = slice(h * HALF, (h + 1) * HALF)
                        cp(X16h[:, c], MX[:, c]).then_inc(half_high[0], 1)
                else:
                    pair(0, before)
                    with act.Fori(1, PAIRS) as i:
                        pair(i, None if a is None else (a, i - 1))
                for c in [v - UNITS] if v is not None and v >= UNITS else []:
                    act.wait_ge(gap_ready, c + 1)
                    nc.scalar.activation(egap[:], gap[:], ACT.Exp).then_inc(egap_ready, 1)

            act.wait_ge(wexp_in, 32)
            for i in range(PAIRS):
                g = slice(i * T, (i + 1) * T)
                cp(W2HL[:, g, 0, :], Xg[:, g, :], WS).then_inc(wexp_scaled, 1)
            nc.scalar.preload_act_table_set("gelu_and_others")
            act.wait_ge(table_ready, 3)

            def gelu(j, b, first):
                e = expert(act, tile_expert, b)
                act.wait_ge(h_full, j + 1)
                if not first:
                    act.wait_ge(hl_ready, j - 1)
                for c in range(HC):
                    k = slice(c * TR, (c + 1) * TR)
                    last = nc.scalar.activation(h32[:, b % 2, k], WIDE[b % 2][:, k], ACT.Gelu, bias=b1T[:, ds(e * HC + c, 1)], scale=1 / WS)
                last.then_inc(h_ready, 1)

            tile_expert = expert_registers(act, "act_expert", IN_BUFS)
            load_experts(act, tile_expert, 0)
            for j in range(IN_BUFS):
                gelu(j, j, j < 2)
            with act.Fori(1, NT // IN_BUFS) as i:
                load_experts(act, tile_expert, i * IN_BUFS)
                for b in range(IN_BUFS):
                    gelu(i * IN_BUFS + b, b, False)
            for b in range(B):
                act.wait_ge(o_full, b + 1)
                cp(X[:, b, :], WIDE[b % 2]).then_inc(o_ready, 1)

        @block.vector
        def _(dve):
            nc.vector.memset(B32[:], 0.0).then_inc(bias_zeroed, 1)
            nc.vector.memset(B16[:], 0.0).then_inc(const_ready, 1)
            nc.vector.memset(ones16[:], 1.0)
            nc.vector.memset(onesb[:], 1.0).then_inc(const_ready, 1)
            nc.vector.memset(VH[:, :, :, P:VW], 1.0)
            nc.vector.memset(rec[:], 0.0).then_inc(mx_free, 1)
            nc.vector.memset(ve[:], 1.0).then_inc(sc_free, 2)
            nc.vector.memset(lnv[:], 0.0).then_inc(e32_free[0], 1)
            nc.vector.memset(Z[:], 0.0).then_inc(e32_free[1], 1)
            nc.vector.memset(nt[:], 0.0).then_inc(half_free[0], 1)
            nc.vector.memset(r0[:], 0.0).then_inc(half_free[1], 1)
            nc.vector.memset(mean[:], 0.0).then_inc(half_free[2], 1)
            nc.vector.memset(nt2[:], 0.0).then_inc(pv_free, 2)
            nc.vector.memset(rstd[:], 0.0).then_inc(z_split, 1)

            dve.wait_ge(w_hi, 1)
            for j in range(2):
                for h in range(2):
                    w = W16[:, 0, j, :, CE * h:CE * h + CE]
                    nc.vector.scalar_tensor_tensor(out=w[:, 1, :], in0=SC[:, 0, CE * j:CE * j + CE], scalar=WS,
                                                   in1=w[:, 0, :], op0=ALU.mult, op1=ALU.subtract)
            nc.vector.scalar_tensor_tensor(out=W16[:, 0, 2, 1, :], in0=SC[:, 0, P:2 * P], scalar=WS,
                                           in1=W16[:, 0, 2, 0, :], op0=ALU.mult, op1=ALU.subtract).then_inc(w_ready, 1)

            def later_weights():
                dve.wait_ge(w_hi, 2)
                nc.vector.scalar_tensor_tensor(out=W16[:, 1, :, 1, :], in0=W32[:, 2:5, :], scalar=WS,
                                               in1=W16[:, 1, :, 0, :], op0=ALU.mult, op1=ALU.subtract) \
                    .then_inc(w_ready, 1)
                r = slice(32, 33)
                nc.vector.scalar_tensor_tensor(out=B16[r, :, :], in0=B32[r, :, :], scalar=WS, in1=B16[r, :, :],
                                               op0=ALU.mult, op1=ALU.subtract).then_inc(w_ready, 1)
                nc.vector.scalar_tensor_tensor(out=WG16[:, 1, :], in0=Wg32[:], scalar=WS, in1=WG16[:, 0, :],
                                               op0=ALU.mult, op1=ALU.subtract).then_inc(w_ready, 1)

            dve.wait_ge(const_ready, 4)
            dve.wait_ge(iotas, 13)
            links = 0

            def link(instruction):
                nonlocal links
                links += 1
                instruction.then_inc(chain, 1)
                dve.wait_ge(chain, links)

            def choose(c):
                for t in range(T):
                    nc.vector.max(top[:, t, :], LG[:, t, :])
                link(nc.vector.memset(gap[:], 0.0))
                for t in range(T):
                    nc.vector.max_index(topi[:, t, :], top[:, t, :], LG[:, t, :])
                nc.vector.tensor_tensor(gap[:], top[:, :, 1], top[:, :, 0], ALU.subtract).then_inc(gap_ready, 1)
                link(nc.vector.memset(den[:], 0.0))
                link(nc.vector.tensor_copy(topf[:], topi[:, :, 0:2].rearrange("p t s -> p s t")))
                nc.vector.tensor_copy(ZN[:, T * c:T * c + T, 1], topf[:, 0, :])
                for q in range(2):
                    last = nc.vector.tensor_tensor(hot[:, q], iota_e[:],
                                                   topf[:, q:q + 1, :].to_broadcast([P, E, T]), ALU.is_equal)
                link(last)
                nc.vector.tensor_tensor(picked[:], hot[:, 0], hot[:, 1], ALU.add).then_inc(picked_ready, 1)
                dve.wait_ge(egap_ready, c + 1)
                link(nc.vector.tensor_scalar(den[:], egap[:], 1.0, None, ALU.add))
                w = WT[:, :, T * c:T * c + T]
                link(nc.vector.reciprocal(w[:, 0, :], den[:]))
                link(nc.vector.tensor_tensor(w[:, 1, :], egap[:], w[:, 0, :], ALU.mult))

            def place(c):
                n = ranked(c)
                def flat(t):
                    return t[:].rearrange("p e t -> p (e t)")
                dve.wait_ge(half_full[0], n + 1)
                link(nc.vector.tensor_copy(flat(tots), PR[:, 0, E * T:2 * E * T]))
                link(nc.vector.tensor_tensor_scan(flat(incl), flat(restart), flat(tots), 0.0, ALU.mult, ALU.add))
                link(nc.vector.tensor_tensor(befo[:], incl[:], tots[:], ALU.subtract))
                nc.vector.tensor_tensor(flat(rank), PR[:, 0, 0:E * T], flat(befo), ALU.add).then_inc(half_free[0], 1)
                dve.wait_ge(half_free[0], n + 2)
                link(nc.vector.tensor_tensor(rows[:], rank[:], start[:].unsqueeze(2).to_broadcast([P, E, T]), ALU.add))
                link(nc.vector.tensor_tensor(start[:], start[:], incl[:, :, T - 1], ALU.add))
                for q in range(2):
                    last = nc.vector.tensor_tensor(mine[:, q], hot[:, q], rows[:], ALU.mult)
                link(last)
                for q in range(2):
                    last = nc.vector.reduce_sum(posf[:, q, :], mine[:, q].rearrange("p e t -> p t e"), AX.X)
                link(last)
                nc.vector.tensor_copy(posi[:, :, T * c:T * c + T], posf[:]).then_inc(rows_ready, 1)

            def tile_table():
                link(nc.vector.tensor_tensor(cnt[:], start[:], ecap[:], ALU.subtract))
                link(nc.vector.tensor_tensor(over[:], cnt[:].unsqueeze(2).to_broadcast([P, E, MT]),
                                             tile_ends[:].unsqueeze(1).to_broadcast([P, E, MT]), ALU.is_gt))
                link(nc.vector.reduce_sum(tiles[:], over[:], AX.X))
                nc.vector.tensor_copy(padrow[:], start[:]).then_inc(table_ready, 1)
                link(nc.vector.tensor_tensor_scan(ends[:], ones8[:], tiles[:], 0.0, ALU.mult, ALU.add))
                link(nc.vector.tensor_scalar(skip[:], tiles[:], -1.0, float(CAP // TR), ALU.mult, ALU.add))
                link(nc.vector.tensor_tensor(past[:], iotaj[:].unsqueeze(2).to_broadcast([P, NT, E]),
                                             ends[:].unsqueeze(1).to_broadcast([P, NT, E]), ALU.is_ge))
                link(nc.vector.tensor_tensor(jump[:], past[:], skip[:].unsqueeze(1).to_broadcast([P, NT, E]), ALU.mult))
                nc.vector.reduce_sum(tabf[:, 1, :], past[:], AX.X)
                link(nc.vector.reduce_sum(tabf[:, 0, :], jump[:], AX.X))
                nc.vector.tensor_tensor(tabi[:, 0, :], tabf[:, 0, :], iotaj[:], ALU.add).then_inc(table_ready, 1)
                nc.vector.tensor_scalar(tabi[:, 1, :], tabf[:, 1, :], float(E - 1), None, ALU.min) \
                    .then_inc(table_ready, 1)

            for s in STEPS:
                u, a, m, v = roles(s)
                n_mx = mx_base(s) + (1 if v is not None and v < B else 0)
                if v is not None and v < B:
                    dve.wait_ge(x_hi, v + 1)
                    nc.vector.tensor_tensor(X16l[:], X[:, v, :], X16h[:], ALU.subtract).then_inc(x_lo, 1)
                if s == 0:
                    later_weights()
                if a is not None and a < B:
                    dve.wait_ge(mx_free, mx_base(a - 2) + 2)
                def low(o, i_, hi, scale=1 / WS):
                    return nc.vector.scalar_tensor_tensor(out=o, in0=i_, scalar=scale, in1=hi, op0=ALU.mult,
                                                          op1=ALU.subtract)

                def transposed(i):
                    half, product_ = product(v, "rows")
                    dve.wait_ge(half_high[half], highs(v, "rows", i) + 1)
                    low(X16l[:, ds(i * 256, 256)], product_, X16h[:, ds(i * 256, 256)], 1.0) \
                        .then_inc(half_free[half], 1)

                def values(i):
                    half, product_ = product(v, "values")
                    dve.wait_ge(half_high[half], highs(v, "values", i) + 1)
                    low(VL[:, v % 4, ds(i * 2, 2), :], product_.rearrange("p (t c) -> p t c", c=P),
                        VH[:, v % 4, ds(i * 2, 2), 0:P]).then_inc(half_free[half], 1)

                def queries(i):
                    half, product_ = product(v, "queries")
                    dve.wait_ge(half_high[half], highs(v, "queries", i) + 1)
                    c = ds(i * 256, 256)
                    low(QL[:, v % 3, c], product_, QH[:, v % 3, c]).then_inc(half_free[half], 1)

                def keys(i):
                    half, product_ = product(v, "keys")
                    dve.wait_ge(half_high[half], highs(v, "keys", i) + 1)
                    c = ds(i * 256, 256)
                    if v < B:
                        r_ = slice(CE, P)
                        low(KH[r_, v % 3, c], product_[r_, :], KH[r_, v % 3, c]).then_inc(half_free[half], 1)
                    else:
                        low(KL[:, v % 3, c], product_, KH[:, v % 3, c]).then_inc(half_free[half], 1)

                def logits(i):
                    half, product_ = product(v, "logits", 2 * E)
                    dve.wait_ge(half_full[half], used(v, "logits", i) + 1)
                    nc.vector.scalar_tensor_tensor(out=LG[:, ds(i * 2, 2), :],
                                                   in0=product_.rearrange("p (t e) -> p t e", e=E),
                                                   scalar=1 / WS, in1=bgb[:].unsqueeze(1).to_broadcast([P, 2, E]),
                                                   op0=ALU.mult, op1=ALU.add).then_inc(half_free[half], 1)

                def maxima(i, p):
                    dve.wait_ge(mx_full, i * 2 + (n_mx + p + 1))
                    nc.vector.reduce_max(mx[:, p:p + 1], MX[:], AX.X).then_inc(mx_free, 1)

                def diagonals(i, p):
                    dve.wait_ge(mx_free, i * 2 + (n_mx + p + 2))
                    nc.vector.tensor_scalar(DG[:, m % 2, ds(i * 2 + p, 1), :], identb[:], mx[:, p:p + 1], -1.0,
                                            ALU.mult, ALU.mult).then_inc(diag_ready, 1)

                def take_wait():
                    nc.vector.memset(carry[:, 2:3], 0.0)

                def written(i, p):
                    dve.wait_ge(pv_free, i * 2 + (T * a + p + 3))

                def counted(i, p):
                    dve.wait_ge(stats_ready, i * 2 + (T * a + p + 1))

                def e_low(i):
                    dve.wait_ge(sc_free, i * 4 + (2 * T * u + 4))
                    nc.vector.tensor_tensor(EL[:, u % 2, ds(i * 2, 1), :], E32[:, 0:1, :],
                                            EH[:, u % 2, ds(i * 2, 1), :], ALU.subtract).then_inc(e32_free[0], 1)

                def sums(i, p):
                    k = i * 2 + (T * a + p)
                    dve.wait_ge(pv_full, k + 1)
                    nc.vector.reciprocal(rec[:], PV[:, p, P:VW]).then_inc(rec_ready, 1)

                def residual(i, p):
                    k = i * 2 + (T * a + p)
                    t = ds(i * 2 + (T * (a % B) + p), 1)
                    dve.wait_ge(rec_ready, k + 1)
                    nc.vector.scalar_tensor_tensor(out=TOK[:, t, :], in0=PV[:, p, 0:P], scalar=rec[:, 0:1],
                                                   in1=TOK[:, t, :], op0=ALU.mult, op1=ALU.add).then_inc(pv_free, 1)

                def statistics(i, p):
                    nc.vector.bn_stats(stats[:, p, :], TOK[:, ds(i * 2 + (T * (a % B) + p), 1), :]) \
                        .then_inc(stats_ready, 1)

                def moments(i, p):
                    nc.vector.bn_aggr(mv[:, p, :], stats[:, p, :]).then_inc(mv_ready, 1)

                def variances(i):
                    dve.wait_ge(mv_ready, i * 2 + (T * a + 2))
                    dve.wait_ge(z_split, i + (PAIRS * a + 1))
                    nc.vector.tensor_copy(mean[:], mv[:, :, 0])
                    nc.vector.tensor_scalar(ve[:], mv[:, :, 1], EPS, None, ALU.add).then_inc(ve_ready, 1)

                def newton_square(a_, i):
                    dve.wait_ge(r0_ready, i + (PAIRS * a_ + 1))
                    nc.vector.tensor_tensor(nt[:], r0[:], r0[:], ALU.mult).then_inc(newton, 1)

                def newton_slope(a_, i):
                    dve.wait_ge(newton, i * 3 + (3 * PAIRS * a_ + 1))
                    nc.vector.scalar_tensor_tensor(out=nt2[:], in0=nt[:], scalar=-0.5, in1=ve[:], op0=ALU.mult,
                                                   op1=ALU.mult).then_inc(newton, 1)

                def newton_end(a_, i):
                    dve.wait_ge(newton, i * 3 + (3 * PAIRS * a_ + 2))
                    nc.vector.scalar_tensor_tensor(out=rstd[:], in0=nt2[:], scalar=1.5, in1=r0[:], op0=ALU.add,
                                                   op1=ALU.mult).then_inc(newton, 1)

                def normalise(a_, i):
                    dve.wait_ge(newton, i * 3 + (3 * PAIRS * a_ + 3))
                    for q in range(2):
                        t = ds(i * 2 + (T * (a_ % B) + q), 1)
                        for o_ in (Z[:, q:q + 1, :], ZZ[:, t, 0:P]):
                            last = nc.vector.tensor_scalar(o_, TOK[:, t, :], mean[:, q:q + 1], rstd[:, q:q + 1],
                                                           ALU.subtract, ALU.mult)
                    last.then_inc(z_ready, 1)

                def split(a_, i):
                    dve.wait_ge(z_ready, i + (PAIRS * (a_ - UNITS + 1) + 2))
                    t = ds(i * 2 + T * (a_ % B), 2)
                    nc.vector.tensor_tensor(ZZ[:, t, P:2 * P], Z[:], ZZ[:, t, 0:P], ALU.subtract).then_inc(z_split, 1)

                on_a, on_m, on_u, on_v = (r is not None for r in (a, m, u, v))
                first_before = pair_before(s)
                if v == UNITS + B - 1:
                    for part in (newton_square, newton_slope, newton_end, normalise, split):
                        part(*first_before)
                    for h in range(2):
                        dve.wait_ge(half_high[0], highs(v, "rows", 0) + h + 1)
                        c = slice(h * HALF, (h + 1) * HALF)
                        low(X16l[:, c], MX[:, c], X16h[:, c], 1.0).then_inc(mx_free, 1)
                    half, product_ = product(v, "logits", T * E)
                    dve.wait_ge(half_full[half], uses_before(v, half) + 1)
                    nc.vector.scalar_tensor_tensor(out=LG[:], in0=product_.rearrange("p (t e) -> p t e", e=E),
                                                   scalar=1 / WS, in1=bgb[:].unsqueeze(1).to_broadcast([P, T, E]),
                                                   op0=ALU.mult, op1=ALU.add).then_inc(half_free[half], 1)
                    dve.wait_ge(half_free[half], uses_before(v, half) + 2)
                    choose(B - 1)
                    place(B - 1)
                    continue

                def pair(i, before):
                    if on_v and v >= B:
                        transposed(i)
                    if on_a:
                        sums(i, 0)
                    if on_u:
                        e_low(i)
                    if before is not None:
                        newton_square(*before)
                        newton_slope(*before)
                    if on_a:
                        residual(i, 0)
                    if before is not None:
                        newton_end(*before)
                        if s >= UNITS:
                            normalise(*before)
                            split(*before)
                    if on_m:
                        maxima(i, 0)
                    if on_a:
                        written(i, 0)
                    if on_v and v < UNITS:
                        values(i)
                    elif on_a:
                        take_wait()
                    if on_a:
                        statistics(i, 0)
                        counted(i, 0)
                    if on_m:
                        diagonals(i, 0)
                    elif on_a:
                        take_wait()
                    if on_a:
                        moments(i, 0)
                    if on_a:
                        sums(i, 1)
                    if on_v and v < UNITS:
                        queries(i)
                    if on_a:
                        residual(i, 1)
                    if on_m:
                        maxima(i, 1)
                    if on_a:
                        written(i, 1)
                    if on_v and v < UNITS:
                        keys(i)
                    elif on_a:
                        take_wait()
                    if on_a:
                        statistics(i, 1)
                        counted(i, 1)
                    if on_m:
                        diagonals(i, 1)
                    elif on_a:
                        take_wait()
                    if on_a:
                        moments(i, 1)
                        variances(i)
                    if on_v and v >= UNITS:
                        logits(i)

                pair(0, first_before)
                with dve.Fori(1, PAIRS) as i:
                    pair(i, (a, i - 1) if on_a else None)
                if on_v and v >= UNITS:
                    dve.wait_ge(half_free[1], uses_before(v, 1) + PAIRS + 1)
                    choose(v - UNITS)
                    place(v - UNITS)
            tile_table()
            for i in range(PAIRS):
                dve.wait_ge(wexp_scaled, PAIRS + i + 1)
                g = slice(i * T, (i + 1) * T)
                nc.vector.scalar_tensor_tensor(out=W2HL[:, g, 1, :], in0=Xg[:, g, :], scalar=WS, in1=W2HL[:, g, 0, :],
                                               op0=ALU.mult, op1=ALU.subtract).then_inc(wexp_lo, 1)

            FT = [PR[:, h, 0:TR].bitcast(F16) for h in range(2)]

            def rows_T(j, b):
                dve.wait_ge(zt_full, j + 1)
                nc.vector.tensor_copy(zT[:, b % 2].rearrange("p h r -> p (h r)"), FT[b % 2]).then_inc(zt_ready, 1)

            def halves(j, b, first=False):
                dve.wait_ge(h_ready, j + 1)
                if not first:
                    dve.wait_ge(y_full, j - 1)
                nc.vector.tensor_copy(hh[:, b % 2, :], h32[:, b % 2, :]).then_inc(hh_ready, 1)
                dve.wait_ge(hh_ready, j + 1)
                nc.vector.tensor_tensor(hl[:, b % 2, :], h32[:, b % 2, :], hh[:, b % 2, :], ALU.subtract) \
                    .then_inc(hl_ready, 1)

            def output_sums(b):
                return MX[:, (b % 2) * HALF:(b % 2 + 1) * HALF].rearrange("p (q k d) -> p q k d", q=2, k=2)

            def output(j, b):
                e = expert(dve, tile_expert, b)
                dve.wait_ge(y_full, j + 1)
                nc.vector.scalar_tensor_tensor(out=y32[:, b], in0=output_sums(b)[:, :, 0, :], scalar=1 / WS,
                                               in1=b2b[:, ds(e * P, P)].unsqueeze(1).to_broadcast([P, 2, P]),
                                               op0=ALU.mult, op1=ALU.add).then_inc(y_half, 1)
                words = tin[:, b, :, 2 * P:ROW].bitcast(I32)
                nc.vector.scalar_tensor_tensor(out=yid[:, b, :], in0=words[:, :, 1], scalar=tabf[:, 1, ds(j, 1)],
                                               in1=words[:, :, 0], op0=ALU.not_equal, op1=ALU.add)

            def output_low(j, b):
                dve.wait_ge(y_half, j + 1)
                nc.vector.scalar_tensor_tensor(out=y32[:, b], in0=output_sums(b)[:, :, 1, :], scalar=1 / WS,
                                               in1=y32[:, b], op0=ALU.mult, op1=ALU.add).then_inc(y_ready, 1)

            dve.wait_ge(table_ready, 3)
            dve.wait_ge(b2_in, 16)
            R = IN_BUFS
            tile_expert = expert_registers(dve, "dve_expert", R)
            load_experts(dve, tile_expert, 0)
            rows_T(0, 0)
            rows_T(1, 1)
            for j in range(R):
                halves(j, j, j < 2)
                if j >= 2:
                    output(j - 2, j - 2)
                rows_T(j + 2, (j + 2) % R)
                if j >= 2:
                    output_low(j - 2, j - 2)
            with dve.Fori(1, NT // R - 1) as i:
                for b in range(R):
                    halves(i * R + b, b)
                    output(i * R + (b - 2), (b - 2) % R)
                    if b == 1:
                        load_experts(dve, tile_expert, i * R)
                    rows_T(i * R + (b + 2), (b + 2) % R)
                    output_low(i * R + (b - 2), (b - 2) % R)
            for j in range(NT - R, NT):
                halves(j, j % R)
                output(j - 2, (j - 2) % R)
                if j == NT - R + 1:
                    load_experts(dve, tile_expert, NT - R)
                if j + 2 < NT:
                    rows_T(j + 2, (j + 2) % R)
                output_low(j - 2, (j - 2) % R)
            for j in (NT - 2, NT - 1):
                output(j, j % R)
                output_low(j, j % R)

            for b in range(B):
                dve.wait_ge(y_in[b], 16)
                for t in range(T):
                    g = T * b + t
                    nc.vector.scalar_tensor_tensor(out=TOK[:, g, :], in0=yin[:, b % 2, t, 0, :], scalar=WT[:, 0, g:g + 1],
                                                   in1=TOK[:, g, :], op0=ALU.mult, op1=ALU.add).then_inc(mixed, 1)
                    if t > 0:
                        dve.wait_ge(mixed, g)
                        h = g - 1
                        nc.vector.scalar_tensor_tensor(out=TOK[:, h, :], in0=yin[:, b % 2, t - 1, 1, :],
                                                       scalar=WT[:, 1, h:h + 1], in1=TOK[:, h, :], op0=ALU.mult,
                                                       op1=ALU.add).then_inc(summed, 1)
                dve.wait_ge(mixed, T * (b + 1))
                h = T * (b + 1) - 1
                nc.vector.scalar_tensor_tensor(out=TOK[:, h, :], in0=yin[:, b % 2, T - 1, 1, :], scalar=WT[:, 1, h:h + 1],
                                               in1=TOK[:, h, :], op0=ALU.mult, op1=ALU.add).then_inc(summed, 1)


_INS = ["x", "L0_conv_theta_w", "L0_conv_phi_w", "L0_conv_proj_w", "L1_attn_Wk", "L1_attn_bk", "L1_attn_Wq",
        "L1_attn_bq", "L1_attn_Wv", "L1_attn_bv", "L1_ffn_Wg", "L1_ffn_bg", "L1_ffn_W1", "L1_ffn_b1", "L1_ffn_W2",
        "L1_ffn_b2"]
_SHAPES = {"x": (B, P, S), "L1_attn_bk": (1, P), "L1_attn_bq": (1, P), "L1_attn_bv": (1, P),
           "L1_ffn_bg": (E,), "L1_ffn_b1": (E * HC, P), "L1_ffn_b2": (E * P,)}


def kernel(**inputs):
    import numpy as np
    import concourse.bacc as bacc
    from concourse.bass_utils import run_bass_kernel_spmd

    nc = bacc.Bacc("TRN2", target_bir_lowering=False, num_devices=1)
    arrays, args = {}, []
    for name in _INS:
        a = np.ascontiguousarray(inputs[name])
        a = a.reshape(_SHAPES.get(name, a.shape))
        arrays[f"in_{name}_dram"] = a
        args.append(nc.dram_tensor(f"in_{name}_dram", a.shape, mybir.dt.from_np(a.dtype), kind="ExternalInput").ap())
    out = nc.dram_tensor("out_0_dram", (B, P, S), F32, kind="ExternalOutput").ap()
    build(nc, *args, out)
    r = run_bass_kernel_spmd(nc, [arrays], core_ids=[0])
    return r.results[0]["out_0_dram"].reshape(B, P, 32, 32)
```

```python
from contextlib import ExitStack

import concourse.bass as bass
from concourse import mybir

F32 = mybir.dt.float32
F16 = mybir.dt.float16
BF16 = mybir.dt.bfloat16
I32 = mybir.dt.int32
U32 = mybir.dt.uint32
ALU = mybir.AluOpType
ACT = mybir.ActivationFunctionType
AX = mybir.AxisListType

P = 128
B = 4
S = 1024
T = S // P
TT = B * T
PAIRS = T // 2
UNITS = 2 * B
CE = 64
SCALE = [CE ** -0.5, P ** -0.5]
EPS = 1e-5
WS = 64.0
HALF = 512
VW = P + 1

E = 8
HID = 512
HC = HID // P
TR = 2 * P
CAP = TT * P + TR
NT = TT * P * 2 // TR + E
MT = TT * P // TR
ROW = 2 * P + 4
PADS = E + E
IN_BUFS = 8


def build(nc, x, theta_w, phi_w, proj_w, Wk, bk, Wq, bq, Wv, bv, Wg, bg, W1, b1, W2, b2, out):
    ds = bass.ds
    with ExitStack() as ctx:
        def sb(name, shape, dt):
            return ctx.enter_context(nc.sbuf_tensor(name, shape, dt))

        def ps(name, shape, dt=F32):
            return ctx.enter_context(nc.psum_tensor(name, shape, dt))

        def sem(name):
            return ctx.enter_context(nc.semaphore(name))

        X = sb("X", [P, B, S], F32)
        X16h = sb("X16h", [P, S], F16)
        X16l = sb("X16l", [P, S], F16)
        TOK = sb("TOK", [P, TT, P], F32)
        ZZ = sb("ZZ", [P, TT, ROW], F16)
        ZN = ZZ[:, :, 2 * P:ROW].bitcast(I32)
        QK = sb("QK", [P, 3, 4, S], F16)
        QH, QL, KH, KL = (QK[:, :, j, :] for j in range(4))
        VH = sb("VH", [P, 4, T, VW], F16)
        VL = sb("VL", [P, 4, T, P], F16)
        EH = sb("EH", [P, 2, T, S], F16)
        EL = sb("EL", [P, 2, T, S], F16)
        E32 = sb("E32", [P, 2, S], F32)
        DG = sb("DG", [P, 2, T, P], BF16)
        mx = sb("mx", [P, T], F32)
        ident16 = sb("ident16", [P, P], F16)
        identb = sb("identb", [P, P], BF16)
        ident32 = sb("ident32", [P, P], F32)
        onesb = sb("onesb", [P, P], BF16)
        ones16 = sb("ones16", [P, 2 * P], F16)
        W32 = sb("W32", [P, 5, P], F32)
        W16 = sb("W16", [P, 2, 3, 2, P], F16)
        B32 = sb("B32", [P, 3, P], F32)
        B16 = sb("B16", [P, 3, P], F16)
        rec = sb("rec", [P, 1], F32)
        stats = sb("stats", [P, 2, 6], F32)
        mv = sb("mv", [P, 2, 2], F32)
        ve = sb("ve", [P, 2], F32)
        lnv = sb("lnv", [P, 2], F32)
        r0 = sb("r0", [P, 2], F32)
        nt = sb("nt", [P, 2], F32)
        nt2 = sb("nt2", [P, 2], F32)
        rstd = sb("rstd", [P, 2], F32)
        mean = sb("mean", [P, 2], F32)
        ZC = sb("ZC", [P, 2, P], F32)
        Z = sb("Z", [P, 2, P], F32)
        carry = sb("carry", [P, 4], F32)
        bgb = sb("bgb", [P, E], F32)
        Wg32 = sb("Wg32", [P, E], F32)
        WG16 = sb("WG16", [P, 2, E], F16)
        LG = sb("LG", [P, T, E], F32)
        top = sb("top", [P, T, 8], F32)
        topi = sb("topi", [P, T, 8], U32)
        topf = sb("topf", [P, 2, T], F32)
        iota_e = sb("iota_e", [P, E, T], F32)
        ecap = sb("ecap", [P, E], F32)
        start = sb("start", [P, E], F32)
        hot = sb("hot", [P, 2, E, T], F32)
        picked = sb("picked", [P, E, T], F16)
        tri = sb("tri", [P, P], F16)
        restart = sb("restart", [P, E, T], F32)
        tots = sb("tots", [P, E, T], F32)
        incl = sb("incl", [P, E, T], F32)
        befo = sb("befo", [P, E, T], F32)
        rank = sb("rank", [P, E, T], F32)
        rows = sb("rows", [P, E, T], F32)
        mine = sb("mine", [P, 2, E, T], F32)
        posf = sb("posf", [P, 2, T], F32)
        posi = sb("posi", [P, 2, B * T], U32)
        gap = sb("gap", [P, T], F32)
        egap = sb("egap", [P, T], F32)
        den = sb("den", [P, T], F32)
        WT = sb("WT", [P, 2, TT], F32)
        padid = sb("padid", [P, PADS, 2, 2], I32)
        zer = sb("zer", [P, 2, 2 * P], F16)
        EH0, EH1 = (EH[:, j].rearrange("p a b -> p (a b)") for j in range(2))
        EL0, EL1 = (EL[:, j].rearrange("p a b -> p (a b)") for j in range(2))
        E32f = E32[:].rearrange("p a b -> p (a b)")
        tile_ends = sb("tile_ends", [P, MT], F32)
        iotaj = sb("iotaj", [P, NT], F32)
        over = E32f[:, 2 * NT * E:2 * NT * E + E * MT].rearrange("p (e n) -> p e n", e=E)
        cnt = sb("cnt", [P, E], F32)
        tiles = sb("tiles", [P, E], F32)
        ends = sb("ends", [P, E], F32)
        skip = sb("skip", [P, E], F32)
        past, jump = (E32f[:, j * NT * E:(j + 1) * NT * E].rearrange("p (j e) -> p j e", e=E) for j in range(2))
        tabf = sb("tabf", [P, 2, NT], F32)
        tabi = sb("tabi", [P, 2, NT], I32)
        padrow = sb("padrow", [P, E], I32)
        ones8 = sb("ones8", [P, E], F32)
        W1H = sb("W1H", [P, E * HID], F16)
        W1L = sb("W1L", [P, E * HID], F16)
        W2HL = EL0.rearrange("p (g k d) -> p g k d", g=E * HC, k=2)
        b1r = sb("b1r", [E * HC, P], F32)
        b1T = sb("b1T", [P, E * HC], F32)
        b2b = DG[:].rearrange("p a b c -> p (a b c)").bitcast(F32)
        Xw = X[:].rearrange("p a b -> p (a b)")
        Xg = Xw.rearrange("p (g d) -> p g d", g=E * HC)
        tin = EH0[:, 0:IN_BUFS * 2 * ROW].rearrange("p (b q r) -> p b q r", q=2, r=ROW)
        zT = EH1[:, 0:4 * TR].rearrange("p (b h r) -> p b h r", b=2, h=2)
        hh, hl = (EH1[:, at:at + 2 * HC * TR].rearrange("p (b r) -> p b r", b=2)
                  for at in (4 * TR, 4 * TR + 2 * HC * TR))
        HERE = 2 * TR
        h32 = E32
        y32 = QK[:, 0].rearrange("p a b -> p (a b)").bitcast(F32).rearrange("p (b q c) -> p b q c", b=IN_BUFS, q=2)
        yid = sb("yid", [P, IN_BUFS, 2], U32)
        yin = [t.bitcast(F32).rearrange("p (b t s c) -> p b t s c", b=2, t=T, s=2)[:, b]
               for t in (EL1, EH0) for b in range(2)]

        zbuf = nc.dram_tensor("zbuf", [E * CAP + E * TR, ROW], F16, kind="Internal").ap()
        ybuf = nc.dram_tensor("ybuf", [2 * TT * P + PADS * TR, P], F32, kind="Internal").ap()

        SC = ps("SC", [P, 2, HALF])
        MX = ps("MX", [P, S])
        PV = ps("PV", [P, 2, HALF])
        PR = ps("PR", [P, 2, HALF])
        WIDE = [t[:].rearrange("p b n -> p (b n)") for t in (SC, PV)]

        x_in = [sem(f"x_in{b}") for b in range(B)]
        w_in = sem("w_in")
        b_in = sem("b_in")
        const_ready = sem("const_ready")
        zero_ready = sem("zero_ready")
        bias_zeroed = sem("bias_zeroed")
        wt_full = sem("wt_full")
        w_hi = sem("w_hi")
        w_ready = sem("w_ready")
        x_hi = sem("x_hi")
        x_lo = sem("x_lo")
        mx_full = sem("mx_full")
        mx_free = sem("mx_free")
        diag_ready = sem("diag_ready")
        sc_full = sem("sc_full")
        sc_free = sem("sc_free")
        e32_free = [sem(f"e32_free{p}") for p in range(2)]
        pr_full = [sem(f"pr_full{h}") for h in range(3)]
        pr_high = [sem(f"pr_high{h}") for h in range(3)]
        rows_high = sem("rows_high")
        pr_free = [sem(f"pr_free{h}") for h in range(3)]
        pv_full = sem("pv_full")
        pv_free = sem("pv_free")
        rec_ready = sem("rec_ready")
        stats_ready = sem("stats_ready")
        mv_ready = sem("mv_ready")
        ve_ready = sem("ve_ready")
        ln_ready = sem("ln_ready")
        r0_ready = sem("r0_ready")
        newton = sem("newton")
        z_ready = sem("z_ready")
        zh_ready = sem("zh_ready")
        zc_ready = sem("zc_ready")
        z_split = sem("z_split")
        out_done = sem("out_done")
        g_in = sem("g_in")
        iotas = sem("iotas")
        tri_zero = sem("tri_zero")
        wexp_in = sem("wexp_in")
        wexp_scaled = sem("wexp_scaled")
        wexp_lo = sem("wexp_lo")
        b1_full = sem("b1_full")
        b2_in = sem("b2_in")
        chain = sem("chain")
        picked_ready = sem("picked_ready")
        gap_ready = sem("gap_ready")
        egap_ready = sem("egap_ready")
        rows_ready = sem("rows_ready")
        scattered = [sem(f"scattered{h}") for h in range(2)]
        table_ready = sem("table_ready")
        pad_done = sem("pad_done")
        pad_static = sem("pad_static")
        tin_full = [sem(f"tin_full{b}") for b in range(IN_BUFS)]
        zt_full = sem("zt_full")
        zt_ready = sem("zt_ready")
        h_full = sem("h_full")
        h_ready = sem("h_ready")
        hh_ready = sem("hh_ready")
        hh_act_ready = sem("hh_act_ready")
        hl_ready = sem("hl_ready")
        y_full = sem("y_full")
        y_half = sem("y_half")
        y_ready = sem("y_ready")
        carried = sem("carried")
        y_out = [sem(f"y_out{b}") for b in range(IN_BUFS)]
        y_in = [sem(f"y_in{k}") for k in range(2 * B)]
        mixed = sem("mixed")
        summed = sem("summed")
        o_full = sem("o_full")
        o_ready = sem("o_ready")

        STEPS = range(-2, UNITS + 2)

        def pair_before(s):
            return (s - 2, PAIRS - 1) if s > 1 else None

        def roles(s):
            return (s if 0 <= s < UNITS else None, s - 1 if 0 <= s - 1 < UNITS else None,
                    s + 1 if 0 <= s + 1 < UNITS else None, s + 2 if s + 2 < UNITS + B else None)

        USES = [{"values": (0, 0), "queries": (1, 0), "keys": (2, 0)},
                {"values": (0, 0), "queries": (1, 0), "keys": (0, 1)},
                {"rows": (0, 0), "values": (1, 0), "queries": (0, 1), "keys": (1, 1)},
                {"rows": (0, 0), "logits": (1, 0)}]

        def uses(v):
            return USES[0 if v < 3 else 1 if v < B else 2 if v < UNITS else 3]

        def per_pair(v, bank):
            return sum(h == bank for h, _ in uses(v).values())

        def whole(v):
            return v is not None and v >= UNITS + 2

        def uses_before(v, bank):
            return (sum(PAIRS * per_pair(w, bank) for w in range(min(v, UNITS + 2)))
                    + max(0, v - UNITS - (2 if bank == 1 else 0)) * (bank < 2))

        def used(v, name, i):
            bank, k = uses(v)[name]
            return i * per_pair(v, bank) + (uses_before(v, bank) + k)

        def highs(v, name, i):
            bank, k = uses(v)[name]
            ranks = max(0, v - UNITS) if bank == 0 else 0
            return i * per_pair(v, bank) + (uses_before(v, bank) - ranks + k)

        def product(v, name, width=256):
            bank, _ = uses(v)[name]
            return bank, (PR[:, bank, 0:width] if bank < 2 else PV[:, 0, 0:width])

        def ranked(c):
            return uses_before(UNITS + c, 0) + (0 if whole(UNITS + c) else PAIRS)

        def mx_base(s):
            return sum((1 if t + 2 < B else 0) + (T if 0 <= t + 1 < UNITS else 0) + (2 if whole(t + 2) else 0)
                       for t in range(-2, s))

        def expert_registers(engine, name, n):
            return [engine.alloc_register(f"{name}{b}") for b in range(n)]

        def load_experts(engine, registers, j):
            n = len(registers)
            engine.load(registers, tabi[0:1, 1, ds(j, n)])

        def expert(engine, registers, b):
            return engine.snap(registers[b], min_val=0, max_val=E - 1)

        block = ctx.enter_context(nc.Block())

        @block.sync
        def _(sp):
            sp.dma_start(W32[0:CE, 0, :], theta_w).then_inc(w_in, 16)
            sp.dma_start(W32[CE:P, 0, :], phi_w).then_inc(w_in, 16)
            sp.dma_start(W32[:, 1, :], proj_w).then_inc(w_in, 16)
            for b in range(B):
                sp.dma_start(X[:, b, :], x[b]).then_inc(x_in[b], 16)
            for j, w in enumerate((Wq, Wk, Wv)):
                sp.dma_start(W32[:, 2 + j, :], w).then_inc(b_in, 16)
            sp.wait_ge(bias_zeroed, 1)
            for j, v in enumerate((bq, bk, bv)):
                for r in (0, 32):
                    sp.dma_start(B32[r:r + 1, j, :], v).then_inc(b_in, 16)
            sp.dma_start(Wg32[:], Wg).then_inc(g_in, 16)
            sp.dma_start(bgb[:], bg.partition_broadcast(P)).then_inc(g_in, 16)
            sp.dma_start(b1r[:], b1).then_inc(g_in, 16)
            sp.wait_ge(iotas, 7)
            unused = zbuf[E * CAP:, :].rearrange("(n q p) r -> n p q r", q=2, p=P)
            for n in range(E):
                sp.dma_start(unused[n, :, :, 0:2 * P], zer[:]).then_inc(pad_static, 16)
                sp.dma_start(unused[n, :, :, 2 * P:ROW], padid[:, E + n].bitcast(F16)).then_inc(pad_static, 16)
            sp.wait_ge(x_lo, B)
            sp.wait_ge(mx_full, mx_base(1) + 1)
            sp.dma_start(Xw.rearrange("p (e h) -> p e h", e=E), W1.rearrange("e d h -> d e h")).then_inc(wexp_in, 16)
            sp.wait_ge(wexp_lo, PAIRS)
            sp.dma_start(Xw.rearrange("p (e c d) -> p e c d", e=E, c=HC),
                         W2.rearrange("e (c h) d -> h e c d", c=HC)).then_inc(wexp_in, 16)
            sp.wait_ge(sc_full, 2 * T * UNITS)
            sp.dma_start(b2b, b2.partition_broadcast(P)).then_inc(b2_in, 16)
            sp.wait_ge(table_ready, 2)
            for e in range(E):
                r = sp.value_load(padrow[0:1, e:e + 1], min_val=e * CAP, max_val=e * CAP + TT * P)
                pad = zbuf[ds(r, TR), :].rearrange("(q p) r -> p q r", q=2)
                sp.dma_start(pad[:, :, 0:2 * P], zer[:]).then_inc(pad_done, 16)
                sp.dma_start(pad[:, :, 2 * P:ROW], padid[:, e].bitcast(F16)).then_inc(pad_done, 16)
            sp.wait_ge(pad_done, 16 * 2 * E)
            sp.wait_ge(pad_static, 16 * 2 * E)
            for h in range(2):
                sp.wait_ge(scattered[h], 16 * T * B)

            def load_tile(j, b, again):
                r = sp.value_load(tabi[0:1, 0, ds(j, 1)], min_val=0, max_val=(E * CAP + E * TR) // TR - 1)
                if again is not None:
                    sp.wait_ge(y_out[b], again)
                sp.dma_start(tin[:, b], zbuf[ds(r * TR, TR), :].rearrange("(q p) r -> p q r", q=2)) \
                    .then_inc(tin_full[b], 16)

            for b in range(IN_BUFS):
                load_tile(b, b, None)
            with sp.Fori(1, NT // IN_BUFS) as i:
                for b in range(IN_BUFS):
                    load_tile(i * IN_BUFS + b, b, i * 32)
            for b in range(IN_BUFS):
                sp.wait_ge(y_out[b], 32 * (NT // IN_BUFS))
            H = T // 2
            for k in range(2 * B):
                y_rows = ybuf[S * k:S * (k + 1), :].rearrange("(t p s) c -> p t s c", p=P, s=2)
                sp.dma_start(yin[k // 2][:, k % 2 * H:(k % 2 + 1) * H], y_rows).then_inc(y_in[k], 16)
            for k in range(2 * B):
                sp.wait_ge(o_ready, k + 1)
                c = slice(k % 2 * HALF, (k % 2 + 1) * HALF)
                sp.dma_start(out[k // 2][:, c], X[:, k // 2, c]).then_inc(out_done, 16)
            sp.wait_ge(out_done, 16 * 2 * B)

        @block.gpsimd
        def _(pool):
            nc.gpsimd.memset(ident32[:], 0.0).then_inc(zero_ready, 1)
            pool.wait_ge(zero_ready, 1)
            nc.gpsimd.affine_select(out=ident32[:], in_=ident32[:], compare_op=ALU.not_equal, fill=1.0, base=0,
                                    pattern=[[-1, P]], channel_multiplier=1).then_inc(zero_ready, 1)
            pool.wait_ge(zero_ready, 2)
            nc.gpsimd.tensor_copy(ident16[:], ident32[:]).then_inc(const_ready, 1)
            nc.gpsimd.tensor_copy(identb[:], ident32[:]).then_inc(const_ready, 1)

            nc.gpsimd.memset(carry[:, 0:2], 0.0).then_inc(iotas, 1)
            nc.gpsimd.memset(carry[:, 3:4], 0.0).then_inc(carried, 1)
            iot = nc.gpsimd.iota
            iot(ZN[:, :, 0], [[2 * P, TT]], base=0, channel_multiplier=2).then_inc(iotas, 1)
            nc.gpsimd.memset(padid[:, :, :, 1], 2 * E)
            iot(padid[:, :, :, 0], [[TR, PADS], [P, 2]], base=2 * TT * P - 1, channel_multiplier=1) \
                .then_inc(iotas, 1)
            nc.gpsimd.memset(zer[:], 0.0).then_inc(iotas, 1)
            kw = dict(channel_multiplier=0, allow_small_or_imprecise_dtypes=True)
            iot(iota_e[:], [[1, E], [0, T]], base=0, **kw).then_inc(iotas, 1)
            iot(tile_ends[:], [[TR, MT]], base=0, **kw).then_inc(iotas, 1)
            iot(iotaj[:], [[1, NT]], base=0, **kw).then_inc(iotas, 1)
            iot(ecap[:], [[CAP, E]], base=0, **kw).then_inc(iotas, 1)
            iot(start[:], [[CAP, E]], base=0, **kw).then_inc(iotas, 1)
            nc.gpsimd.memset(restart[:], 1.0).then_inc(iotas, 1)
            nc.gpsimd.memset(ones8[:], 1.0).then_inc(iotas, 1)
            nc.gpsimd.memset(tri[:], 1.0).then_inc(tri_zero, 1)
            pool.wait_ge(tri_zero, 1)
            pool.wait_ge(iotas, 11)
            nc.gpsimd.affine_select(out=tri[:], in_=tri[:], compare_op=ALU.is_gt, fill=0.0, base=0,
                                    pattern=[[1, P]], channel_multiplier=-1).then_inc(iotas, 1)
            nc.gpsimd.memset(restart[:, :, 0:1], 0.0).then_inc(iotas, 1)

            def scatter(t):
                for q in range(2):
                    nc.gpsimd.indirect_dma_start(
                        out=zbuf, out_offset=bass.IndirectOffsetOnAxis(ap=posi[:, q, t:t + 1], axis=0),
                        in_=ZZ[:, t, :], in_offset=None).then_inc(scattered[q], 16)

            for s in STEPS:
                u, a, _, _ = roles(s)
                before = pair_before(s)
                if s >= UNITS or (u is None and a is None and before is None):
                    continue

                def normalise(a_, i):
                    n = i + (PAIRS * a_ + 1)
                    t = ds(i * 2 + T * (a_ % B), 2)

                    def wide(r):
                        return r[:].unsqueeze(2).to_broadcast([P, 2, P])
                    pool.wait_ge(ve_ready, n)
                    nc.gpsimd.tensor_tensor(ZC[:], TOK[:, t, :], wide(mean), ALU.subtract).then_inc(zc_ready, 1)
                    pool.wait_ge(zc_ready, n)
                    pool.wait_ge(newton, i * 3 + (3 * PAIRS * a_ + 3))
                    nc.gpsimd.tensor_tensor(ZZ[:, t, 0:P], ZC[:], wide(rstd), ALU.mult)
                    nc.gpsimd.tensor_tensor(Z[:], ZC[:], wide(rstd), ALU.mult).then_inc(zh_ready, 1)

                def split(a_, i):
                    pool.wait_ge(zh_ready, i + (PAIRS * a_ + 1))
                    t = ds(i * 2 + T * (a_ % B), 2)
                    nc.gpsimd.tensor_tensor(ZZ[:, t, P:2 * P], Z[:], ZZ[:, t, 0:P], ALU.subtract).then_inc(z_split, 1)

                def e_low(i):
                    pool.wait_ge(sc_free, i * 4 + (2 * T * u + 6))
                    nc.gpsimd.tensor_tensor(EL[:, u % 2, ds(i * 2 + 1, 1), :], E32[:, 1:2, :],
                                            EH[:, u % 2, ds(i * 2 + 1, 1), :], ALU.subtract).then_inc(e32_free[1], 1)

                def pair(i, before):
                    if before is not None:
                        normalise(*before)
                        split(*before)
                    if u is not None:
                        e_low(i)

                if s < UNITS - 1:
                    def low_weights(i):
                        pool.wait_ge(wexp_scaled, i + 1)
                        c = ds(i * S, S)
                        nc.gpsimd.tensor_tensor(W1L[:, c], Xw[:, c], W1H[:, c], ALU.subtract).then_inc(wexp_lo, 1)

                    pair(0, before)
                    if s == 4:
                        low_weights(0)
                    with pool.Fori(1, PAIRS) as i:
                        pair(i, None if a is None else (a, i - 1))
                        if s == 4:
                            low_weights(i)
                else:
                    for i in range(PAIRS):
                        pair(i, (a, i - 1) if i else before)
                        if i == 0:
                            pool.wait_ge(rows_ready, 1)
                        scatter(i)
            for t in range(PAIRS, TT):
                if t % T == 0:
                    pool.wait_ge(rows_ready, t // T + 1)
                scatter(t)

            def put(j4, b):
                pool.wait_ge(y_ready, j4 + (b + 1))
                pool.wait_ge(carried, j4 + (b + 1))
                nc.gpsimd.tensor_tensor(carry[:, 0:1], carry[:, 1:2], carry[:, 1:2], ALU.add).then_inc(carried, 1)
                for q in range(2):
                    nc.gpsimd.indirect_dma_start(
                        out=ybuf, out_offset=bass.IndirectOffsetOnAxis(ap=yid[:, b, q:q + 1], axis=0),
                        in_=y32[:, b, q, :], in_offset=None).then_inc(y_out[b], 16)

            with pool.Fori(0, NT // IN_BUFS) as i:
                for b in range(IN_BUFS):
                    put(i * IN_BUFS, b)

        @block.tensor
        def _(pe):
            def mm(o, w, r, start, stop):
                return nc.tensor.matmul(o, w, r, start=start, stop=stop)

            pe.wait_ge(const_ready, 4)
            pe.wait_ge(w_in, 16 * 3)
            nc.tensor.transpose(SC[:, 0, 0:P], W32[:, 0, :], ident32[:])
            nc.tensor.transpose(SC[:, 0, P:2 * P], W32[:, 1, :], ident32[:]).then_inc(wt_full, 1)

            for s in STEPS:
                u, a, m, v = roles(s)
                n_mx = mx_base(s)
                n_mx += 1 if v is not None and v < B else 0

                def residual_stream():
                    pe.wait_ge(x_in[v], 16)
                    pe.wait_ge(mx_free, n_mx)
                    for t in range(T):
                        last = nc.tensor.transpose(MX[:, t * P:(t + 1) * P], X[:, v, t * P:(t + 1) * P], ident32[:])
                    last.then_inc(mx_full, 1)
                    if s == -1:
                        pe.wait_ge(g_in, 48)
                        nc.tensor.transpose(SC[:, 1, 0:E * HC], b1r[:], ident32[0:E * HC, 0:E * HC]) \
                            .then_inc(b1_full, 1)

                lay = None if v is None else 0 if v < B else 1
                if v == B:
                    pe.wait_ge(w_ready, 4)

                def transposes(i):
                    bank, o_ = product(v, "rows")
                    pe.wait_ge(pr_free[bank], used(v, "rows", i) + 1)
                    pe.wait_ge(z_split, i + (PAIRS * (v - B) + 2))
                    for q in range(2):
                        t = i * 2 + (T * (v % B) + q)
                        for h in range(2):
                            last = mm(o_[:, q * P:(q + 1) * P], ZZ[:, ds(t, 1), h * P:(h + 1) * P], ident16[:],
                                      h == 0, h == 1)
                    last.then_inc(pr_full[bank], 1)

                def values(i):
                    bank, o = product(v, "values")
                    pe.wait_ge(pr_free[bank], used(v, "values", i) + 1)
                    if lay:
                        pe.wait_ge(pr_free[0], used(v, "rows", i) + 2)
                    for q in range(2):
                        c = i * 256 + q * P
                        o_ = o[:, q * P:(q + 1) * P]
                        mm(o_, X16h[:, ds(c, P)], W16[:, lay, 2, 0, :], True, False)
                        mm(o_, X16h[:, ds(c, P)], W16[:, lay, 2, 1, :], False, False)
                        last = mm(o_, X16l[:, ds(c, P)], W16[:, lay, 2, 0, :], False, lay == 0)
                        if lay:
                            last = mm(o_, ones16[:, 0:P], B16[:, 2, :], False, True)
                    last.then_inc(pr_full[bank], 1)

                def projected(name, i):
                    bank, o_ = product(v, name)
                    j = 0 if name == "queries" else 1
                    pe.wait_ge(pr_free[bank], used(v, name, i) + 1)
                    mm(o_, W16[:, lay, j, 0, :], X16h[:, ds(i * 256, 256)], True, False)
                    mm(o_, W16[:, lay, j, 0, :], X16l[:, ds(i * 256, 256)], False, False)
                    last = mm(o_, W16[:, lay, j, 1, :], X16h[:, ds(i * 256, 256)], False, lay == 0)
                    if lay:
                        last = mm(o_, B16[:, j, :], ones16[:], False, True)
                    last.then_inc(pr_full[bank], 1)

                def maxima(i, p):
                    pe.wait_ge(mx_free, i * 2 + (n_mx + p + 1))
                    for h in range(2):
                        last = mm(MX[:, h * HALF:(h + 1) * HALF], QH[:, m % 3, ds(i * 256 + p * P, P)],
                                  KH[:, m % 3, h * HALF:(h + 1) * HALF], True, True)
                    last.then_inc(mx_full, 1)

                def scores(i, p, h):
                    w = u % 3
                    kh = KH[:, w, ds(i * 256 + p * P, P)]
                    pe.wait_ge(sc_free, i * 4 + (2 * T * u + 2 * p + h + 1))
                    c = slice(h * HALF, (h + 1) * HALF)
                    o_ = SC[:, h, :]
                    mm(o_, kh, QH[:, w, c], True, False)
                    mm(o_, kh, QL[:, w, c], False, False)
                    if u >= B:
                        mm(o_, KL[:, w, ds(i * 256 + p * P, P)], QH[:, w, c], False, False)
                    pe.wait_ge(diag_ready, T * u + T // 2 * (h + 1))
                    mm(o_, onesb[:], DG[:, u % 2, 4 * h:4 * h + 4, :], False, True).then_inc(sc_full, 1)

                def outputs(i, p):
                    pe.wait_ge(pv_free, i * 2 + (T * a + p + 1))
                    o_ = PV[:, p, 0:VW]
                    for j in range(T):
                        e = ds(i * 256 + p * P, P)
                        mm(o_, EH[:, a % 2, j, e], VH[:, a % 4, j, :], j == 0, False)
                        mm(o_[:, 0:P], EH[:, a % 2, j, e], VL[:, a % 4, j, :], False, False)
                        last = mm(o_, EL[:, a % 2, j, e], VH[:, a % 4, j, :], False, j == T - 1)
                    last.then_inc(pv_full, 1)

                def router(o_, c):
                    mm(o_, X16h[:, c], WG16[:, 0, :], True, False)
                    mm(o_, X16l[:, c], WG16[:, 0, :], False, False)
                    return mm(o_, X16h[:, c], WG16[:, 1, :], False, True)

                def logits(i):
                    bank, o_ = product(v, "logits")
                    pe.wait_ge(pr_free[bank], used(v, "logits", i) + 1)
                    pe.wait_ge(pr_free[0], used(v, "rows", i) + 2)
                    for q in range(2):
                        last = router(o_[:, q * E:(q + 1) * E], ds(i * 256 + q * P, P))
                    last.then_inc(pr_full[bank], 1)

                def rank(c):
                    pe.wait_ge(pr_free[0], ranked(c) + 1)
                    pe.wait_ge(picked_ready, c + 1)
                    flat = picked[:].rearrange("p e t -> p (e t)")
                    mm(PR[:, 0, 0:E * T], tri[:], flat, True, True)
                    mm(PR[:, 0, E * T:2 * E * T], ones16[:, 0:P], flat, True, True).then_inc(pr_full[0], 1)

                if whole(v):
                    for h in range(2):
                        if h == 0:
                            pe.wait_ge(mx_free, n_mx + 1)
                        for t in range(h * PAIRS, (h + 1) * PAIRS):
                            if t % 2 == 0:
                                pe.wait_ge(z_split, t // 2 + (PAIRS * (v - B) + 2))
                            for k in range(2):
                                last = mm(MX[:, t * P:(t + 1) * P], ZZ[:, T * (v % B) + t, k * P:(k + 1) * P],
                                          ident16[:], k == 0, k == 1)
                        last.then_inc(mx_full, 1)
                    bank, o_ = product(v, "logits")
                    pe.wait_ge(pr_free[bank], uses_before(v, bank) + 1)
                    for h in range(2):
                        pe.wait_ge(mx_free, n_mx + h + 2)
                        for t in range(h * PAIRS, (h + 1) * PAIRS):
                            last = router(o_[:, t * E:(t + 1) * E], slice(t * P, (t + 1) * P))
                    last.then_inc(pr_full[bank], 1)
                    rank(v - UNITS)
                    v = None

                if a is None and v is None:
                    continue
                late_rank = s == UNITS - 1

                def pair(i, first):
                    if u is not None:
                        scores(i, 0, 0)
                    if v is not None and v >= B and not (first and late_rank):
                        transposes(i)
                    if u is not None:
                        scores(i, 0, 1)
                    if first and v is not None and v < B:
                        residual_stream()
                    if first and a is not None:
                        for p in range(2):
                            pe.wait_ge(e32_free[p], PAIRS * (a + 1) + 1)
                    if a is not None:
                        outputs(i, 0)
                    if u is not None:
                        scores(i, 1, 0)
                    if first and late_rank:
                        rank(0)
                        transposes(i)
                    if first and m is not None:
                        for h in range(3):
                            pe.wait_ge(pr_free[h], uses_before(m + 1, h) + 1)
                    if m is not None:
                        maxima(i, 0)
                    if first and v is not None and v < B:
                        pe.wait_ge(w_ready, 1)
                        pe.wait_ge(x_lo, v + 1)
                    if v is not None and v < UNITS:
                        values(i)
                    if u is not None:
                        scores(i, 1, 1)
                    if v is not None and v < UNITS:
                        projected("queries", i)
                    if a is not None:
                        outputs(i, 1)
                    if v is not None and v < UNITS:
                        projected("keys", i)
                    if v is not None and v >= UNITS:
                        logits(i)
                    if m is not None:
                        maxima(i, 1)

                pair(0, True)
                with pe.Fori(1, PAIRS) as i:
                    pair(i, False)
                if v == UNITS + 1:
                    rank(1)

            FT = [PR[:, h, :].bitcast(F16) for h in range(2)]

            def rows_T(j, b, n):
                pe.wait_ge(tin_full[b], n)
                if j is not None:
                    pe.wait_ge(zt_ready, j - 1)
                for h in range(2):
                    for q in range(2):
                        at = h * TR + q * P
                        last = nc.tensor.transpose(FT[b % 2][:, at:at + P], tin[:, b, q, h * P:(h + 1) * P], ident16[:])
                last.then_inc(zt_full, 1)

            def hidden(j, b, first):
                e = expert(pe, tile_expert, b)
                pe.wait_ge(zt_ready, j + 1)
                if not first:
                    pe.wait_ge(h_ready, j - 1)
                for c in range(HC):
                    o_ = WIDE[b % 2][:, c * TR:(c + 1) * TR]
                    w = ds(e * HID + c * P, P)
                    mm(o_, W1H[:, w], zT[:, b % 2, 0, :], True, False)
                    mm(o_, W1H[:, w], zT[:, b % 2, 1, :], False, False)
                    last = mm(o_, W1L[:, w], zT[:, b % 2, 0, :], False, True)
                last.then_inc(h_full, 1)

            def output(j, b, first, carried_over=False):
                e = expert(pe, last_experts if carried_over else tile_expert, b % 2 if carried_over else b)
                pe.wait_ge(hl_ready, j + 1)
                if not first:
                    pe.wait_ge(y_ready, j - 1)
                for q in range(2):
                    o_ = MX[:, (b % 2) * HALF + q * TR:(b % 2) * HALF + (q + 1) * TR]
                    for c in range(HC):
                        k = slice(c * TR + q * P, c * TR + (q + 1) * P)
                        g = ds(e * HC + c, 1)
                        def high():
                            return mm(o_, hh[:, b % 2, k], W2HL[:, g, :, :], c == 0, c == HC - 1)

                        def low():
                            mm(o_[:, 0:P], hl[:, b % 2, k], W2HL[:, g, 0, :], False, False)
                        if c == 0:
                            high()
                            low()
                        else:
                            low()
                            last = high()
                last.then_inc(y_full, 1)

            pe.wait_ge(table_ready, 3)
            pe.wait_ge(wexp_lo, 2 * PAIRS)
            pe.wait_ge(egap_ready, B)
            tile_expert = expert_registers(pe, "pe_expert", IN_BUFS)
            last_experts = expert_registers(pe, "pe_last_expert", 2)
            load_experts(pe, tile_expert, 0)
            rows_T(None, 0, 16)
            rows_T(None, 1, 16)
            hidden(0, 0, True)
            rows_T(2, 2, 16)
            hidden(1, 1, True)
            rows_T(3, 3, 16)
            R = IN_BUFS
            for j in range(2, R):
                hidden(j, j, False)
                output(j - 2, j - 2, j < 4)
                rows_T(j + 2, (j + 2) % R, 16 * ((j + 2) // R + 1))
            with pe.Fori(1, NT // R - 1) as i:
                load_experts(pe, last_experts, i * R - 2)
                load_experts(pe, tile_expert, i * R)
                for b in range(R):
                    hidden(i * R + b, b, False)
                    output(i * R + (b - 2), (b - 2) % R, False, b < 2)
                    rows_T(i * R + (b + 2), (b + 2) % R, i * 16 + 16 * ((b + 2) // R + 1))
            load_experts(pe, last_experts, NT - R - 2)
            load_experts(pe, tile_expert, NT - R)
            for j in range(NT - R, NT):
                hidden(j, j % R, False)
                output(j - 2, (j - 2) % R, False, j < NT - R + 2)
                if j + 2 < NT:
                    rows_T(j + 2, (j + 2) % R, 16 * (NT // R))
            for j in (NT - 2, NT - 1):
                output(j, j % R, False)

            for b in range(B):
                if b == 0:
                    pe.wait_ge(y_ready, NT)
                for t in range(T):
                    if b >= 2 and t % PAIRS == 0:
                        pe.wait_ge(o_ready, 2 * b - 3 + t // PAIRS)
                    pe.wait_ge(summed, T * b + t + 1)
                    last = nc.tensor.transpose(WIDE[b % 2][:, t * P:(t + 1) * P], TOK[:, T * b + t, :], ident32[:])
                    if t % PAIRS == PAIRS - 1:
                        last.then_inc(o_full, 1)

        @block.scalar
        def _(act):
            def cp(o, i_, scale=1.0):
                return nc.scalar.activation(o, i_, ACT.Copy, scale=scale)

            nc.scalar.preload_act_table_set("natural_log_exp_and_others")
            act.wait_ge(wt_full, 1)
            for j in range(2):
                for h in range(2):
                    cp(W16[:, 0, j, 0, CE * h:CE * h + CE], SC[:, 0, CE * j:CE * j + CE], WS)
            cp(W16[:, 0, 2, 0, :], SC[:, 0, P:2 * P], WS).then_inc(w_hi, 1)

            def later_weights():
                act.wait_ge(b_in, 16 * 9)
                cp(W16[:, 1, :, 0, :], W32[:, 2:5, :], WS)
                cp(B16[0:1, :, :], B32[0:1, :, :], WS)
                cp(B16[32:33, :, :], B32[32:33, :, :], WS)
                act.wait_ge(b1_full, 1)
                cp(b1T[:], SC[:, 1, 0:E * HC])
                cp(WG16[:, 0, :], Wg32[:], WS).then_inc(w_hi, 1)

            for s in STEPS:
                u, a, m, v = roles(s)
                n_mx = mx_base(s)

                def high_x():
                    if v > 0:
                        for h in range(3):
                            act.wait_ge(pr_full[h], uses_before(v, h))
                    act.wait_ge(x_in[v], 16)
                    cp(X16h[:], X[:, v, :]).then_inc(x_hi, 1)

                def residual_stream():
                    act.wait_ge(mx_full, n_mx + 1)
                    cp(TOK[:, T * v:T * v + T, :], MX[:]).then_inc(mx_free, 1)

                if s == 3:
                    act.wait_ge(wexp_in, 16)

                def first_weights(i):
                    c = ds(i * S, S)
                    cp(W1H[:, c], Xw[:, c], WS)
                    cp(Xw[:, c], Xw[:, c], WS).then_inc(wexp_scaled, 1)

                def transposed(i):
                    bank, product_ = product(v, "rows")
                    act.wait_ge(pr_full[bank], used(v, "rows", i) + 1)
                    cp(X16h[:, ds(i * 256, 256)], product_).then_inc(pr_high[bank], 1)

                def values(i):
                    bank, product_ = product(v, "values")
                    act.wait_ge(pr_full[bank], used(v, "values", i) + 1)
                    cp(VH[:, v % 4, ds(i * 2, 2), 0:P], product_, 1 / WS).then_inc(pr_high[bank], 1)

                def projected(name, i):
                    bank, product_ = product(v, name)
                    act.wait_ge(pr_full[bank], used(v, name, i) + 1)
                    cp((QH if name == "queries" else KH)[:, v % 3, ds(i * 256, 256)], product_, 1 / WS) \
                        .then_inc(pr_high[bank], 1)

                def exponentials(i, p, h):
                    n = i * 4 + (2 * T * u + 2 * p + h + 1)
                    sc = SCALE[0 if u < B else 1]
                    c = slice(h * HALF, (h + 1) * HALF)
                    act.wait_ge(sc_full, n)
                    if h == 0:
                        act.wait_ge(e32_free[p], i + (PAIRS * u + 1))
                    nc.scalar.activation(E32[:, p, c], SC[:, h, :], ACT.Exp, scale=sc)
                    nc.scalar.activation(EH[:, u % 2, ds(i * 2 + p, 1), c], SC[:, h, :], ACT.Exp, scale=sc) \
                        .then_inc(sc_free, 1)

                def rstds(a_, i):
                    k = i + (PAIRS * a_ + 1)
                    act.wait_ge(ve_ready, k)
                    nc.scalar.activation(lnv[:], ve[:], ACT.Ln).then_inc(ln_ready, 1)
                    act.wait_ge(ln_ready, k)
                    nc.scalar.activation(r0[:], lnv[:], ACT.Exp, scale=-0.5).then_inc(r0_ready, 1)

                def pair(i, before, first=False):
                    if u is not None:
                        exponentials(i, 0, 0)
                    if first and v is not None and v < B:
                        high_x()
                    if v is not None and v >= B:
                        transposed(i)
                    if u is not None:
                        exponentials(i, 0, 1)
                    if first and v is not None and v < B:
                        residual_stream()
                    if first and s == -1:
                        later_weights()
                    if before is not None:
                        rstds(*before)
                    if v is not None and v < UNITS:
                        values(i)
                    if u is not None:
                        exponentials(i, 1, 0)
                        exponentials(i, 1, 1)
                    if v is not None and v < UNITS:
                        projected("queries", i)
                        projected("keys", i)
                    if s == 3:
                        first_weights(i)

                before = pair_before(s)

                def gaps(c):
                    act.wait_ge(gap_ready, c + 1)
                    nc.scalar.activation(egap[:], gap[:], ACT.Exp).then_inc(egap_ready, 1)

                if whole(v):
                    rstds(*before)
                    for h in range(2):
                        act.wait_ge(mx_full, n_mx + h + 1)
                        c = slice(h * HALF, (h + 1) * HALF)
                        cp(X16h[:, c], MX[:, c]).then_inc(rows_high, 1)
                    gaps(v - UNITS)
                    v = before = None
                    if a is None:
                        continue
                pair(0, before, True)
                with act.Fori(1, PAIRS) as i:
                    pair(i, None if a is None else (a, i - 1))
                if v is not None and v >= UNITS:
                    gaps(v - UNITS)

            act.wait_ge(wexp_in, 32)
            for i in range(PAIRS):
                g = slice(i * T, (i + 1) * T)
                cp(W2HL[:, g, 0, :], Xg[:, g, :], WS).then_inc(wexp_scaled, 1)
            nc.scalar.preload_act_table_set("gelu_and_others")
            act.wait_ge(table_ready, 3)

            def gelu(j, b, first):
                e = expert(act, tile_expert, b)
                act.wait_ge(h_full, j + 1)
                if not first:
                    act.wait_ge(hl_ready, j - 1)
                for c in range(HC):
                    k = slice(c * TR, (c + 1) * TR)
                    last = nc.scalar.activation(h32[:, b % 2, k], WIDE[b % 2][:, k], ACT.Gelu,
                                                bias=b1T[:, ds(e * HC + c, 1)], scale=1 / WS)
                last.then_inc(h_ready, 1)
                act.wait_ge(h_ready, j + 1)
                if not first:
                    act.wait_ge(y_full, j - 1)
                cp(hh[:, b % 2, HERE:], h32[:, b % 2, HERE:]).then_inc(hh_act_ready, 1)

            tile_expert = expert_registers(act, "act_expert", IN_BUFS)
            load_experts(act, tile_expert, 0)
            for j in range(IN_BUFS):
                gelu(j, j, j < 2)
            with act.Fori(1, NT // IN_BUFS) as i:
                load_experts(act, tile_expert, i * IN_BUFS)
                for b in range(IN_BUFS):
                    gelu(i * IN_BUFS + b, b, False)
            for k in range(2 * B):
                act.wait_ge(o_full, k + 1)
                c = slice(k % 2 * HALF, (k % 2 + 1) * HALF)
                cp(X[:, k // 2, c], WIDE[k // 2 % 2][:, c]).then_inc(o_ready, 1)

        @block.vector
        def _(dve):
            nc.vector.memset(B32[:], 0.0).then_inc(bias_zeroed, 1)
            nc.vector.memset(B16[:], 0.0).then_inc(const_ready, 1)
            nc.vector.memset(ones16[:], 1.0)
            nc.vector.memset(onesb[:], 1.0).then_inc(const_ready, 1)
            nc.vector.memset(VH[:, :, :, P:VW], 1.0)
            nc.vector.memset(rec[:], 0.0).then_inc(mx_free, 1)
            nc.vector.memset(ve[:], 1.0).then_inc(sc_free, 2)
            nc.vector.memset(lnv[:], 0.0).then_inc(e32_free[0], 1)
            nc.vector.memset(Z[:], 0.0).then_inc(e32_free[1], 1)
            nc.vector.memset(nt[:], 0.0).then_inc(pr_free[0], 1)
            nc.vector.memset(r0[:], 0.0).then_inc(pr_free[1], 1)
            nc.vector.memset(mean[:], 0.0).then_inc(pr_free[2], 1)
            nc.vector.memset(nt2[:], 0.0).then_inc(pv_free, 2)
            nc.vector.memset(rstd[:], 0.0).then_inc(z_split, 1)

            dve.wait_ge(w_hi, 1)
            for j in range(2):
                for h in range(2):
                    w = W16[:, 0, j, :, CE * h:CE * h + CE]
                    nc.vector.scalar_tensor_tensor(out=w[:, 1, :], in0=SC[:, 0, CE * j:CE * j + CE], scalar=WS,
                                                   in1=w[:, 0, :], op0=ALU.mult, op1=ALU.subtract)
            nc.vector.scalar_tensor_tensor(out=W16[:, 0, 2, 1, :], in0=SC[:, 0, P:2 * P], scalar=WS,
                                           in1=W16[:, 0, 2, 0, :], op0=ALU.mult, op1=ALU.subtract).then_inc(w_ready, 1)

            def later_weights():
                dve.wait_ge(w_hi, 2)
                nc.vector.scalar_tensor_tensor(out=W16[:, 1, :, 1, :], in0=W32[:, 2:5, :], scalar=WS,
                                               in1=W16[:, 1, :, 0, :], op0=ALU.mult, op1=ALU.subtract) \
                    .then_inc(w_ready, 1)
                r = slice(32, 33)
                nc.vector.scalar_tensor_tensor(out=B16[r, :, :], in0=B32[r, :, :], scalar=WS, in1=B16[r, :, :],
                                               op0=ALU.mult, op1=ALU.subtract).then_inc(w_ready, 1)
                nc.vector.scalar_tensor_tensor(out=WG16[:, 1, :], in0=Wg32[:], scalar=WS, in1=WG16[:, 0, :],
                                               op0=ALU.mult, op1=ALU.subtract).then_inc(w_ready, 1)

            dve.wait_ge(const_ready, 4)
            dve.wait_ge(iotas, 13)
            links = 0

            def link(instruction):
                nonlocal links
                links += 1
                instruction.then_inc(chain, 1)
                dve.wait_ge(chain, links)

            def choose(c):
                for t in range(T):
                    nc.vector.max(top[:, t, :], LG[:, t, :])
                link(nc.vector.memset(gap[:], 0.0))
                for t in range(T):
                    nc.vector.max_index(topi[:, t, :], top[:, t, :], LG[:, t, :])
                nc.vector.tensor_tensor(gap[:], top[:, :, 1], top[:, :, 0], ALU.subtract).then_inc(gap_ready, 1)
                link(nc.vector.memset(den[:], 0.0))
                link(nc.vector.tensor_copy(topf[:], topi[:, :, 0:2].rearrange("p t s -> p s t")))
                nc.vector.tensor_copy(ZN[:, T * c:T * c + T, 1], topf[:, 0, :])
                for q in range(2):
                    last = nc.vector.tensor_tensor(hot[:, q], iota_e[:],
                                                   topf[:, q:q + 1, :].to_broadcast([P, E, T]), ALU.is_equal)
                link(last)
                nc.vector.tensor_tensor(picked[:], hot[:, 0], hot[:, 1], ALU.add).then_inc(picked_ready, 1)
                dve.wait_ge(egap_ready, c + 1)
                link(nc.vector.tensor_scalar(den[:], egap[:], 1.0, None, ALU.add))
                w = WT[:, :, T * c:T * c + T]
                link(nc.vector.reciprocal(w[:, 0, :], den[:]))
                link(nc.vector.tensor_tensor(w[:, 1, :], egap[:], w[:, 0, :], ALU.mult))

            def place(c):
                n = ranked(c)
                def flat(t):
                    return t[:].rearrange("p e t -> p (e t)")
                dve.wait_ge(pr_full[0], n + 1)
                link(nc.vector.tensor_copy(flat(tots), PR[:, 0, E * T:2 * E * T]))
                link(nc.vector.tensor_tensor_scan(flat(incl), flat(restart), flat(tots), 0.0, ALU.mult, ALU.add))
                link(nc.vector.tensor_tensor(befo[:], incl[:], tots[:], ALU.subtract))
                nc.vector.tensor_tensor(flat(rank), PR[:, 0, 0:E * T], flat(befo), ALU.add).then_inc(pr_free[0], 1)
                dve.wait_ge(pr_free[0], n + 2)
                link(nc.vector.tensor_tensor(rows[:], rank[:], start[:].unsqueeze(2).to_broadcast([P, E, T]), ALU.add))
                link(nc.vector.tensor_tensor(start[:], start[:], incl[:, :, T - 1], ALU.add))
                for q in range(2):
                    last = nc.vector.tensor_tensor(mine[:, q], hot[:, q], rows[:], ALU.mult)
                link(last)
                for q in range(2):
                    last = nc.vector.reduce_sum(posf[:, q, :], mine[:, q].rearrange("p e t -> p t e"), AX.X)
                link(last)
                nc.vector.tensor_copy(posi[:, :, T * c:T * c + T], posf[:]).then_inc(rows_ready, 1)

            def tile_table():
                link(nc.vector.tensor_tensor(cnt[:], start[:], ecap[:], ALU.subtract))
                link(nc.vector.tensor_tensor(over[:], cnt[:].unsqueeze(2).to_broadcast([P, E, MT]),
                                             tile_ends[:].unsqueeze(1).to_broadcast([P, E, MT]), ALU.is_gt))
                link(nc.vector.reduce_sum(tiles[:], over[:], AX.X))
                nc.vector.tensor_copy(padrow[:], start[:]).then_inc(table_ready, 1)
                link(nc.vector.tensor_tensor_scan(ends[:], ones8[:], tiles[:], 0.0, ALU.mult, ALU.add))
                link(nc.vector.tensor_scalar(skip[:], tiles[:], -1.0, float(CAP // TR), ALU.mult, ALU.add))
                link(nc.vector.tensor_tensor(past[:], iotaj[:].unsqueeze(2).to_broadcast([P, NT, E]),
                                             ends[:].unsqueeze(1).to_broadcast([P, NT, E]), ALU.is_ge))
                link(nc.vector.tensor_tensor(jump[:], past[:], skip[:].unsqueeze(1).to_broadcast([P, NT, E]), ALU.mult))
                nc.vector.reduce_sum(tabf[:, 1, :], past[:], AX.X)
                link(nc.vector.reduce_sum(tabf[:, 0, :], jump[:], AX.X))
                nc.vector.tensor_tensor(tabi[:, 0, :], tabf[:, 0, :], iotaj[:], ALU.add).then_inc(table_ready, 1)
                nc.vector.tensor_scalar(tabi[:, 1, :], tabf[:, 1, :], float(E - 1), None, ALU.min) \
                    .then_inc(table_ready, 1)

            for s in STEPS:
                u, a, m, v = roles(s)
                n_mx = mx_base(s) + (1 if v is not None and v < B else 0)
                if v is not None and v < B:
                    dve.wait_ge(x_hi, v + 1)
                    nc.vector.tensor_tensor(X16l[:], X[:, v, :], X16h[:], ALU.subtract).then_inc(x_lo, 1)
                if s == 0:
                    later_weights()
                if a is not None and a < B:
                    dve.wait_ge(mx_free, mx_base(a - 2) + 2)
                def low(o, i_, hi, scale=1 / WS):
                    return nc.vector.scalar_tensor_tensor(out=o, in0=i_, scalar=scale, in1=hi, op0=ALU.mult,
                                                          op1=ALU.subtract)

                def transposed(i):
                    bank, product_ = product(v, "rows")
                    dve.wait_ge(pr_high[bank], highs(v, "rows", i) + 1)
                    low(X16l[:, ds(i * 256, 256)], product_, X16h[:, ds(i * 256, 256)], 1.0) \
                        .then_inc(pr_free[bank], 1)

                def values(i):
                    bank, product_ = product(v, "values")
                    dve.wait_ge(pr_high[bank], highs(v, "values", i) + 1)
                    low(VL[:, v % 4, ds(i * 2, 2), :], product_.rearrange("p (t c) -> p t c", c=P),
                        VH[:, v % 4, ds(i * 2, 2), 0:P]).then_inc(pr_free[bank], 1)

                def queries(i):
                    bank, product_ = product(v, "queries")
                    dve.wait_ge(pr_high[bank], highs(v, "queries", i) + 1)
                    c = ds(i * 256, 256)
                    low(QL[:, v % 3, c], product_, QH[:, v % 3, c]).then_inc(pr_free[bank], 1)

                def keys(i):
                    bank, product_ = product(v, "keys")
                    dve.wait_ge(pr_high[bank], highs(v, "keys", i) + 1)
                    c = ds(i * 256, 256)
                    if v < B:
                        r_ = slice(CE, P)
                        low(KH[r_, v % 3, c], product_[r_, :], KH[r_, v % 3, c]).then_inc(pr_free[bank], 1)
                    else:
                        low(KL[:, v % 3, c], product_, KH[:, v % 3, c]).then_inc(pr_free[bank], 1)

                def logits(i):
                    bank, product_ = product(v, "logits", 2 * E)
                    dve.wait_ge(pr_full[bank], used(v, "logits", i) + 1)
                    nc.vector.scalar_tensor_tensor(out=LG[:, ds(i * 2, 2), :],
                                                   in0=product_.rearrange("p (t e) -> p t e", e=E),
                                                   scalar=1 / WS, in1=bgb[:].unsqueeze(1).to_broadcast([P, 2, E]),
                                                   op0=ALU.mult, op1=ALU.add).then_inc(pr_free[bank], 1)

                def maxima(i, p):
                    dve.wait_ge(mx_full, i * 2 + (n_mx + p + 1))
                    nc.vector.reduce_max(mx[:, p:p + 1], MX[:], AX.X).then_inc(mx_free, 1)

                def diagonals(i, p):
                    dve.wait_ge(mx_free, i * 2 + (n_mx + p + 2))
                    nc.vector.tensor_scalar(DG[:, m % 2, ds(i * 2 + p, 1), :], identb[:], mx[:, p:p + 1], -1.0,
                                            ALU.mult, ALU.mult).then_inc(diag_ready, 1)

                def take_wait():
                    nc.vector.memset(carry[:, 2:3], 0.0)

                def written(i, p):
                    dve.wait_ge(pv_free, i * 2 + (T * a + p + 3))

                def counted(i, p):
                    dve.wait_ge(stats_ready, i * 2 + (T * a + p + 1))

                def e_low(i):
                    dve.wait_ge(sc_free, i * 4 + (2 * T * u + 4))
                    nc.vector.tensor_tensor(EL[:, u % 2, ds(i * 2, 1), :], E32[:, 0:1, :],
                                            EH[:, u % 2, ds(i * 2, 1), :], ALU.subtract).then_inc(e32_free[0], 1)

                def sums(i, p):
                    k = i * 2 + (T * a + p)
                    dve.wait_ge(pv_full, k + 1)
                    nc.vector.reciprocal(rec[:], PV[:, p, P:VW]).then_inc(rec_ready, 1)

                def residual(i, p):
                    k = i * 2 + (T * a + p)
                    t = ds(i * 2 + (T * (a % B) + p), 1)
                    dve.wait_ge(rec_ready, k + 1)
                    nc.vector.scalar_tensor_tensor(out=TOK[:, t, :], in0=PV[:, p, 0:P], scalar=rec[:, 0:1],
                                                   in1=TOK[:, t, :], op0=ALU.mult, op1=ALU.add).then_inc(pv_free, 1)

                def statistics(i, p):
                    nc.vector.bn_stats(stats[:, p, :], TOK[:, ds(i * 2 + (T * (a % B) + p), 1), :]) \
                        .then_inc(stats_ready, 1)

                def moments(i, p):
                    nc.vector.bn_aggr(mv[:, p, :], stats[:, p, :]).then_inc(mv_ready, 1)

                def variances(i):
                    dve.wait_ge(mv_ready, i * 2 + (T * a + 2))
                    dve.wait_ge(z_split, i + (PAIRS * a + 1))
                    nc.vector.tensor_copy(mean[:], mv[:, :, 0])
                    nc.vector.tensor_scalar(ve[:], mv[:, :, 1], EPS, None, ALU.add).then_inc(ve_ready, 1)

                def newton_square(a_, i):
                    dve.wait_ge(r0_ready, i + (PAIRS * a_ + 1))
                    nc.vector.tensor_tensor(nt[:], r0[:], r0[:], ALU.mult).then_inc(newton, 1)

                def newton_slope(a_, i):
                    dve.wait_ge(newton, i * 3 + (3 * PAIRS * a_ + 1))
                    nc.vector.scalar_tensor_tensor(out=nt2[:], in0=nt[:], scalar=-0.5, in1=ve[:], op0=ALU.mult,
                                                   op1=ALU.mult).then_inc(newton, 1)

                def newton_end(a_, i):
                    dve.wait_ge(newton, i * 3 + (3 * PAIRS * a_ + 2))
                    nc.vector.scalar_tensor_tensor(out=rstd[:], in0=nt2[:], scalar=1.5, in1=r0[:], op0=ALU.add,
                                                   op1=ALU.mult).then_inc(newton, 1)

                def normalise(a_, i):
                    dve.wait_ge(newton, i * 3 + (3 * PAIRS * a_ + 3))
                    for q in range(2):
                        t = ds(i * 2 + (T * (a_ % B) + q), 1)
                        for o_ in (Z[:, q:q + 1, :], ZZ[:, t, 0:P]):
                            last = nc.vector.tensor_scalar(o_, TOK[:, t, :], mean[:, q:q + 1], rstd[:, q:q + 1],
                                                           ALU.subtract, ALU.mult)
                    last.then_inc(z_ready, 1)

                def split(a_, i):
                    dve.wait_ge(z_ready, i + (PAIRS * (a_ - UNITS + 1) + 2))
                    t = ds(i * 2 + T * (a_ % B), 2)
                    nc.vector.tensor_tensor(ZZ[:, t, P:2 * P], Z[:], ZZ[:, t, 0:P], ALU.subtract).then_inc(z_split, 1)

                on_a, on_m, on_u, on_v = (r is not None for r in (a, m, u, v))
                first_before = pair_before(s)
                if whole(v):
                    for part in (newton_square, newton_slope, newton_end, normalise, split):
                        part(*first_before)
                    for h in range(2):
                        dve.wait_ge(rows_high, 2 * (v - UNITS - 2) + h + 1)
                        c = slice(h * HALF, (h + 1) * HALF)
                        low(X16l[:, c], MX[:, c], X16h[:, c], 1.0).then_inc(mx_free, 1)
                    bank, product_ = product(v, "logits", T * E)
                    dve.wait_ge(pr_full[bank], uses_before(v, bank) + 1)
                    nc.vector.scalar_tensor_tensor(out=LG[:], in0=product_.rearrange("p (t e) -> p t e", e=E),
                                                   scalar=1 / WS, in1=bgb[:].unsqueeze(1).to_broadcast([P, T, E]),
                                                   op0=ALU.mult, op1=ALU.add).then_inc(pr_free[bank], 1)
                    dve.wait_ge(pr_free[bank], uses_before(v, bank) + 2)
                    choose(v - UNITS)
                    place(v - UNITS)
                    v = first_before = None
                    on_v = False
                    if a is None:
                        continue

                def pair(i, before):
                    if on_v and v >= B:
                        transposed(i)
                    if on_a:
                        sums(i, 0)
                    if on_u:
                        e_low(i)
                    if before is not None:
                        newton_square(*before)
                        newton_slope(*before)
                    if on_a:
                        residual(i, 0)
                    if before is not None:
                        newton_end(*before)
                    if on_m:
                        maxima(i, 0)
                    if on_a:
                        written(i, 0)
                    if on_v and v < UNITS:
                        values(i)
                    elif on_a:
                        take_wait()
                    if on_a:
                        statistics(i, 0)
                        counted(i, 0)
                    if on_m:
                        diagonals(i, 0)
                    elif on_a:
                        take_wait()
                    if on_a:
                        moments(i, 0)
                    if on_a:
                        sums(i, 1)
                    if on_v and v < UNITS:
                        queries(i)
                    if on_a:
                        residual(i, 1)
                    if on_m:
                        maxima(i, 1)
                    if on_a:
                        written(i, 1)
                    if on_v and v < UNITS:
                        keys(i)
                    elif on_a:
                        take_wait()
                    if on_a:
                        statistics(i, 1)
                        counted(i, 1)
                    if on_m:
                        diagonals(i, 1)
                    elif on_a:
                        take_wait()
                    if on_a:
                        moments(i, 1)
                        variances(i)
                    if on_v and v >= UNITS:
                        logits(i)

                def last_unit_pair(i, before):
                    sums(i, 0)
                    if before is not None:
                        newton_square(*before)
                    residual(i, 0)
                    if before is not None:
                        newton_slope(*before)
                    written(i, 0)
                    if before is not None:
                        newton_end(*before)
                    else:
                        take_wait()
                    statistics(i, 0)
                    if before is not None:
                        normalise(*before)
                    counted(i, 0)
                    take_wait()
                    moments(i, 0)
                    sums(i, 1)
                    if before is not None:
                        split(*before)
                    residual(i, 1)
                    written(i, 1)
                    take_wait()
                    statistics(i, 1)
                    counted(i, 1)
                    take_wait()
                    moments(i, 1)
                    variances(i)

                if s == UNITS:
                    pair = last_unit_pair
                pair(0, first_before)
                with dve.Fori(1, PAIRS) as i:
                    pair(i, (a, i - 1) if on_a else None)
                if on_v and v >= UNITS:
                    dve.wait_ge(pr_free[1], uses_before(v, 1) + PAIRS + 1)
                    choose(v - UNITS)
                    place(v - UNITS)
            tile_table()
            for i in range(PAIRS):
                dve.wait_ge(wexp_scaled, PAIRS + i + 1)
                g = slice(i * T, (i + 1) * T)
                nc.vector.scalar_tensor_tensor(out=W2HL[:, g, 1, :], in0=Xg[:, g, :], scalar=WS, in1=W2HL[:, g, 0, :],
                                               op0=ALU.mult, op1=ALU.subtract).then_inc(wexp_lo, 1)

            FT = [PR[:, h, 0:TR].bitcast(F16) for h in range(2)]

            def rows_T(j, b):
                dve.wait_ge(zt_full, j + 1)
                nc.vector.tensor_copy(zT[:, b % 2].rearrange("p h r -> p (h r)"), FT[b % 2]).then_inc(zt_ready, 1)

            def halves(j, b, first=False):
                dve.wait_ge(h_ready, j + 1)
                if not first:
                    dve.wait_ge(y_full, j - 1)
                nc.vector.tensor_copy(hh[:, b % 2, 0:HERE], h32[:, b % 2, 0:HERE]).then_inc(hh_ready, 1)
                dve.wait_ge(hh_ready, j + 1)
                dve.wait_ge(hh_act_ready, j + 1)
                nc.vector.tensor_tensor(hl[:, b % 2, :], h32[:, b % 2, :], hh[:, b % 2, :], ALU.subtract) \
                    .then_inc(hl_ready, 1)

            def output_sums(b):
                return MX[:, (b % 2) * HALF:(b % 2 + 1) * HALF].rearrange("p (q k d) -> p q k d", q=2, k=2)

            def output(j, b):
                e = expert(dve, tile_expert, b)
                dve.wait_ge(y_full, j + 1)
                nc.vector.scalar_tensor_tensor(out=y32[:, b], in0=output_sums(b)[:, :, 0, :], scalar=1 / WS,
                                               in1=b2b[:, ds(e * P, P)].unsqueeze(1).to_broadcast([P, 2, P]),
                                               op0=ALU.mult, op1=ALU.add).then_inc(y_half, 1)
                words = tin[:, b, :, 2 * P:ROW].bitcast(I32)
                nc.vector.scalar_tensor_tensor(out=yid[:, b, :], in0=words[:, :, 1], scalar=tabf[:, 1, ds(j, 1)],
                                               in1=words[:, :, 0], op0=ALU.not_equal, op1=ALU.add)

            def output_low(j, b):
                dve.wait_ge(y_half, j + 1)
                nc.vector.scalar_tensor_tensor(out=y32[:, b], in0=output_sums(b)[:, :, 1, :], scalar=1 / WS,
                                               in1=y32[:, b], op0=ALU.mult, op1=ALU.add).then_inc(y_ready, 1)

            dve.wait_ge(table_ready, 3)
            dve.wait_ge(b2_in, 16)
            R = IN_BUFS
            tile_expert = expert_registers(dve, "dve_expert", R)
            load_experts(dve, tile_expert, 0)
            rows_T(0, 0)
            rows_T(1, 1)
            for j in range(R):
                halves(j, j, j < 2)
                rows_T(j + 2, (j + 2) % R)
                if j >= 2:
                    output(j - 2, j - 2)
                    output_low(j - 2, j - 2)
            with dve.Fori(1, NT // R - 1) as i:
                for b in range(R):
                    halves(i * R + b, b)
                    rows_T(i * R + (b + 2), (b + 2) % R)
                    output(i * R + (b - 2), (b - 2) % R)
                    output_low(i * R + (b - 2), (b - 2) % R)
                    if b == 1:
                        load_experts(dve, tile_expert, i * R)
            for j in range(NT - R, NT):
                halves(j, j % R)
                if j + 2 < NT:
                    rows_T(j + 2, (j + 2) % R)
                output(j - 2, (j - 2) % R)
                output_low(j - 2, (j - 2) % R)
                if j == NT - R + 1:
                    load_experts(dve, tile_expert, NT - R)
            for j in (NT - 2, NT - 1):
                output(j, j % R)
                output_low(j, j % R)

            for b in range(B):
                for t in range(T):
                    if t % PAIRS == 0:
                        dve.wait_ge(y_in[2 * b + t // PAIRS], 16)
                    g = T * b + t
                    nc.vector.scalar_tensor_tensor(out=TOK[:, g, :], in0=yin[b][:, t, 0, :], scalar=WT[:, 0, g:g + 1],
                                                   in1=TOK[:, g, :], op0=ALU.mult, op1=ALU.add).then_inc(mixed, 1)
                    if t > 0:
                        dve.wait_ge(mixed, g)
                        h = g - 1
                        nc.vector.scalar_tensor_tensor(out=TOK[:, h, :], in0=yin[b][:, t - 1, 1, :],
                                                       scalar=WT[:, 1, h:h + 1], in1=TOK[:, h, :], op0=ALU.mult,
                                                       op1=ALU.add).then_inc(summed, 1)
                dve.wait_ge(mixed, T * (b + 1))
                h = T * (b + 1) - 1
                nc.vector.scalar_tensor_tensor(out=TOK[:, h, :], in0=yin[b][:, T - 1, 1, :], scalar=WT[:, 1, h:h + 1],
                                               in1=TOK[:, h, :], op0=ALU.mult, op1=ALU.add).then_inc(summed, 1)


_INS = ["x", "L0_conv_theta_w", "L0_conv_phi_w", "L0_conv_proj_w", "L1_attn_Wk", "L1_attn_bk", "L1_attn_Wq",
        "L1_attn_bq", "L1_attn_Wv", "L1_attn_bv", "L1_ffn_Wg", "L1_ffn_bg", "L1_ffn_W1", "L1_ffn_b1", "L1_ffn_W2",
        "L1_ffn_b2"]
_SHAPES = {"x": (B, P, S), "L1_attn_bk": (1, P), "L1_attn_bq": (1, P), "L1_attn_bv": (1, P),
           "L1_ffn_bg": (E,), "L1_ffn_b1": (E * HC, P), "L1_ffn_b2": (E * P,)}


def kernel(**inputs):
    import numpy as np
    import concourse.bacc as bacc
    from concourse.bass_utils import run_bass_kernel_spmd

    nc = bacc.Bacc("TRN2", target_bir_lowering=False, num_devices=1)
    arrays, args = {}, []
    for name in _INS:
        a = np.ascontiguousarray(inputs[name])
        a = a.reshape(_SHAPES.get(name, a.shape))
        arrays[f"in_{name}_dram"] = a
        args.append(nc.dram_tensor(f"in_{name}_dram", a.shape, mybir.dt.from_np(a.dtype), kind="ExternalInput").ap())
    out = nc.dram_tensor("out_0_dram", (B, P, S), F32, kind="ExternalOutput").ap()
    build(nc, *args, out)
    r = run_bass_kernel_spmd(nc, [arrays], core_ids=[0])
    return r.results[0]["out_0_dram"].reshape(B, P, 32, 32)
```
